# Optimizing a Trainium2 kernel written in Bass

```python
import numpy as np
import jax
import jax.numpy as jnp

def _softmax(x, axis=-1):
    return jax.nn.softmax(x, axis=axis)

def _gelu(x):
    return jax.nn.gelu(x, approximate=True)

def _silu(x):
    return jax.nn.silu(x)

def _sigmoid(x):
    return jax.nn.sigmoid(x)

def _layernorm(x, axis=-1, eps=1e-05):
    m = jnp.mean(x, axis=axis, keepdims=True)
    v = jnp.var(x, axis=axis, keepdims=True)
    return (x - m) / jnp.sqrt(v + eps)

def _scatter_add(tgt, idx, src, axis=0):
    return tgt.at[idx].add(src)

def _segment_sum(src, seg, n):
    return jax.ops.segment_sum(src, seg, n)
kernel_name = 'mk_recurrent_d1_jaxref_r8_7eb575'

def setup_inputs(seed: int=0):
    np.random.seed(seed)
    _w = jnp.asarray

    def _L0_attn_setup():
        import jax, jax.numpy as jnp
        import numpy as np
        EMBED_DIM = 128
        NUM_HEADS = 16
        HEAD_DIM = EMBED_DIM // NUM_HEADS
        SEQ_LEN = 128
        BATCH = 4
        MAX_REL_POS = 2

        def _rel_index(length_q, length_k):
            q = jnp.arange(length_q)[:, None]
            k = jnp.arange(length_k)[None, :]
            return jnp.clip(k - q, -MAX_REL_POS, MAX_REL_POS) + MAX_REL_POS
        key = jax.random.key(seed)
        ks = jax.random.split(key, 12)
        s = 1.0 / np.sqrt(EMBED_DIM)
        x = jax.random.normal(ks[0], (BATCH, SEQ_LEN, EMBED_DIM), dtype=jnp.float32)
        W_q = jax.random.normal(ks[1], (EMBED_DIM, EMBED_DIM), dtype=jnp.float32) * s
        b_q = jnp.zeros((EMBED_DIM,), dtype=jnp.float32)
        W_k = jax.random.normal(ks[2], (EMBED_DIM, EMBED_DIM), dtype=jnp.float32) * s
        b_k = jnp.zeros((EMBED_DIM,), dtype=jnp.float32)
        W_v = jax.random.normal(ks[3], (EMBED_DIM, EMBED_DIM), dtype=jnp.float32) * s
        b_v = jnp.zeros((EMBED_DIM,), dtype=jnp.float32)
        W_o = jax.random.normal(ks[4], (EMBED_DIM, EMBED_DIM), dtype=jnp.float32) * s
        b_o = jnp.zeros((EMBED_DIM,), dtype=jnp.float32)
        lim = float(np.sqrt(6.0 / (2 * MAX_REL_POS + 1 + HEAD_DIM)))
        rel_k_table = jax.random.uniform(ks[5], (2 * MAX_REL_POS + 1, HEAD_DIM), jnp.float32, -lim, lim)
        rel_v_table = jax.random.uniform(ks[6], (2 * MAX_REL_POS + 1, HEAD_DIM), jnp.float32, -lim, lim)
        return {'x': x, 'W_q': W_q, 'b_q': b_q, 'W_k': W_k, 'b_k': b_k, 'W_v': W_v, 'b_v': b_v, 'W_o': W_o, 'b_o': b_o, 'rel_k_table': rel_k_table, 'rel_v_table': rel_v_table}
    _L0_attn_in = _L0_attn_setup()

    def _L0_ffn_setup():
        import jax, jax.numpy as jnp
        import numpy as np
        HIDDEN = 128
        FFN = 4 * HIDDEN
        NUM_EXPERTS = 8
        TOP_K = 2
        B, S = (4, 256)
        key = jax.random.key(seed)
        ks = jax.random.split(key, 7)
        scale = 0.02
        return {'x': jax.random.normal(ks[0], (B, S, HIDDEN), dtype=jnp.float32), 'gate_w': jax.random.normal(ks[1], (HIDDEN, NUM_EXPERTS), dtype=jnp.float32) * scale, 'gate_b': jnp.zeros((NUM_EXPERTS,), dtype=jnp.float32), 'w1': jax.random.normal(ks[2], (NUM_EXPERTS, HIDDEN, FFN), dtype=jnp.float32) * scale, 'b1': jnp.zeros((NUM_EXPERTS, FFN), dtype=jnp.float32), 'w2': jax.random.normal(ks[3], (NUM_EXPERTS, FFN, HIDDEN), dtype=jnp.float32) * scale, 'b2': jnp.zeros((NUM_EXPERTS, HIDDEN), dtype=jnp.float32)}
    _L0_ffn_in = _L0_ffn_setup()
    _d = {'L0_attn_x': _L0_attn_in['x'], 'L0_attn_W_q': _L0_attn_in['W_q'], 'L0_attn_b_q': _L0_attn_in['b_q'], 'L0_attn_W_k': _L0_attn_in['W_k'], 'L0_attn_b_k': _L0_attn_in['b_k'], 'L0_attn_W_v': _L0_attn_in['W_v'], 'L0_attn_b_v': _L0_attn_in['b_v'], 'L0_attn_W_o': _L0_attn_in['W_o'], 'L0_attn_b_o': _L0_attn_in['b_o'], 'L0_attn_rel_k_table': _L0_attn_in['rel_k_table'], 'L0_attn_rel_v_table': _L0_attn_in['rel_v_table'], 'L0_ffn_gate_w': _L0_ffn_in['gate_w'], 'L0_ffn_gate_b': _L0_ffn_in['gate_b'], 'L0_ffn_w1': _L0_ffn_in['w1'], 'L0_ffn_b1': _L0_ffn_in['b1'], 'L0_ffn_w2': _L0_ffn_in['w2'], 'L0_ffn_b2': _L0_ffn_in['b2']}
    _x0 = _d['L0_attn_x']
    _d['L0_attn_x'] = jax.random.normal(jax.random.fold_in(jax.random.key(seed), 1), (32, 256, 128), dtype=_x0.dtype)
    del _x0
    return _d

def reference(L0_attn_x, L0_attn_W_q, L0_attn_b_q, L0_attn_W_k, L0_attn_b_k, L0_attn_W_v, L0_attn_b_v, L0_attn_W_o, L0_attn_b_o, L0_attn_rel_k_table, L0_attn_rel_v_table, L0_ffn_gate_w, L0_ffn_gate_b, L0_ffn_w1, L0_ffn_b1, L0_ffn_w2, L0_ffn_b2):

    def _L0_attn_ref(x, W_q, b_q, W_k, b_k, W_v, b_v, W_o, b_o, rel_k_table, rel_v_table):
        import jax, jax.numpy as jnp
        import numpy as np
        EMBED_DIM = 128
        NUM_HEADS = 16
        HEAD_DIM = EMBED_DIM // NUM_HEADS
        SEQ_LEN = 128
        BATCH = 4
        MAX_REL_POS = 2

        def _rel_index(length_q, length_k):
            q = jnp.arange(length_q)[:, None]
            k = jnp.arange(length_k)[None, :]
            return jnp.clip(k - q, -MAX_REL_POS, MAX_REL_POS) + MAX_REL_POS
        B, S, E = x.shape
        H, D = (NUM_HEADS, HEAD_DIM)
        scale = jnp.sqrt(jnp.asarray(D, x.dtype))
        Q = x @ W_q + b_q
        K = x @ W_k + b_k
        V = x @ W_v + b_v
        Qh = Q.reshape(B, S, H, D).transpose(0, 2, 1, 3)
        Kh = K.reshape(B, S, H, D).transpose(0, 2, 1, 3)
        Vh = V.reshape(B, S, H, D).transpose(0, 2, 1, 3)
        scores = jnp.einsum('bhqd,bhkd->bhqk', Qh, Kh)
        idx = _rel_index(S, S)
        rel_k = rel_k_table[idx]
        scores = (scores + jnp.einsum('bhqd,qkd->bhqk', Qh, rel_k)) / scale
        causal = jnp.tril(jnp.ones((S, S), dtype=bool))
        scores = jnp.where(causal[None, None], scores, jnp.asarray(-1000000000.0, scores.dtype))
        attn = jax.nn.softmax(scores, axis=-1)
        out = jnp.einsum('bhqk,bhkd->bhqd', attn, Vh)
        rel_v = rel_v_table[idx]
        out = out + jnp.einsum('bhqk,qkd->bhqd', attn, rel_v)
        out = out.transpose(0, 2, 1, 3).reshape(B, S, E)
        return out @ W_o + b_o

    def _L0_ffn_ref(x, gate_w, gate_b, w1, b1, w2, b2):
        import jax, jax.numpy as jnp
        import numpy as np
        HIDDEN = 128
        FFN = 4 * HIDDEN
        NUM_EXPERTS = 8
        TOP_K = 2
        B, S = (4, 256)
        b, s, h = x.shape
        xt = x.reshape(b * s, h)
        probs = jax.nn.softmax(xt @ gate_w + gate_b, axis=-1)
        _, idx = jax.lax.top_k(probs, TOP_K)
        one_hot = jax.nn.one_hot(idx, NUM_EXPERTS, dtype=xt.dtype)
        mask = (one_hot.sum(axis=1) > 0).astype(xt.dtype)
        h1 = jax.nn.relu(jnp.einsum('th,ehf->etf', xt, w1) + b1[:, None, :])
        out_e = jnp.einsum('etf,efh->eth', h1, w2) + b2[:, None, :]
        out = jnp.einsum('eth,te->th', out_e, mask)
        return out.reshape(b, s, h)
    x = L0_attn_x
    xn = _layernorm(x, axis=-1)
    s = _L0_attn_ref(xn, L0_attn_W_q, L0_attn_b_q, L0_attn_W_k, L0_attn_b_k, L0_attn_W_v, L0_attn_b_v, L0_attn_W_o, L0_attn_b_o, L0_attn_rel_k_table, L0_attn_rel_v_table)
    g = _silu(_L0_ffn_ref(xn, L0_ffn_gate_w, L0_ffn_gate_b, L0_ffn_w1, L0_ffn_b1, L0_ffn_w2, L0_ffn_b2))
    x = x + s * g
    return x

_drawn_inputs = setup_inputs


def setup_inputs(seed=0):
    import zlib

    import numpy as np

    out = dict(_drawn_inputs(seed))
    spreads = {'L0_attn_b_q': (0.0, 0.8),
     'L0_attn_b_k': (0.0, 0.8),
     'L0_attn_b_v': (0.0, 0.8),
     'L0_attn_b_o': (0.0, 0.8),
     'L0_ffn_gate_b': (0.0, 0.286),
     'L0_ffn_b1': (0.0, 0.8),
     'L0_ffn_b2': (0.0, 0.282)}
    factors = {'L0_attn_W_q': 3.618,
     'L0_attn_W_k': 3.52,
     'L0_attn_W_v': 2.703,
     'L0_attn_rel_k_table': 8.0,
     'L0_ffn_w1': 3.047}
    for name, (base, spread) in spreads.items():
        noise = np.random.default_rng([zlib.crc32(name.encode()), seed]).standard_normal(out[name].shape)
        drawn = base * np.exp(spread * noise) if base else spread * noise
        out[name] = jnp.asarray(drawn.astype(out[name].dtype))
    for name, factor in factors.items():
        out[name] = (out[name] * factor).astype(out[name].dtype)
    return out
```

```python
from contextlib import ExitStack

import concourse.bass as bass
import numpy as np
from concourse import mybir

F32 = mybir.dt.float32
BF16 = mybir.dt.bfloat16
ALU = mybir.AluOpType
ACT = mybir.ActivationFunctionType
AX = mybir.AxisListType

P = 128
S = 256
E = 128
H = 16
D = E // H
TT = S // P
NEAR = 3
FFN = 512
NEXP = 8
FC = FFN // P
EPS = 1e-5
NEG = -1.0e9

PAIRS = P // 2
EDGE = PAIRS
PROD = EDGE + 1
Q_PARTS = [0, 1, 2, 0, 1, 0]
K_PARTS = [0, 0, 0, 1, 1, 2]
MAXROW = PROD + len(Q_PARTS) * D
ROWS = MAXROW + 3


def shape_constants(nb):
    bf = mybir.dt.np(BF16)
    q = np.arange(S)
    stair_q = np.zeros((PROD, S), np.float32)
    stair_q[(q % P) // 2, q] = 1.0
    stair_q[EDGE, P:P + 2] = 1.0
    stair_k = np.zeros((PROD, S), np.float32)
    for j in range(PAIRS):
        stair_k[j, (q % P) > 2 * j - 2] = NEG
    stair_k[EDGE, P - 1] = NEG
    near = np.zeros((P, TT, NEAR, H), np.float32)
    near[0::2, :, 2] = NEG
    near[0, 0, 1] = NEG
    near[0:2, 0, 2] = NEG
    return {
        "c_stair_q": stair_q.astype(bf), "c_stair_k": stair_k.astype(bf),
        "c_ones": np.ones((3, S), bf),
        "c_near": near.reshape(P, TT * NEAR * H),
        "c_ident": np.eye(P, dtype=np.float32), "c_ident_bf": np.eye(P).astype(bf),
    }


def program(nc, x, W_q, b_q, W_k, b_k, W_v, b_v, W_o, b_o, rel_k, rel_v, gate_w, gate_b,
            w1, b1, w2, b2, c, out):
    NB = x.shape[0]
    NT = NB * TT
    CH = 4
    NCH = NT // CH
    RS = float(D) ** -0.5

    x_t = x.rearrange("b (t p) e -> p (b t) e", p=P)
    out_t = out.rearrange("b (t p) e -> p (b t) e", p=P)

    with ExitStack() as ctx:
        def sb(name, shape, dt=F32):
            return ctx.enter_context(nc.sbuf_tensor(name, shape, dt))

        def sem(name):
            return ctx.enter_context(nc.semaphore(name))

        xnT = sb("xnT", [P, NT * P])
        attn_all = sb("attn_all", [P, NT, E])
        ident = sb("ident", [P, P])
        ident_bf = sb("ident_bf", [P, P], BF16)
        wqkv = sb("wqkv", [P, 3 * E])
        wo = sb("wo", [P, E])
        gw = sb("gw", [P, NEXP])
        mask_all = sb("mask_all", [P, NT, NEXP])
        bo_row = sb("bo_row", [P, E])

        with ExitStack() as c0:
            def sb0(name, shape, dt=F32):
                return c0.enter_context(nc.sbuf_tensor(name, shape, dt))

            x_all = sb0("x_all", [P, NT, E])
            stats = sb0("stats", [P, NT, 6])
            mean = sb0("mean", [P, NT])
            diff = sb0("diff", [P, NT])
            var = sb0("var", [P, NT])
            rstd = sb0("rstd", [P, NT])
            eps = sb0("eps", [P, 1])
            xn_chunk = sb0("xn_chunk", [P, 2, CH, E])
            gT = sb0("gT", [NEXP, 2, CH * P])
            gb_row = sb0("gb_row", [P, NEXP])
            logits = sb0("logits", [P, NT, NEXP])
            top = sb0("top", [P, NT])
            ex = sb0("ex", [P, NT, NEXP])
            esum = sb0("esum", [P, NT])
            beats = sb0("beats", [P, NT, NEXP, NEXP])
            rank = sb0("rank", [P, NT, NEXP])
            ps_t = [c0.enter_context(nc.psum_tensor(f"ps_t{i}", [P, CH * P], F32)) for i in range(2)]
            ps_g = [c0.enter_context(nc.psum_tensor(f"ps_g{i}", [NEXP, CH * P], F32)) for i in range(2)]
            ps_l = [c0.enter_context(nc.psum_tensor(f"ps_l{i}", [P, CH, NEXP], F32)) for i in range(2)]

            NG = 4
            GT, GC = NT // NG, NCH // NG
            x_in = [sem(f"x_in{g}") for g in range(NG)]
            wt_in = sem("wt_in")
            stat_done = sem("stat_done")
            mv_done = sem("mv_done")
            std_done = sem("std_done")
            rstd_done = sem("rstd_done")
            eps_done = sem("eps_done")
            xn_done = sem("xn_done")
            tr_done = sem("tr_done")
            xT_done = sem("xT_done")
            gate_done = sem("gate_done")
            gT_done = sem("gT_done")
            lg_ps = sem("lg_ps")
            lg_done = sem("lg_done")
            sm0 = sem("sm0")
            xn_free = sem("xn_free")
            ps_t_free = sem("ps_t_free")
            ps_l_free = sem("ps_l_free")
            ex_done = sem("ex_done")

            WT = 16 * 9
            with nc.Block() as block:
                @block.sync
                def _(sp):
                    sp.dma_start(ident[:], c["c_ident"]).then_inc(wt_in, 16)
                    sp.dma_start(gw[:], gate_w).then_inc(wt_in, 16)
                    sp.dma_start(gb_row[:], gate_b[None, :].to_broadcast([P, NEXP])).then_inc(wt_in, 16)
                    sp.dma_start(ident_bf[:], c["c_ident_bf"]).then_inc(wt_in, 16)
                    sp.dma_start(bo_row[:], b_o[None, :].to_broadcast([P, E])).then_inc(wt_in, 16)
                    for g in range(NG):
                        sp.dma_start(x_all[:, g * GT:(g + 1) * GT, :], x_t[:, g * GT:(g + 1) * GT, :]).then_inc(x_in[g], 16)

                @block.vector
                def _(dve):
                    dve.wait_ge(wt_in, WT)

                    nc.vector.memset(eps[:], EPS).then_inc(eps_done, 1)

                    def statistics(g):
                        dve.wait_ge(x_in[g], 16)
                        with dve.Fori(g * GC, (g + 1) * GC) as k:
                            for t in range(CH):
                                nc.vector.bn_stats(stats[:, bass.ds(k * CH + t, 1), :].rearrange("p a e -> p (a e)"), x_all[:, bass.ds(k * CH + t, 1), :]
                                                   .rearrange("p a e -> p (a e)")).then_inc(stat_done, 1)
                        ts = slice(g * GT, (g + 1) * GT)
                        me, mo, ve, vo = (stats[:, ts, i] for i in (1, 4, 2, 5))
                        dve.wait_ge(stat_done, (g + 1) * GT)
                        nc.vector.tensor_tensor(mean[:, ts], me, mo, ALU.add).then_inc(mv_done, 1)
                        nc.vector.tensor_tensor(diff[:, ts], me, mo, ALU.subtract).then_inc(mv_done, 1)
                        nc.vector.tensor_tensor(var[:, ts], ve, vo, ALU.add).then_inc(mv_done, 1)
                        dve.wait_ge(mv_done, g * 6 + 2)
                        nc.vector.tensor_scalar(mean[:, ts], mean[:, ts], 0.5, None, ALU.mult).then_inc(mv_done, 1)
                        nc.vector.tensor_tensor(diff[:, ts], diff[:, ts], diff[:, ts], ALU.mult).then_inc(mv_done, 1)
                        dve.wait_ge(mv_done, g * 6 + 5)
                        nc.vector.scalar_tensor_tensor(var[:, ts], diff[:, ts], E / 4.0, var[:, ts],
                                                       ALU.mult, ALU.add).then_inc(mv_done, 1)

                    def normalise(g):
                        ts = slice(g * GT, (g + 1) * GT)
                        dve.wait_ge(std_done, g + 1)
                        nc.vector.reciprocal(rstd[:, ts], rstd[:, ts]).then_inc(rstd_done, 1)
                        dve.wait_ge(rstd_done, g + 1)
                        with dve.Fori(g * GC, (g + 1) * GC) as k:
                            dve.wait_ge(xn_free, k + 1)
                            for t in range(CH):
                                nc.vector.tensor_scalar(xn_chunk[:, 0, t, :], x_all[:, bass.ds(k * CH + t, 1), :]
                                                        .rearrange("p a e -> p (a e)"),
                                                        mean[:, bass.ds(k * CH + t, 1)], rstd[:, bass.ds(k * CH + t, 1)],
                                                        ALU.subtract, ALU.mult).then_inc(xn_done, 1)
                            dve.wait_ge(lg_ps, k + 1)
                            nc.vector.tensor_tensor(logits[:, bass.ds(k * CH, CH), :], ps_l[0][:],
                                                    gb_row[:, None, :].to_broadcast([P, CH, NEXP]),
                                                    ALU.add).then_inc(lg_done, 1)
                            dve.wait_ge(lg_done, k + 1)
                            dve.sem_inc(ps_l_free, 1)

                    statistics(0)
                    for g in range(NG):
                        if g + 1 < NG:
                            statistics(g + 1)
                        normalise(g)
                    dve.wait_ge(lg_done, NCH)
                    nc.vector.tensor_reduce(top[:], logits[:], AX.X, ALU.max).then_inc(sm0, 1)
                    dve.wait_ge(sm0, 1)
                    nc.vector.tensor_tensor(logits[:], logits[:], top[:, :, None].to_broadcast([P, NT, NEXP]),
                                            ALU.subtract).then_inc(sm0, 1)
                    dve.wait_ge(ex_done, 1)
                    nc.vector.tensor_reduce(esum[:], ex[:], AX.X, ALU.add).then_inc(sm0, 1)
                    dve.wait_ge(sm0, 3)
                    nc.vector.reciprocal(top[:], esum[:]).then_inc(sm0, 1)
                    dve.wait_ge(sm0, 4)
                    nc.vector.tensor_tensor(ex[:], ex[:], top[:, :, None].to_broadcast([P, NT, NEXP]),
                                            ALU.mult).then_inc(sm0, 1)
                    dve.wait_ge(sm0, 5)
                    n = 5
                    for f in range(NEXP):
                        for lo, hi, op in ((0, f + 1, ALU.is_gt), (f + 1, NEXP, ALU.is_ge)):
                            if lo < hi:
                                nc.vector.tensor_tensor(beats[:, :, lo:hi, f],
                                                        ex[:, :, f:f + 1].to_broadcast([P, NT, hi - lo]),
                                                        ex[:, :, lo:hi], op).then_inc(sm0, 1)
                                n += 1
                    dve.wait_ge(sm0, n)
                    nc.vector.tensor_reduce(rank[:], beats[:], AX.X, ALU.add).then_inc(sm0, 1)
                    dve.wait_ge(sm0, n + 1)
                    nc.vector.tensor_scalar(mask_all[:], rank[:], 2.0, None, ALU.is_lt).then_inc(sm0, 1)

                @block.tensor
                def _(pe):
                    for s in (xn_free, ps_t_free, ps_l_free):
                        pe.sem_inc(s, 1)
                    pe.wait_ge(wt_in, WT)
                    with pe.Fori(0, NCH) as k:
                        pe.wait_ge(xn_done, k * CH + CH)
                        pe.wait_ge(ps_t_free, k + 1)
                        for t in range(CH):
                            last = nc.tensor.transpose(ps_t[0][:, t * P:(t + 1) * P], xn_chunk[:, 0, t, :], ident[:])
                        last.then_inc(tr_done, 1)
                        pe.wait_ge(xT_done, k + 1)
                        pe.sem_inc(xn_free, 1)
                        pe.sem_inc(ps_t_free, 1)
                        nc.tensor.matmul(ps_g[0][:], gw[:], xnT[:, bass.ds(k * CH * P, CH * P)],
                                         start=True, stop=True).then_inc(gate_done, 1)
                        pe.wait_ge(gT_done, k + 1)
                        pe.wait_ge(ps_l_free, k + 1)
                        for t in range(CH):
                            last = nc.tensor.matmul(ps_l[0][:, t, :], gT[:, 0, t * P:(t + 1) * P],
                                                    ident[0:NEXP, 0:NEXP], start=True, stop=True, skip_group_check=True)
                        last.then_inc(lg_ps, 1)

                @block.scalar
                def _(act):
                    act.dma_start(wqkv[:, 0:E], W_q).then_inc(wt_in, 16)
                    act.dma_start(wqkv[:, E:2 * E], W_k).then_inc(wt_in, 16)
                    act.dma_start(wqkv[:, 2 * E:], W_v).then_inc(wt_in, 16)
                    act.dma_start(wo[:], W_o).then_inc(wt_in, 16)
                    act.wait_ge(eps_done, 1)

                    def deviation(g):
                        ts = slice(g * GT, (g + 1) * GT)
                        act.wait_ge(mv_done, (g + 1) * 6)
                        nc.scalar.activation(rstd[:, ts], var[:, ts], ACT.Sqrt, bias=eps[:], scale=1.0 / E).then_inc(std_done, 1)

                    deviation(0)
                    for g in range(NG):
                        if g + 1 < NG:
                            deviation(g + 1)
                        with act.Fori(g * GC, (g + 1) * GC) as k:
                            act.wait_ge(tr_done, k + 1)
                            nc.scalar.activation(xnT[:, bass.ds(k * CH * P, CH * P)], ps_t[0][:],
                                                 ACT.Copy).then_inc(xT_done, 1)
                            act.wait_ge(gate_done, k + 1)
                            nc.scalar.activation(gT[:, 0, :], ps_g[0][:], ACT.Copy).then_inc(gT_done, 1)
                    act.wait_ge(sm0, 2)
                    nc.scalar.activation(ex[:], logits[:], ACT.Exp).then_inc(ex_done, 1)

        with ExitStack() as c1:
            attention(nc, c1, NB, RS, xnT, attn_all, wqkv, wo, ident, ident_bf, bo_row,
                      b_q, b_k, b_v, rel_k, rel_v, c)

        with ExitStack() as c2:
            experts(nc, c2, NT, x_t, xnT, attn_all, mask_all, w1, b1, w2, b2, out_t)


def attention(nc, ctx, NB, RS, xnT, attn_all, wqkv, wo, ident, ident_bf, bo_row, b_q, b_k, b_v, rel_k, rel_v, c):
    def sb(name, shape, dt=F32):
        return ctx.enter_context(nc.sbuf_tensor(name, shape, dt))

    def sem(name):
        return ctx.enter_context(nc.semaphore(name))

    def bank(name, n=1):
        return ctx.enter_context(nc.psum_tensor(name, [P, n * 512], F32))

    HH = H // 2
    q_st = [sb(f"q_st{i}", [P, H, S], BF16) for i in range(2)]
    k_st = [sb(f"k_st{i}", [P, H, S], BF16) for i in range(2)]
    w_turn = sb("w_turn", [P, 2, E])
    xb = [sb(f"xb{i}", [P, S]) for i in range(2)]
    qk32 = sb("qk32", [P, 2, S])
    rem = sb("rem", [P, 2, S])
    parts = [sb(f"parts{i}", [P, 2, 3, S], BF16) for i in range(2)]
    tok_a = [sb(f"tok_a{i}", [P, TT, 3 * E]) for i in range(2)]
    tok_b = [sb(f"tok_b{i}", [P, TT, 2 * E]) for i in range(2)]
    near_kv = [sb(f"near_kv{i}", [P, TT, NEAR, 2 * E]) for i in range(2)]
    v_aug = [sb(f"v_aug{i}", [P, TT, H, 32]) for i in range(2)]
    prod = sb("prod", [P, TT, NEAR, E])
    pv_near = sb("pv_near", [P, TT, NEAR, E])
    s_near = sb("s_near", [P, TT, NEAR, H])
    near_top = sb("near_top", [P, TT, H])
    far_top = sb("far_top", [P, TT, H])
    row_max = sb("row_max", [P, TT, H])
    neg_res = [sb(f"neg_res{i}", [P, TT, HH]) for i in range(2)]
    max_parts = sb("max_parts", [P, 2, TT, 3, HH], BF16)
    max_T = [sb(f"max_T{i}", [3 * HH, S], BF16) for i in range(2)]
    near_diff = sb("near_diff", [P, TT, NEAR, H])
    p_near = [sb(f"p_near{i}", [P, TT, NEAR, H]) for i in range(2)]
    num_near = [sb(f"num_near{i}", [P, TT, E]) for i in range(2)]
    den_near = [sb(f"den_near{i}", [P, TT, H]) for i in range(2)]
    probs = [sb(f"probs{i}", [P, 1024]) for i in range(6)]
    ctx_T = sb("ctx_T", [P, 4, S])
    num = sb("num", [P, TT, E])
    den = sb("den", [P, TT, H])
    rden = sb("rden", [P, TT, H])
    o_tok = sb("o_tok", [P, TT, E])
    o_T = sb("o_T", [P, S])
    near_mask = sb("near_mask", [P, TT * NEAR * H])
    bias_col = sb("bias_col", [P, 4])
    rk_all = sb("rk_all", [P, NEAR, D])
    rv_all = sb("rv_all", [P, NEAR, D])
    b_rows = sb("b_rows", [P, 3 * E])
    bias_a = sb("bias_a", [P, 3 * E])
    bias_b = sb("bias_b", [P, 2 * E])
    bias_c = sb("bias_c", [P, 2 * E])

    ps_max = bank("ps_max", 2)
    ps_exp = bank("ps_exp", 2)
    ps_ctx = bank("ps_ctx", 2)
    X0 = bank("ps_x0")
    X1 = bank("ps_x1")

    cst_in = sem("cst_in")
    zeroed = sem("zeroed")
    bias_done = sem("bias_done")
    xb_done = sem("xb_done")
    qk_ps = sem("qk_ps")
    qk_cp = sem("qk_cp")
    part_a = sem("part_a")
    part_p = sem("part_p")
    stack_in = [[sem(f"stack_in{v}{h}") for h in range(2)] for v in range(2)]
    tok_ps = sem("tok_ps")
    tok_ev = sem("tok_ev")
    shift_in = [sem(f"shift_in{v}") for v in range(2)]
    vaug_done = sem("vaug_done")
    prod_done = sem("prod_done")
    sn_done = sem("sn_done")
    max_ps = sem("max_ps")
    max_rd = sem("max_rd")
    mrow = sem("mrow")
    diff_done = sem("diff_done")
    mT_ps = sem("mT_ps")
    mT_cp = sem("mT_cp")
    mrow_in = [sem(f"mrow_in{h}") for h in range(2)]
    p_done = sem("p_done")
    pvn_done = sem("pvn_done")
    nn_done = sem("nn_done")
    exp_ps = sem("exp_ps")
    exp_done = sem("exp_done")
    ctx_ps = sem("ctx_ps")
    ctx_cp = sem("ctx_cp")
    cx_ps = sem("cx_ps")
    nd = sem("nd")
    fin = sem("fin")
    oT_ps = sem("oT_ps")
    oT_cp = sem("oT_cp")
    o_ps = sem("o_ps")
    o_done = sem("o_done")

    MAX_STEPS = [(1, 0), (1, 1), (0, 0), (1, 2), (1, 3), (0, 1)]
    EXP_STEPS = [(0, 0), (0, 1), (1, 0), (0, 2), (0, 3), (1, 1)]
    NS = len(MAX_STEPS)
    NCST = 6 + 1 + 6 + 5
    hd = "p (h d) -> p h d"

    def pipeline(eng, body):
        def one(b, hb, u, known):
            body(lambda k: (b + k, (u + k) % 2, hb + (u + k) // 2),
                 {k: known is None or 0 <= known + k < NB for k in range(-2, 4)})

        for b in range(-2, 2):
            one(b, b // 2, b % 2, b)
        if NB > 6:
            with eng.Fori(0, (NB - 6) // 2) as j:
                for u in range(2):
                    one(j * 2 + (2 + u), j + 1, u, None)
        for b in range(max(NB - 4, 2), NB + 2):
            one(b, b // 2, b % 2, b)

    with nc.Block() as block:
        @block.sync
        def _(sp):
            def cst(dst, src):
                sp.dma_start(dst, src, allow_slow_non_contiguous=True).then_inc(cst_in, 16)

            for i in range(2):
                cst(q_st[i][0:PROD, :, :], c["c_stair_q"][:, None, :].to_broadcast([PROD, H, S]))
                cst(k_st[i][0:PROD, :, :], c["c_stair_k"][:, None, :].to_broadcast([PROD, H, S]))
                cst(k_st[i][MAXROW:ROWS, :, :], c["c_ones"][:, None, :].to_broadcast([3, H, S]))
            cst(near_mask[:], c["c_near"])
            for a in range(2):
                rows, cols = slice(a * P // 2, (a + 1) * P // 2), slice(a * E // 2, (a + 1) * E // 2)
                cst(bias_col[rows, 0:1], b_q[cols].rearrange("(h d o) -> d h o", d=D, o=1))
                cst(bias_col[rows, 1:2], b_k[cols].rearrange("(h d o) -> d h o", d=D, o=1))
                cst(bias_col[rows, 2:3], rel_k[0, :].rearrange("(d h o) -> d h o", h=1, o=1).to_broadcast([D, HH, 1]))
            cst(b_rows[:, 0:E], b_q[None, :].to_broadcast([P, E]))
            cst(b_rows[:, E:2 * E], b_k[None, :].to_broadcast([P, E]))
            cst(b_rows[:, 2 * E:], b_v[None, :].to_broadcast([P, E]))
            cst(rk_all[:], rel_k[None, 0:NEAR, :].to_broadcast([P, NEAR, D]))
            cst(rv_all[:], rel_v[None, 0:NEAR, :].to_broadcast([P, NEAR, D]))

            def stack(half, src_parity, dst_half_sem):
                v = src_parity
                hs = slice(half * HH, (half + 1) * HH)
                rows = slice(half * P // 2, (half + 1) * P // 2)
                for st, w, order in ((q_st[v], 0, Q_PARTS), (k_st[v], 1, K_PARTS)):
                    for i, part in enumerate(order):
                        sp.dma_start(st[PROD + i * D:PROD + (i + 1) * D, hs, :],
                                     parts[v][rows, w, part, :]).then_inc(dst_half_sem, 16)

            def body(at, on):
                b, u, hb = at(0)

                def rows_of_max(k, half):
                    n, v, hn = at(k)
                    sp.wait_ge(mT_cp, n * 2 + half + 1)
                    for i in range(3):
                        sp.dma_start(q_st[v][MAXROW + i:MAXROW + i + 1, half * HH:(half + 1) * HH, :],
                                     max_T[half][i * HH:(i + 1) * HH, :]).then_inc(mrow_in[half], 16)

                if on[0]:
                    rows_of_max(0, 1)
                if on[2]:
                    n, v, hn = at(2)
                    sp.wait_ge(part_p, n * 2 + 2)
                    for half in range(2):
                        if on[0]:
                            sp.wait_ge(exp_ps, b * NS + 3 * (half + 1))
                        stack(half, v, stack_in[v][half])
                        if half == 0:
                            sp.wait_ge(tok_ev, n * 6 + 6)
                            a, kb, nr = tok_a[v], tok_b[v], near_kv[v]
                            for dst, src in ((nr[2:P, :, 2, :], a[0:P - 2, :, E:]), (nr[0:2, 1, 2, :], a[P - 2:P, 0, E:]),
                                             (nr[1:P, :, 1, :], kb[0:P - 1, :, :]), (nr[0:1, 1, 1, :], kb[P - 1:P, 0, :])):
                                sp.dma_start(dst, src).then_inc(shift_in[v], 16)
                            if on[1]:
                                rows_of_max(1, 0)
                elif on[1]:
                    rows_of_max(1, 0)

            pipeline(sp, body)

        NSTK = 12 * 16

        @block.gpsimd
        def _(pool):
            for i in range(2):
                nc.gpsimd.memset(near_kv[i][:], 0.0).then_inc(zeroed, 1)
                nc.gpsimd.memset(v_aug[i][:], 0.0).then_inc(zeroed, 1)
            pool.wait_ge(zeroed, 4)
            for i in range(2):
                nc.gpsimd.memset(v_aug[i][:, :, :, D:D + 1], 1.0).then_inc(zeroed, 1)

            def body(at, on):
                b, u, hb = at(0)
                if on[1]:
                    n, v, hn = at(1)
                    pool.wait_ge(shift_in[v], hn * 64 + 64)
                    if on[0]:
                        pool.wait_ge(sn_done, b * 3 + 1)
                    for t in range(TT):
                        last = nc.gpsimd.tensor_tensor(prod[:, t, :, :], near_kv[v][:, t, :, 0:E],
                                                       tok_a[v][:, t, None, 0:E].to_broadcast([P, NEAR, E]), ALU.mult)
                    last.then_inc(prod_done, 1)
                if on[0]:
                    pool.wait_ge(p_done, b + 1)
                    if on[-1]:
                        pool.wait_ge(nn_done, b * 2)
                    for t in range(TT):
                        for n in range(NEAR):
                            last = nc.gpsimd.tensor_tensor(pv_near[:, t, n, :].rearrange(hd, d=D),
                                                           near_kv[u][:, t, n, E:].rearrange(hd, d=D),
                                                           p_near[u][:, t, n, :, None].to_broadcast([P, H, D]), ALU.mult)
                    last.then_inc(pvn_done, 1)
                if on[2]:
                    n, v, hn = at(2)
                    pool.wait_ge(part_a, n * 2 + 1)
                    nc.gpsimd.tensor_tensor(rem[:], qk32[:], parts[v][:, :, 0, :], ALU.subtract).then_inc(part_p, 1)
                    pool.wait_ge(part_a, n * 2 + 2)
                    nc.gpsimd.tensor_tensor(parts[v][:, :, 2, :], rem[:], parts[v][:, :, 1, :], ALU.subtract).then_inc(part_p, 1)

            pipeline(pool, body)

        @block.scalar
        def _(act):
            act.wait_ge(bias_done, 12)
            act.wait_ge(zeroed, 6)

            def body(at, on):
                b, u, hb = at(0)

                def step(s):
                    act.wait_ge(exp_ps, b * NS + s + 1)
                    if on[-1]:
                        act.wait_ge(ctx_ps, b * 2 - (1 if s < 3 else 0))
                    nc.scalar.activation(probs[s][:], ps_exp[:], ACT.Exp, scale=RS).then_inc(exp_done, 1)

                def qk():
                    n, v, hn = at(2)
                    act.wait_ge(qk_ps, n + 1)
                    if on[1]:
                        act.wait_ge(part_p, n * 2)
                    nc.scalar.activation(qk32[:, 0, :], X0[:, 0:S], ACT.Identity, bias=bias_col[:, 0:1]).then_inc(qk_cp, 1)
                    nc.scalar.activation(qk32[:, 1, :], X0[:, S:2 * S], ACT.Identity, bias=bias_col[:, 3:4]).then_inc(qk_cp, 1)
                    act.wait_ge(qk_cp, n * 2 + 2)
                    if on[0]:
                        for half in range(2):
                            act.wait_ge(stack_in[v][half], hn * NSTK)
                    nc.scalar.activation(parts[v][:, :, 0, :], qk32[:], ACT.Copy).then_inc(part_a, 1)

                def qk2():
                    n, v, hn = at(2)
                    act.wait_ge(part_p, n * 2 + 1)
                    nc.scalar.activation(parts[v][:, :, 1, :], rem[:], ACT.Copy).then_inc(part_a, 1)

                def vaug():
                    n, v, hn = at(1)
                    act.wait_ge(tok_ev, n * 6 + 6)
                    if on[-1]:
                        act.wait_ge(ctx_ps, b * 2)
                    nc.scalar.activation(v_aug[v][:, :, :, 0:D], tok_a[v][:, :, 2 * E:].rearrange("p t (h d) -> p t h d", d=D),
                                         ACT.Copy).then_inc(vaug_done, 1)

                def ctx_copy(k, half):
                    n, v, hn = at(k)
                    act.wait_ge(ctx_ps, n * 2 + half + 1)
                    if half == 0 and on[-1]:
                        act.wait_ge(cx_ps, b * 2)
                    nc.scalar.activation(ctx_T[:, 2 * half:2 * half + 2, :], ps_ctx[:, half * 512:(half + 1) * 512],
                                         ACT.Copy).then_inc(ctx_cp, 1)

                def max_copy(k, half):
                    n, v, hn = at(k)
                    act.wait_ge(mT_ps, n * 2 + half + 1)
                    if on[k - 1]:
                        act.wait_ge(mrow_in[half], n * 48)
                    nc.scalar.activation(max_T[half][:], X1[0:3 * HH, 0:S // 2].bitcast(BF16), ACT.Copy).then_inc(mT_cp, 1)

                if on[0]:
                    act.wait_ge(diff_done, b + 1)
                    nc.scalar.activation(p_near[u][:], near_diff[:], ACT.Exp, scale=RS).then_inc(p_done, 1)
                for s in range(NS):
                    if on[0]:
                        step(s)
                    if s == 0:
                        if on[0]:
                            max_copy(0, 1)
                        if on[2]:
                            qk()
                        if on[-1]:
                            ctx_copy(-1, 1)
                    if s == 1:
                        if on[1]:
                            vaug()
                        if on[2]:
                            qk2()
                    if s == 2 and on[-2]:
                        n, v, hn = at(-2)
                        act.wait_ge(oT_ps, n + 1)
                        nc.scalar.activation(o_T[:], X1[:, 0:S], ACT.Copy).then_inc(oT_cp, 1)
                    if s == 4 and on[1]:
                        max_copy(1, 0)
                    if s == 5 and on[0]:
                        ctx_copy(0, 0)

            pipeline(act, body)

        @block.vector
        def _(dve):
            dve.wait_ge(cst_in, 16 * NCST)
            nc.vector.tensor_tensor(bias_col[:, 3:4], bias_col[:, 1:2], bias_col[:, 2:3], ALU.add).then_inc(bias_done, 1)
            nc.vector.tensor_copy(bias_a[:, 0:E], b_rows[:, 0:E]).then_inc(bias_done, 1)
            for dst, first, entry in ((bias_a, E, 0), (bias_b, 0, 1), (bias_c, 0, 2)):
                for w, tab in ((0, rk_all), (1, rv_all)):
                    nc.vector.tensor_tensor(dst[:, first + w * E:first + (w + 1) * E].rearrange(hd, d=D),
                                            b_rows[:, (1 + w) * E:(2 + w) * E].rearrange(hd, d=D),
                                            tab[:, entry, None, :].to_broadcast([P, H, D]), ALU.add).then_inc(bias_done, 1)
            for w in range(2):
                for a in range(2):
                    cols = slice(a * E // 2, (a + 1) * E // 2)
                    nc.vector.tensor_copy(w_turn[:, w, cols].rearrange("p (d h) -> p d h", d=D),
                                          wqkv[:, w * E + a * E // 2:w * E + (a + 1) * E // 2]
                                          .rearrange("p (h d) -> p d h", d=D)).then_inc(bias_done, 1)
            dve.wait_ge(bias_done, 12)
            dve.wait_ge(zeroed, 6)
            nc.vector.tensor_copy(xb[0][:], xnT[:, 0:S]).then_inc(xb_done, 1)

            def body(at, on):
                b, u, hb = at(0)

                def tok(t):
                    n, v, hn = at(2)
                    dve.wait_ge(tok_ps, n * 2 + t + 1)
                    if t == 0 and on[0]:
                        dve.wait_ge(shift_in[v], hn * 64)
                        dve.wait_ge(pvn_done, b + 1)
                        dve.wait_ge(vaug_done, b + 1)
                    nc.vector.tensor_tensor(tok_a[v][:, t, :], X1[:, 0:3 * E], bias_a[:], ALU.add).then_inc(tok_ev, 1)
                    nc.vector.tensor_tensor(tok_b[v][:, t, :], X1[:, E:3 * E], bias_b[:], ALU.add).then_inc(tok_ev, 1)
                    nc.vector.tensor_tensor(near_kv[v][:, t, 0, :], X1[:, E:3 * E], bias_c[:], ALU.add).then_inc(tok_ev, 1)

                def max_step(s):
                    n, v, hn = at(1)
                    t, g = MAX_STEPS[s]
                    dve.wait_ge(max_ps, n * NS + s + 1)
                    w = 4 if t == 1 else 8
                    nc.vector.tensor_reduce(far_top[:, t, w * g:w * g + w], ps_max[:].rearrange("p (h k) -> p h k", h=w),
                                            AX.X, ALU.max).then_inc(max_rd, 1)

                def near_scores():
                    n, v, hn = at(1)
                    dve.wait_ge(prod_done, n + 1)
                    nc.vector.tensor_reduce(s_near[:], prod[:].rearrange("p t n (h d) -> p (t n) h d", d=D),
                                            AX.X, ALU.add).then_inc(sn_done, 1)
                    dve.wait_ge(sn_done, n * 3 + 1)
                    flat = s_near[:].rearrange("p t n h -> p (t n h)")
                    nc.vector.tensor_tensor(flat, flat, near_mask[:], ALU.add).then_inc(sn_done, 1)
                    dve.wait_ge(sn_done, n * 3 + 2)
                    nc.vector.tensor_reduce(near_top[:], s_near[:].rearrange("p t n h -> p t h n"),
                                            AX.X, ALU.max).then_inc(sn_done, 1)

                def row_max_half(half):
                    n, v, hn = at(1)
                    first = n * 12 + half * 6
                    hs = slice(half * HH, (half + 1) * HH)
                    m = row_max[:, :, hs]
                    mp = [max_parts[:, half, :, i, :] for i in range(3)]
                    dve.wait_ge(max_rd, n * NS + 3 * half + 3)
                    dve.wait_ge(sn_done, n * 3 + 3)
                    nc.vector.tensor_tensor(m, far_top[:, :, hs], near_top[:, :, hs], ALU.max).then_inc(mrow, 1)
                    dve.wait_ge(mrow, first + 1)
                    if on[0]:
                        dve.wait_ge(mT_ps, n * 2 - 1 + half)
                    nc.vector.tensor_scalar(mp[0], m, -1.0, None, ALU.mult).then_inc(mrow, 1)
                    dve.wait_ge(mrow, first + 2)
                    nc.vector.scalar_tensor_tensor(neg_res[0][:], m, -1.0, mp[0], ALU.mult, ALU.subtract).then_inc(mrow, 1)
                    dve.wait_ge(mrow, first + 3)
                    nc.vector.tensor_copy(mp[1], neg_res[0][:]).then_inc(mrow, 1)
                    dve.wait_ge(mrow, first + 4)
                    nc.vector.tensor_tensor(neg_res[1][:], neg_res[0][:], mp[1], ALU.subtract).then_inc(mrow, 1)
                    dve.wait_ge(mrow, first + 5)
                    nc.vector.tensor_copy(mp[2], neg_res[1][:]).then_inc(mrow, 1)

                def near_sums():
                    dve.wait_ge(p_done, b + 1)
                    nc.vector.tensor_reduce(den_near[u][:], p_near[u][:].rearrange("p t n h -> p t h n"),
                                            AX.X, ALU.add).then_inc(nn_done, 1)
                    dve.wait_ge(pvn_done, b + 1)
                    nc.vector.tensor_reduce(num_near[u][:], pv_near[:].rearrange("p t n e -> p t e n"),
                                            AX.X, ALU.add).then_inc(nn_done, 1)

                def out_tile(t):
                    n, v, hn = at(-1)
                    dve.wait_ge(cx_ps, n * 2 + t + 1)
                    if t == 0:
                        dve.wait_ge(nn_done, n * 2 + 2)
                    acc = X0[:].rearrange("p (h r) -> p h r", r=32)
                    nc.vector.tensor_tensor(den[:, t, :], acc[:, :, D], den_near[v][:, t, :], ALU.add).then_inc(nd, 1)
                    nc.vector.tensor_tensor(num[:, t, :].rearrange(hd, d=D), acc[:, :, 0:D],
                                            num_near[v][:, t, :].rearrange(hd, d=D), ALU.add).then_inc(nd, 1)
                    dve.wait_ge(nd, n * 4 + 2 * t + 1)
                    nc.vector.reciprocal(rden[:, t, :], den[:, t, :]).then_inc(fin, 1)
                    dve.wait_ge(fin, n * 4 + 2 * t + 1)
                    dve.wait_ge(nd, n * 4 + 2 * t + 2)
                    if t == 0 and on[-2]:
                        dve.wait_ge(oT_ps, n)
                    nc.vector.tensor_tensor(o_tok[:, t, :].rearrange(hd, d=D), num[:, t, :].rearrange(hd, d=D),
                                            rden[:, t, :, None].to_broadcast([P, H, D]), ALU.mult).then_inc(fin, 1)

                def store_out():
                    n, v, hn = at(-2)
                    dve.wait_ge(o_ps, n + 1)
                    nc.vector.tensor_tensor(attn_all[:, bass.ds(n * 2, 2), :],
                                            X1[:, 256:512].rearrange("p (t e) -> p t e", t=TT),
                                            bo_row[:, None, :].to_broadcast([P, TT, E]), ALU.add).then_inc(o_done, 1)

                for s in range(NS):
                    if on[1]:
                        max_step(s)
                    if s == 1 and on[2]:
                        tok(0)
                    if s == 1 and on[1]:
                        near_scores()
                    if s == 2 and on[1]:
                        row_max_half(0)
                    if s == 2 and on[-1]:
                        out_tile(0)
                    if s == 3 and on[-2]:
                        store_out()
                    if s == 3 and on[2]:
                        tok(1)
                    if s == 4 and on[-1]:
                        out_tile(1)
                    if s == 4 and on[0]:
                        near_sums()
                if on[1]:
                    row_max_half(1)
                    n, v, hn = at(1)
                    if on[0]:
                        dve.wait_ge(p_done, n)
                    dve.wait_ge(mrow, n * 12 + 7)
                    nc.vector.tensor_tensor(near_diff[:], s_near[:], row_max[:, :, None, :].to_broadcast([P, TT, NEAR, H]),
                                            ALU.subtract).then_inc(diff_done, 1)
                if on[3]:
                    n, v, hn = at(3)
                    if on[1]:
                        dve.wait_ge(tok_ps, (n - 1) * 2)
                    nc.vector.tensor_copy(xb[v][:], xnT[:, bass.ds(n * S, S)]).then_inc(xb_done, 1)

            pipeline(dve, body)

        @block.tensor
        def _(pe):
            pe.wait_ge(bias_done, 12)
            pe.wait_ge(zeroed, 6)

            def body(at, on):
                b, u, hb = at(0)

                def qk_proj():
                    n, v, hn = at(2)
                    pe.wait_ge(xb_done, n + 1)
                    if on[-2]:
                        pe.wait_ge(nd, b * 4 - 4)
                    elif on[1]:
                        pe.wait_ge(qk_cp, n * 2)
                    nc.tensor.matmul(X0[:, 0:S], w_turn[:, 0, :], xb[v][:], start=True, stop=True, skip_group_check=True)
                    nc.tensor.matmul(X0[:, S:], w_turn[:, 1, :], xb[v][:], start=True, stop=True,
                                     skip_group_check=True).then_inc(qk_ps, 1)

                def tok_proj(t):
                    n, v, hn = at(2)
                    if t == 0:
                        if on[0]:
                            pe.wait_ge(mT_cp, b * 2 + 2)
                        elif on[1]:
                            pe.wait_ge(tok_ev, n * 6)
                    else:
                        if on[-2]:
                            pe.wait_ge(o_done, b - 1)
                        else:
                            pe.wait_ge(tok_ev, n * 6 + 3)
                    nc.tensor.matmul(X1[:, 0:3 * E], xb[v][:, t * P:(t + 1) * P], wqkv[:], start=True, stop=True,
                                     skip_group_check=True).then_inc(tok_ps, 1)

                def max_step(s):
                    n, v, hn = at(1)
                    t, g = MAX_STEPS[s]
                    if s % 3 == 0:
                        pe.wait_ge(stack_in[v][s // 3], hn * NSTK + NSTK)
                    if s > 0 or on[0]:
                        pe.wait_ge(max_rd, n * NS + s)
                    q, k = q_st[v], k_st[v]
                    if t == 1:
                        for i in range(4):
                            nc.tensor.matmul(ps_max[:, i * S + P:(i + 1) * S], q[0:MAXROW, 4 * g + i, P:],
                                             k[0:MAXROW, 4 * g + i, P:], start=True, stop=True, skip_group_check=True)
                        for i in range(4):
                            last = nc.tensor.matmul(ps_max[:, i * S:i * S + P], q[EDGE:MAXROW, 4 * g + i, P:],
                                                    k[EDGE:MAXROW, 4 * g + i, 0:P], start=True, stop=True, skip_group_check=True)
                    else:
                        for i in range(8):
                            last = nc.tensor.matmul(ps_max[:, i * P:(i + 1) * P], q[0:MAXROW, 8 * g + i, 0:P],
                                                    k[0:MAXROW, 8 * g + i, 0:P], start=True, stop=True, skip_group_check=True)
                    last.then_inc(max_ps, 1)

                def exp_step(s):
                    t, g = EXP_STEPS[s]
                    if s % 3 == 0:
                        pe.wait_ge(mrow_in[s // 3], b * 48 + 48)
                    if s > 0 or on[-1]:
                        pe.wait_ge(exp_done, b * NS + s)
                    q, k = q_st[u], k_st[u]
                    if t == 0:
                        for i in range(4):
                            nc.tensor.matmul(ps_exp[:, i * S:i * S + P], k[0:ROWS, 4 * g + i, 0:P],
                                             q[0:ROWS, 4 * g + i, 0:P], start=True, stop=True, skip_group_check=True)
                        for i in range(4):
                            last = nc.tensor.matmul(ps_exp[:, i * S + P:(i + 1) * S], k[EDGE:ROWS, 4 * g + i, 0:P],
                                                    q[EDGE:ROWS, 4 * g + i, P:], start=True, stop=True, skip_group_check=True)
                    else:
                        for i in range(8):
                            last = nc.tensor.matmul(ps_exp[:, i * P:(i + 1) * P], k[0:ROWS, 8 * g + i, P:],
                                                    q[0:ROWS, 8 * g + i, P:], start=True, stop=True, skip_group_check=True)
                    last.then_inc(exp_ps, 1)

                def pv(k, s):
                    n, v, hn = at(k)
                    t, g = EXP_STEPS[s]
                    if s == 0:
                        pe.wait_ge(vaug_done, n + 1)
                    if s % 3 == 0 and on[-1]:
                        pe.wait_ge(ctx_cp, n * 2 - 1 + s // 3)
                    pe.wait_ge(exp_done, n * NS + s + 1)
                    for i in range(4 if t == 0 else 8):
                        h = 4 * g + i if t == 0 else 8 * g + i
                        gg, row = h // 4, 32 * (h % 4)
                        if t == 0:
                            last = nc.tensor.matmul(ps_ctx[row:row + 32, gg * S:(gg + 1) * S], v_aug[v][:, 0, h, :],
                                                    probs[s][:, i * S:(i + 1) * S], start=(gg % 2 == 0), stop=False,
                                                    skip_group_check=True)
                        else:
                            last = nc.tensor.matmul(ps_ctx[row:row + 32, gg * S + P:(gg + 1) * S], v_aug[v][:, 1, h, :],
                                                    probs[s][:, i * P:(i + 1) * P], start=False, stop=True,
                                                    skip_group_check=True)
                    if s % 3 == 2:
                        last.then_inc(ctx_ps, 1)

                def ctx_turn(t):
                    n, v, hn = at(-1)
                    if t == 0:
                        pe.wait_ge(ctx_cp, n * 2 + 2)
                        if on[2]:
                            pe.wait_ge(qk_cp, b * 2 + 6)
                        elif on[-2]:
                            pe.wait_ge(nd, b * 4 - 4)
                    else:
                        pe.wait_ge(nd, n * 4 + 2)
                    for g in range(4):
                        last = nc.tensor.transpose(X0[:, g * P:(g + 1) * P], ctx_T[:, g, t * P:(t + 1) * P], ident[:])
                    last.then_inc(cx_ps, 1)

                def max_turn(k, half):
                    n, v, hn = at(k)
                    pe.wait_ge(mrow, n * 12 + 6 * half + 6)
                    if half == 0:
                        if on[2]:
                            pe.wait_ge(tok_ev, (b + 2) * 6 + 6)
                        elif on[-2]:
                            pe.wait_ge(o_done, b - 1)
                    else:
                        pe.wait_ge(mT_cp, n * 2 + 1)
                    for t in range(TT):
                        last = nc.tensor.transpose(X1[0:3 * HH, t * P // 2:(t + 1) * P // 2].bitcast(BF16),
                                                   max_parts[:, half, t, :, :].rearrange("p n h -> p (n h)"), ident_bf[:])
                    last.then_inc(mT_ps, 1)

                def out_proj():
                    n, v, hn = at(-2)
                    pe.wait_ge(fin, n * 4 + 4)
                    if on[2]:
                        pe.wait_ge(tok_ev, (b + 2) * 6 + 3)
                    elif on[0]:
                        pe.wait_ge(mT_cp, b * 2 + 2)
                    else:
                        pe.wait_ge(o_done, b - 2)
                    for t in range(TT):
                        last = nc.tensor.transpose(X1[:, t * P:(t + 1) * P], o_tok[:, t, :], ident[:])
                    last.then_inc(oT_ps, 1)
                    pe.wait_ge(oT_cp, n + 1)
                    for t in range(TT):
                        last = nc.tensor.matmul(X1[:, 256 + t * P:256 + (t + 1) * P], o_T[:, t * P:(t + 1) * P], wo[:],
                                                start=True, stop=True, skip_group_check=True)
                    last.then_inc(o_ps, 1)

                for s in range(NS):
                    if on[1]:
                        max_step(s)
                    if on[0]:
                        exp_step(s)
                    if s == 0:
                        if on[-1]:
                            pv(-1, NS - 1)
                        if on[0]:
                            max_turn(0, 1)
                        if on[2]:
                            qk_proj()
                    if s == 1 and on[2]:
                        tok_proj(0)
                    if s == 2 and on[-2]:
                        out_proj()
                    if s == 2 and on[-1]:
                        ctx_turn(0)
                    if s == 3 and on[2]:
                        tok_proj(1)
                    if s == 4 and on[1]:
                        max_turn(1, 0)
                    if s == 4 and on[-1]:
                        ctx_turn(1)
                    if s > 0 and on[0]:
                        pv(0, s - 1)

            pipeline(pe, body)


def experts(nc, ctx, NT, x_t, xnT, attn_all, mask_all, w1, b1, w2, b2, out_t):
    def sb(name, shape, dt=F32):
        return ctx.enter_context(nc.sbuf_tensor(name, shape, dt))

    def sem(name):
        return ctx.enter_context(nc.semaphore(name))

    CH = 4
    NCH = NT // CH
    x_all = sb("x_again", [P, NT, E])
    w1_sb = sb("w1_sb", [P, NEXP, FFN])
    w2_sb = sb("w2_sb", [P, NEXP, FC, E])
    b1_sb = sb("b1_sb", [P, NEXP, FC])
    b2_row = sb("b2_row", [P, NEXP, E])
    hT = [sb(f"hT{i}", [P, FC, CH * P]) for i in range(2)]
    yb = sb("yb", [P, CH, E])
    acc = sb("acc", [P, CH, E])
    sg = sb("sg", [P, CH, E])
    ps_h = [ctx.enter_context(nc.psum_tensor(f"ps_h{i}", [P, CH * P], F32)) for i in range(4)]
    ps_y = [ctx.enter_context(nc.psum_tensor(f"ps_y{i}", [P, CH, E], F32)) for i in range(2)]
    w_in = sem("w_in")
    h_ps = sem("h_ps")
    h_cp = sem("h_cp")
    y_ps = sem("y_ps")
    y_rd = sem("y_rd")
    ac = sem("ac")
    sgs = sem("sgs")
    fin2 = sem("fin2")
    sgs2 = sem("sgs2")
    st_out = sem("st_out")
    with nc.Block() as block:
        @block.sync
        def _(sp):
            sp.dma_start(w1_sb[:], w1.rearrange("e p f -> p e f")).then_inc(w_in, 16)
            for e in range(NEXP):
                sp.dma_start(w2_sb[:, e, :, :], w2[e].rearrange("(c p) n -> p c n", p=P)).then_inc(w_in, 16)
            sp.dma_start(b1_sb[:], b1.rearrange("e (c p) -> p e c", p=P), allow_slow_non_contiguous=True).then_inc(w_in, 16)
            sp.dma_start(b2_row[:], b2[None, :, :].to_broadcast([P, NEXP, E])).then_inc(w_in, 16)
            sp.dma_start(x_all[:], x_t).then_inc(w_in, 16)
            with sp.Fori(0, NCH) as k:
                sp.wait_ge(fin2, k + 1)
                sp.dma_start(out_t[:, bass.ds(k * CH, CH), :], x_all[:, bass.ds(k * CH, CH), :]).then_inc(st_out, 16)
            sp.wait_ge(st_out, 16 * NCH)

        @block.tensor
        def _(pe):
            pe.wait_ge(w_in, 16 * 12)
            pe.sem_inc(h_cp, 4)
            pe.sem_inc(y_rd, 2)
            pe.sem_inc(y_ps, 2)

            def down(k, e):
                pe.wait_ge(h_cp, k * 32 + 4 * e + 8)
                pe.wait_ge(y_rd, k * 8 + e + 1)
                for t in range(CH):
                    for f in range(FC):
                        last = nc.tensor.matmul(ps_y[e % 2][:, t, :], hT[e % 2][:, f, t * P:(t + 1) * P], w2_sb[:, e, f, :],
                                                start=(f == 0), stop=(f == FC - 1))
                last.then_inc(y_ps, 1)

            with pe.Fori(0, NCH) as k:
                for e in range(NEXP):
                    for f in range(FC):
                        pe.wait_ge(h_cp, k * 32 + (4 * e + f + 1))
                        nc.tensor.matmul(ps_h[f][:], w1_sb[:, e, f * P:(f + 1) * P], xnT[:, bass.ds(k * CH * P, CH * P)],
                                         start=True, stop=True).then_inc(h_ps, 1)
                    if e > 0:
                        down(k, e - 1)
                down(k, NEXP - 1)

        @block.scalar
        def _(act):
            act.wait_ge(w_in, 16 * 12)
            with act.Fori(0, NCH) as k:
                for e in range(NEXP):
                    for f in range(FC):
                        act.wait_ge(h_ps, k * 32 + 4 * e + f + 1)
                        if f == 0:
                            act.wait_ge(y_ps, k * 8 + (e + 1))
                        nc.scalar.activation(hT[e % 2][:, f, :], ps_h[f][:], ACT.Relu,
                                             bias=b1_sb[:, e, f:f + 1]).then_inc(h_cp, 1)
                act.wait_ge(ac, k * 33 + 33)
                nc.scalar.activation(sg[:], acc[:], ACT.Silu).then_inc(sgs, 1)

        @block.vector
        def _(dve):
            dve.wait_ge(w_in, 16 * 12)
            with dve.Fori(0, NCH) as k:
                nc.vector.memset(acc[:], 0.0).then_inc(ac, 1)
                n = 1
                for e in range(NEXP):
                    dve.wait_ge(y_ps, k * 8 + e + 3)
                    dve.wait_ge(ac, k * 33 + n)
                    nc.vector.tensor_tensor(yb[:], ps_y[e % 2][:], b2_row[:, e:e + 1, :].to_broadcast([P, CH, E]),
                                            ALU.add).then_inc(y_rd, 1)
                    dve.wait_ge(y_rd, k * 8 + e + 3)
                    for t in range(CH):
                        last = nc.vector.scalar_tensor_tensor(acc[:, t, :], yb[:, t, :],
                                                              mask_all[:, bass.ds(k * CH + t, 1), e],
                                                              acc[:, t, :], ALU.mult, ALU.add).then_inc(ac, 1)
                        n += 1
                dve.wait_ge(sgs, k + 1)
                nc.vector.tensor_tensor(sg[:], sg[:], attn_all[:, bass.ds(k * CH, CH), :], ALU.mult).then_inc(sgs2, 1)
                dve.wait_ge(sgs2, k + 1)
                nc.vector.tensor_tensor(x_all[:, bass.ds(k * CH, CH), :], x_all[:, bass.ds(k * CH, CH), :], sg[:],
                                        ALU.add).then_inc(fin2, 1)

    return


NAMES = ["L0_attn_x", "L0_attn_W_q", "L0_attn_b_q", "L0_attn_W_k", "L0_attn_b_k", "L0_attn_W_v", "L0_attn_b_v",
         "L0_attn_W_o", "L0_attn_b_o", "L0_attn_rel_k_table", "L0_attn_rel_v_table", "L0_ffn_gate_w", "L0_ffn_gate_b",
         "L0_ffn_w1", "L0_ffn_b1", "L0_ffn_w2", "L0_ffn_b2"]


def kernel(**inputs):
    import concourse.bacc as bacc
    from concourse.bass_utils import run_bass_kernel_spmd

    nc = bacc.Bacc("TRN2", target_bir_lowering=False, num_devices=1)
    arrays, args = {}, []
    for name in NAMES:
        a = np.ascontiguousarray(inputs[name])
        arrays[f"in_{name}"] = a
        args.append(nc.dram_tensor(f"in_{name}", a.shape, mybir.dt.from_np(a.dtype), kind="ExternalInput").ap())
    shape = arrays["in_L0_attn_x"].shape
    consts = {}
    for name, a in shape_constants(shape[0]).items():
        arrays[name] = a
        consts[name] = nc.dram_tensor(name, a.shape, mybir.dt.from_np(a.dtype), kind="ExternalInput").ap()
    out = nc.dram_tensor("out_0_dram", shape, F32, kind="ExternalOutput").ap()
    program(nc, *args, consts, out)
    r = run_bass_kernel_spmd(nc, [arrays], core_ids=[0])
    return r.results[0]["out_0_dram"]
```

```python
from contextlib import ExitStack

import concourse.bass as bass
import numpy as np
from concourse import mybir

F32 = mybir.dt.float32
U32 = mybir.dt.uint32
BF16 = mybir.dt.bfloat16
ALU = mybir.AluOpType
ACT = mybir.ActivationFunctionType
AX = mybir.AxisListType

P = 128
S = 256
E = 128
H = 16
D = E // H
TT = S // P
NEAR = 3
FFN = 512
NEXP = 8
FC = FFN // P
TOPK = 2
SLOT_T = 256
RING = 8
PADS = RING * SLOT_T // P
EPS = 1e-5
NEG = -1.0e9

PAIRS = P // 2
EDGE = PAIRS
PROD = EDGE + 1
Q_PARTS = [0, 0, 0, 1, 1, 2]
K_PARTS = [2, 0, 1, 0, 1, 0]
MAXROW = PROD + len(Q_PARTS) * D
ROWS = MAXROW + 3


def expert_tiles(nb):
    return -(-(nb * S * TOPK // SLOT_T + NEXP - 1) // RING) * RING


def shape_constants(nb):
    tokens = nb * S
    ntile = expert_tiles(nb)
    ids = (np.arange(TOPK)[:, None] * tokens + np.arange(tokens)).astype(np.uint32)
    pad = np.zeros((P, PADS, E + 1), np.uint32)
    pad[:, :, E] = TOPK * tokens + np.arange(PADS) * P + np.arange(P)[:, None]
    bf = mybir.dt.np(BF16)
    q = np.arange(S)
    stair_q = np.zeros((PROD, S), np.float32)
    stair_q[(q % P) // 2, q] = 1.0
    stair_q[EDGE, P:P + 2] = 1.0
    stair_k = np.zeros((PROD, S), np.float32)
    for j in range(PAIRS):
        stair_k[j, (q % P) > 2 * j - 2] = NEG
    stair_k[EDGE, P - 1] = NEG
    near = np.zeros((P, TT, NEAR, H), np.float32)
    near[0::2, :, 2] = NEG
    near[0, 0, 1] = NEG
    near[0:2, 0, 2] = NEG
    return {
        "c_stair_q": stair_q.astype(bf), "c_stair_k": stair_k.astype(bf),
        "c_ones": np.ones((3, S), bf),
        "c_near": near.reshape(P, TT * NEAR * H),
        "c_dest": np.ascontiguousarray(ids.reshape(TOPK, tokens // P, P).transpose(2, 0, 1)),
        "c_pad": pad.view(np.float32),
        "c_before": np.triu(np.ones((P, P), np.float32), 1), "c_all": np.ones((P, P), np.float32),
        "c_tile": np.broadcast_to(np.arange(ntile, dtype=np.float32), (P, ntile)).copy(),
        "c_tile_start": np.broadcast_to(SLOT_T * np.arange(ntile, dtype=np.float32), (P, ntile)).copy(),
        "c_ident": np.eye(P, dtype=np.float32), "c_ident_bf": np.eye(P).astype(bf),
    }


def program(nc, x, W_q, b_q, W_k, b_k, W_v, b_v, W_o, b_o, rel_k, rel_v, gate_w, gate_b,
            w1, b1, w2, b2, c, out):
    NB = x.shape[0]
    NT = NB * TT
    CH = 4
    NCH = NT // CH
    RS = float(D) ** -0.5

    x_t = x.rearrange("b (t p) e -> p (b t) e", p=P)
    out_t = out.rearrange("b (t p) e -> p (b t) e", p=P)

    with ExitStack() as ctx:
        def sb(name, shape, dt=F32):
            return ctx.enter_context(nc.sbuf_tensor(name, shape, dt))

        def sem(name):
            return ctx.enter_context(nc.semaphore(name))

        N = NB * S
        NTILE = expert_tiles(NB)
        attn_all = sb("attn_all", [P, NT, E])
        ident = sb("ident", [P, P])
        ident_bf = sb("ident_bf", [P, P], BF16)
        wqkv = sb("wqkv", [P, 3 * E])
        wo = sb("wo", [P, E])
        bo_row = sb("bo_row", [P, E])
        b1_sb = sb("b1_sb", [P, NEXP, FC])
        pos_all = sb("pos_all", [P, NT, TOPK], U32)
        dest_all = sb("dest_all", [P, TOPK, NT], U32)
        tile_expert = sb("tile_expert", [P, NTILE], U32)
        turned = ctx.enter_context(ExitStack())
        xnT = turned.enter_context(nc.sbuf_tensor("xnT", [P, NT * P], F32))
        xn_dram = nc.dram_tensor("xn_dram", [P, NT, E], F32, kind="Internal").ap()
        xd = nc.dram_tensor("slots_dram", [NTILE * SLOT_T, E + 1], F32, kind="Internal").ap()
        pad_out = sem("pad_out")

        with ExitStack() as c0:
            def sb0(name, shape, dt=F32):
                return c0.enter_context(nc.sbuf_tensor(name, shape, dt))

            x_all = sb0("x_all", [P, NT, E])
            pad = sb0("pad", [P, PADS, E + 1])
            stats = sb0("stats", [P, NT, 6])
            mean = sb0("mean", [P, NT])
            diff = sb0("diff", [P, NT])
            var = sb0("var", [P, NT])
            rstd = sb0("rstd", [P, NT])
            eps = sb0("eps", [P, 1])
            gw = sb0("gw", [P, NEXP])
            gb_row = sb0("gb_row", [P, NEXP])
            before = sb0("before", [P, P])
            ones = sb0("ones", [P, P])
            tile_no = sb0("tile_no", [P, NTILE])
            tile_start = sb0("tile_start", [P, NTILE])
            xn_chunk = [sb0(f"xn_chunk{i}", [P, CH, E]) for i in range(2)]
            gT = [sb0(f"gT{i}", [NEXP, CH * P]) for i in range(2)]
            logits = sb0("logits", [P, NT, NEXP])
            top = sb0("top", [P, NT])
            ex = sb0("ex", [P, NT, NEXP])
            esum = sb0("esum", [P, NT])
            beats = sb0("beats", [P, NT, NEXP, NEXP])
            rank = sb0("rank", [P, NT, NEXP])
            chosen = sb0("chosen", [P, NT, NEXP])
            choice = sb0("choice", [P, TOPK, NT, NEXP])
            upto = [sb0(f"upto{i}", [P, NT, NEXP]) for i in range(2)]
            place = sb0("place", [P, NT, NEXP])
            tiles_over = sb0("tiles_over", [P, NEXP, NTILE])
            tiles_of = sb0("tiles_of", [P, NEXP])
            tiles_upto = [sb0(f"tiles_upto{i}", [P, NEXP]) for i in range(2)]
            base = sb0("base", [P, NEXP])
            experts_over = sb0("experts_over", [P, NTILE, NEXP])
            expert_no = sb0("expert_no", [P, NTILE])
            pos = sb0("pos", [P, NT, TOPK])
            ps_t = [c0.enter_context(nc.psum_tensor(f"ps_t{i}", [P, CH * P], F32)) for i in range(2)]
            ps_g = [c0.enter_context(nc.psum_tensor(f"ps_g{i}", [NEXP, CH * P], F32)) for i in range(2)]
            ps_l = c0.enter_context(nc.psum_tensor("ps_l", [P, NT, NEXP], F32))
            ps_before = c0.enter_context(nc.psum_tensor("ps_before", [P, NT, NEXP], F32))
            ps_total = c0.enter_context(nc.psum_tensor("ps_total", [P, NT, NEXP], F32))

            NG = max(NCH // 4, 1)
            GT, GC = NT // NG, NCH // NG
            x_in = [sem(f"x_in{g}") for g in range(NG)]
            wt_in = sem("wt_in")
            pad_in = sem("pad_in")
            dest_in = sem("dest_in")
            stat_done = sem("stat_done")
            mv_done = sem("mv_done")
            std_done = sem("std_done")
            rstd_done = sem("rstd_done")
            eps_done = sem("eps_done")
            xn_done = sem("xn_done")
            xn_out = [sem(f"xn_out{i}") for i in range(2)]
            tr_done = sem("tr_done")
            xT_done = sem("xT_done")
            gate_done = sem("gate_done")
            gT_done = sem("gT_done")
            lg_ps = sem("lg_ps")
            route = sem("route")
            ex_done = sem("ex_done")
            count_ps = sem("count_ps")

            WT = 16 * 14
            R_SHIFTED, R_CHOSEN = 3, 7 + 2 * NEXP

            with nc.Block() as block:
                @block.sync
                def _(sp):
                    for i in range(2):
                        sp.sem_inc(xn_out[i], 16)
                    for g in range(NG):
                        sp.dma_start(x_all[:, g * GT:(g + 1) * GT, :], x_t[:, g * GT:(g + 1) * GT, :]).then_inc(x_in[g], 16)
                    sp.dma_start(b1_sb[:], b1.rearrange("e (c p) -> p e c", p=P), allow_slow_non_contiguous=True).then_inc(wt_in, 16)
                    with sp.Fori(0, NCH // 2) as k:
                        for u in range(2):
                            sp.wait_ge(xn_done, k * 2 * CH + (u + 1) * CH)
                            sp.dma_start(xn_dram[:, bass.ds(k * 2 * CH + u * CH, CH), :], xn_chunk[u][:]).then_inc(xn_out[u], 16)
                    for i in range(2):
                        sp.wait_ge(xn_out[i], 16 + 16 * (NCH // 2))

                @block.gpsimd
                def _(pool):
                    pool.wait_ge(pad_in, 16)
                    pool.wait_ge(x_in[NG - 1], 16)
                    slots = xd.rearrange("(m j p) e -> j p m e", j=PADS, p=P)
                    for j in range(PADS):
                        pool.dma_start(slots[j], pad[:, j, None, :].to_broadcast([P, NTILE * SLOT_T // P // PADS, E + 1])
                                       ).then_inc(pad_out, 16)

                @block.vector
                def _(dve):
                    nc.vector.memset(eps[:], EPS).then_inc(eps_done, 1)

                    def statistics(g):
                        dve.wait_ge(x_in[g], 16)
                        with dve.Fori(g * GC, (g + 1) * GC) as k:
                            for t in range(CH):
                                nc.vector.bn_stats(stats[:, bass.ds(k * CH + t, 1), :].rearrange("p a e -> p (a e)"),
                                                   x_all[:, bass.ds(k * CH + t, 1), :]
                                                   .rearrange("p a e -> p (a e)")).then_inc(stat_done, 1)
                        ts = slice(g * GT, (g + 1) * GT)
                        me, mo, ve, vo = (stats[:, ts, i] for i in (1, 4, 2, 5))
                        dve.wait_ge(stat_done, (g + 1) * GT)
                        nc.vector.tensor_tensor(mean[:, ts], me, mo, ALU.add).then_inc(mv_done, 1)
                        nc.vector.tensor_tensor(diff[:, ts], me, mo, ALU.subtract).then_inc(mv_done, 1)
                        nc.vector.tensor_tensor(var[:, ts], ve, vo, ALU.add).then_inc(mv_done, 1)
                        dve.wait_ge(mv_done, g * 6 + 2)
                        nc.vector.tensor_scalar(mean[:, ts], mean[:, ts], 0.5, None, ALU.mult).then_inc(mv_done, 1)
                        nc.vector.tensor_tensor(diff[:, ts], diff[:, ts], diff[:, ts], ALU.mult).then_inc(mv_done, 1)
                        dve.wait_ge(mv_done, g * 6 + 5)
                        nc.vector.scalar_tensor_tensor(var[:, ts], diff[:, ts], E / 4.0, var[:, ts],
                                                       ALU.mult, ALU.add).then_inc(mv_done, 1)

                    def normalise(g):
                        ts = slice(g * GT, (g + 1) * GT)
                        dve.wait_ge(std_done, g + 1)
                        nc.vector.reciprocal(rstd[:, ts], rstd[:, ts]).then_inc(rstd_done, 1)
                        dve.wait_ge(rstd_done, g + 1)
                        with dve.Fori(g * GC // 2, (g + 1) * GC // 2) as k:
                            for u in range(2):
                                dve.wait_ge(tr_done, k * 2 + (u + 1))
                                dve.wait_ge(xn_out[u], k * 16 + 16)
                                for t in range(CH):
                                    i = k * 2 * CH + (u * CH + t)
                                    nc.vector.tensor_scalar(xn_chunk[u][:, t, :], x_all[:, bass.ds(i, 1), :]
                                                            .rearrange("p a e -> p (a e)"),
                                                            mean[:, bass.ds(i, 1)], rstd[:, bass.ds(i, 1)],
                                                            ALU.subtract, ALU.mult).then_inc(xn_done, 1)

                    statistics(0)
                    for g in range(NG):
                        if g + 1 < NG:
                            statistics(g + 1)
                        normalise(g)

                    steps = [0]

                    def step(instruction):
                        instruction.then_inc(route, 1)
                        steps[0] += 1

                    per_tile = [P, NT, NEXP]
                    dve.wait_ge(wt_in, WT)
                    dve.wait_ge(lg_ps, NCH)
                    step(nc.vector.tensor_tensor(logits[:], ps_l[:], gb_row[:, None, :].to_broadcast(per_tile), ALU.add))
                    dve.wait_ge(route, steps[0])
                    step(nc.vector.tensor_reduce(top[:], logits[:], AX.X, ALU.max))
                    dve.wait_ge(route, steps[0])
                    step(nc.vector.tensor_tensor(logits[:], logits[:], top[:, :, None].to_broadcast(per_tile), ALU.subtract))
                    assert steps[0] == R_SHIFTED
                    dve.wait_ge(ex_done, 1)
                    step(nc.vector.tensor_reduce(esum[:], ex[:], AX.X, ALU.add))
                    dve.wait_ge(route, steps[0])
                    step(nc.vector.reciprocal(top[:], esum[:]))
                    dve.wait_ge(route, steps[0])
                    step(nc.vector.tensor_tensor(ex[:], ex[:], top[:, :, None].to_broadcast(per_tile), ALU.mult))
                    dve.wait_ge(route, steps[0])
                    for f in range(NEXP):
                        for lo, hi, op in ((0, f + 1, ALU.is_gt), (f + 1, NEXP, ALU.is_ge)):
                            if lo < hi:
                                step(nc.vector.tensor_tensor(beats[:, :, lo:hi, f],
                                                             ex[:, :, f:f + 1].to_broadcast([P, NT, hi - lo]),
                                                             ex[:, :, lo:hi], op))
                    dve.wait_ge(route, steps[0])
                    step(nc.vector.tensor_reduce(rank[:], beats[:], AX.X, ALU.add))
                    dve.wait_ge(route, steps[0])
                    step(nc.vector.tensor_scalar(chosen[:], rank[:], float(TOPK), None, ALU.is_lt))
                    assert steps[0] == R_CHOSEN
                    for s in range(TOPK):
                        step(nc.vector.tensor_scalar(choice[:, s], rank[:], float(s), None, ALU.is_equal))
                    dve.wait_ge(count_ps, 2)
                    step(nc.vector.tensor_copy(upto[0][:], ps_total[:]))
                    dve.wait_ge(route, steps[0])
                    cur, shift = 0, 1
                    while shift < NT:
                        step(nc.vector.tensor_tensor(upto[1 - cur][:, shift:], upto[cur][:, shift:],
                                                     upto[cur][:, :NT - shift], ALU.add))
                        step(nc.vector.tensor_copy(upto[1 - cur][:, 0:shift], upto[cur][:, 0:shift]))
                        dve.wait_ge(route, steps[0])
                        cur, shift = 1 - cur, shift * 2
                    total, spare = upto[cur], upto[1 - cur]
                    step(nc.vector.tensor_tensor(spare[:], total[:], ps_total[:], ALU.subtract))
                    wide = [P, NEXP, NTILE]
                    step(nc.vector.tensor_tensor(tiles_over[:], total[:, NT - 1, :, None].to_broadcast(wide),
                                                 tile_start[:, None, :].to_broadcast(wide), ALU.is_gt))
                    dve.wait_ge(route, steps[0])
                    step(nc.vector.tensor_tensor(place[:], spare[:], ps_before[:], ALU.add))
                    step(nc.vector.tensor_reduce(tiles_of[:], tiles_over[:], AX.X, ALU.add))
                    dve.wait_ge(route, steps[0])
                    step(nc.vector.tensor_copy(tiles_upto[0][:], tiles_of[:]))
                    dve.wait_ge(route, steps[0])
                    cur, shift = 0, 1
                    while shift < NEXP:
                        step(nc.vector.tensor_tensor(tiles_upto[1 - cur][:, shift:], tiles_upto[cur][:, shift:],
                                                     tiles_upto[cur][:, :NEXP - shift], ALU.add))
                        step(nc.vector.tensor_copy(tiles_upto[1 - cur][:, 0:shift], tiles_upto[cur][:, 0:shift]))
                        dve.wait_ge(route, steps[0])
                        cur, shift = 1 - cur, shift * 2
                    step(nc.vector.tensor_tensor(base[:], tiles_upto[cur][:], tiles_of[:], ALU.subtract))
                    step(nc.vector.tensor_tensor(experts_over[:], tile_no[:, :, None].to_broadcast([P, NTILE, NEXP]),
                                                 tiles_upto[cur][:, None, :].to_broadcast([P, NTILE, NEXP]), ALU.is_ge))
                    dve.wait_ge(route, steps[0])
                    step(nc.vector.tensor_scalar(base[:], base[:], float(SLOT_T), None, ALU.mult))
                    step(nc.vector.tensor_reduce(expert_no[:], experts_over[:], AX.X, ALU.add))
                    dve.wait_ge(route, steps[0])
                    step(nc.vector.tensor_scalar(tile_expert[:], expert_no[:], float(NEXP - 1), None, ALU.min))
                    step(nc.vector.tensor_tensor(place[:], place[:], base[:, None, :].to_broadcast(per_tile), ALU.add))
                    dve.wait_ge(route, steps[0])
                    for s in range(TOPK):
                        step(nc.vector.tensor_tensor(choice[:, s], choice[:, s], place[:], ALU.mult))
                    dve.wait_ge(route, steps[0])
                    for s in range(TOPK):
                        step(nc.vector.tensor_reduce(pos[:, :, s], choice[:, s], AX.X, ALU.add))
                    dve.wait_ge(route, steps[0])
                    step(nc.vector.tensor_copy(pos_all[:], pos[:]))

                @block.tensor
                def _(pe):
                    pe.sem_inc(tr_done, 2)
                    pe.wait_ge(wt_in, WT)

                    def turn(k, u):
                        pe.wait_ge(xn_done, k * 2 * CH + (u + 1) * CH)
                        pe.wait_ge(xT_done, k * 2 + (u + 1))
                        for t in range(CH):
                            last = nc.tensor.transpose(ps_t[u % 2][:, t * P:(t + 1) * P], xn_chunk[u % 2][:, t, :], ident[:])
                        last.then_inc(tr_done, 1)

                    def gate(k, u):
                        pe.wait_ge(xT_done, k * 2 + (u + 3))
                        nc.tensor.matmul(ps_g[u % 2][:], gw[:], xnT[:, bass.ds(k * 2 * CH * P + u * CH * P, CH * P)],
                                         start=True, stop=True).then_inc(gate_done, 1)

                    def turn_back(k, u):
                        pe.wait_ge(gT_done, k * 2 + (u + 1))
                        for t in range(CH):
                            last = nc.tensor.matmul(ps_l[:, bass.ds(k * 2 * CH + (u * CH + t), 1), :].rearrange("p a e -> p (a e)"),
                                                    gT[u % 2][:, t * P:(t + 1) * P],
                                                    ident[0:NEXP, 0:NEXP], start=True, stop=True, skip_group_check=True)
                        last.then_inc(lg_ps, 1)

                    turn(0, 0)
                    turn(0, 1)
                    gate(0, 0)
                    with pe.Fori(0, NCH // 2 - 1) as k:
                        for u in range(2):
                            turn(k, u + 2)
                            turn_back(k, u)
                            gate(k, u + 1)
                    turn_back(NCH // 2 - 1, 0)
                    gate(NCH // 2 - 1, 1)
                    turn_back(NCH // 2 - 1, 1)
                    pe.wait_ge(route, R_CHOSEN)
                    nc.tensor.matmul(ps_total[:], ones[:], chosen[:], start=True, stop=True).then_inc(count_ps, 1)
                    nc.tensor.matmul(ps_before[:], before[:], chosen[:], start=True, stop=True).then_inc(count_ps, 1)

                @block.scalar
                def _(act):
                    act.sem_inc(xT_done, 2)
                    act.dma_start(ident[:], c["c_ident"]).then_inc(wt_in, 16)
                    act.dma_start(gw[:], gate_w).then_inc(wt_in, 16)
                    act.dma_start(gb_row[:], gate_b[None, :].to_broadcast([P, NEXP])).then_inc(wt_in, 16)
                    act.dma_start(ones[:], c["c_all"]).then_inc(wt_in, 16)
                    act.dma_start(before[:], c["c_before"]).then_inc(wt_in, 16)
                    act.dma_start(pad[:], c["c_pad"]).then_inc(pad_in, 16)
                    act.dma_start(tile_no[:], c["c_tile"]).then_inc(wt_in, 16)
                    act.dma_start(tile_start[:], c["c_tile_start"]).then_inc(wt_in, 16)
                    act.dma_start(ident_bf[:], c["c_ident_bf"]).then_inc(wt_in, 16)
                    act.dma_start(bo_row[:], b_o[None, :].to_broadcast([P, E])).then_inc(wt_in, 16)
                    act.dma_start(wqkv[:, 0:E], W_q).then_inc(wt_in, 16)
                    act.dma_start(wqkv[:, E:2 * E], W_k).then_inc(wt_in, 16)
                    act.dma_start(wqkv[:, 2 * E:], W_v).then_inc(wt_in, 16)
                    act.dma_start(wo[:], W_o).then_inc(wt_in, 16)
                    act.dma_start(dest_all[:], c["c_dest"]).then_inc(dest_in, 16)
                    act.wait_ge(eps_done, 1)

                    def deviation(g):
                        ts = slice(g * GT, (g + 1) * GT)
                        act.wait_ge(mv_done, (g + 1) * 6)
                        nc.scalar.activation(rstd[:, ts], var[:, ts], ACT.Sqrt, bias=eps[:], scale=1.0 / E).then_inc(std_done, 1)

                    deviation(0)
                    for g in range(NG):
                        if g + 1 < NG:
                            deviation(g + 1)
                        with act.Fori(g * GC // 2, (g + 1) * GC // 2) as k:
                            for u in range(2):
                                act.wait_ge(tr_done, k * 2 + (u + 3))
                                nc.scalar.activation(xnT[:, bass.ds(k * 2 * CH * P + u * CH * P, CH * P)], ps_t[u][:],
                                                     ACT.Copy).then_inc(xT_done, 1)
                                act.wait_ge(gate_done, k * 2 + (u + 1))
                                nc.scalar.activation(gT[u][:], ps_g[u][:], ACT.Copy).then_inc(gT_done, 1)
                    act.wait_ge(route, R_SHIFTED)
                    nc.scalar.activation(ex[:], logits[:], ACT.Exp).then_inc(ex_done, 1)
                    act.wait_ge(dest_in, 16)

        with ExitStack() as c1:
            attention(nc, c1, NB, RS, xnT, attn_all, wqkv, wo, ident, ident_bf, bo_row,
                      b_q, b_k, b_v, rel_k, rel_v, c, xn_dram, xd, pos_all, dest_all, pad_out)

        turned.close()
        with ExitStack() as c2:
            experts(nc, c2, NT, x_t, attn_all, tile_expert, ident, b1_sb, w1, w2, b2, xd, out_t)


def attention(nc, ctx, NB, RS, xnT, attn_all, wqkv, wo, ident, ident_bf, bo_row, b_q, b_k, b_v, rel_k, rel_v, c,
              xn_dram, xd, pos_all, dest_all, pad_out):
    def sb(name, shape, dt=F32):
        return ctx.enter_context(nc.sbuf_tensor(name, shape, dt))

    def sem(name):
        return ctx.enter_context(nc.semaphore(name))

    def bank(name, n=1):
        return ctx.enter_context(nc.psum_tensor(name, [P, n * 512], F32))

    HH = H // 2
    NP = len(Q_PARTS)
    q_st = [sb(f"q_st{i}", [P, H, S], BF16) for i in range(2)]
    k_st = [sb(f"k_st{i}", [P, H, S], BF16) for i in range(2)]
    w_turn = sb("w_turn", [P, 2, E])
    xb = [sb(f"xb{i}", [P, S]) for i in range(2)]
    qk32 = sb("qk32", [P, 2, S])
    rem = sb("rem", [P, 2, S])
    parts = [sb(f"parts{i}", [P, 2, NP, S], BF16) for i in range(2)]
    parts_dram = [nc.dram_tensor(f"parts_dram{i}", [2, NP, P, S], BF16, kind="Internal").ap() for i in range(2)]
    tok_a = [sb(f"tok_a{i}", [P, TT, 3 * E]) for i in range(2)]
    tok_b = [sb(f"tok_b{i}", [P, TT, 2 * E]) for i in range(2)]
    near_kv = [sb(f"near_kv{i}", [P, TT, NEAR, 2 * E]) for i in range(2)]
    v_aug = [sb(f"v_aug{i}", [P, TT, H, 32]) for i in range(2)]
    prod = sb("prod", [P, TT, NEAR, E])
    pv_near = sb("pv_near", [P, TT, NEAR, E])
    s_near = sb("s_near", [P, TT, NEAR, H])
    near_top = sb("near_top", [P, TT, H])
    far_top = sb("far_top", [P, TT, H])
    row_max = sb("row_max", [P, TT, H])
    neg_res = [sb(f"neg_res{i}", [P, TT, HH]) for i in range(2)]
    max_parts = sb("max_parts", [P, 2, TT, 3, HH], BF16)
    max_T = [sb(f"max_T{i}", [3 * HH, S], BF16) for i in range(2)]
    near_diff = sb("near_diff", [P, TT, NEAR, H])
    p_near = [sb(f"p_near{i}", [P, TT, NEAR, H]) for i in range(2)]
    num_near = [sb(f"num_near{i}", [P, TT, E]) for i in range(2)]
    den_near = [sb(f"den_near{i}", [P, TT, H]) for i in range(2)]
    probs = [sb(f"probs{i}", [P, 1024]) for i in range(6)]
    ctx_T = sb("ctx_T", [P, 4, S])
    num = sb("num", [P, TT, E])
    den = sb("den", [P, TT, H])
    rden = sb("rden", [P, TT, H])
    o_tok = [sb(f"o_tok{i}", [P, TT, E]) for i in range(2)]
    o_T = sb("o_T", [P, S])
    near_mask = sb("near_mask", [P, TT * NEAR * H])
    bias_col = sb("bias_col", [P, 4])
    rk_all = sb("rk_all", [P, NEAR, D])
    rv_all = sb("rv_all", [P, NEAR, D])
    b_rows = sb("b_rows", [P, 3 * E])
    bias_a = sb("bias_a", [P, 3 * E])
    bias_b = sb("bias_b", [P, 2 * E])
    bias_c = sb("bias_c", [P, 2 * E])

    ps_max = bank("ps_max", 2)
    ps_exp = bank("ps_exp", 2)
    ps_ctx = bank("ps_ctx", 2)
    X0 = bank("ps_x0")
    X1 = bank("ps_x1")

    stage = sb("stage", [P, TOPK, TT, E + 1])
    stage_pos = sb("stage_pos", [P, TT, TOPK], U32)

    staged = sem("staged")
    tagged = sem("tagged")
    stage_ready = sem("stage_ready")
    scattered = sem("scattered")
    cst_in = sem("cst_in")
    zeroed = sem("zeroed")
    bias_done = sem("bias_done")
    xb_done = sem("xb_done")
    qk_ps = sem("qk_ps")
    qk_cp = sem("qk_cp")
    part_a = sem("part_a")
    part_p = sem("part_p")
    stack_in = [[sem(f"stack_in{v}{h}") for h in range(2)] for v in range(2)]
    parts_out = [[sem(f"parts_out{v}{h}") for h in range(2)] for v in range(2)]
    tok_ps = sem("tok_ps")
    tok_ev = sem("tok_ev")
    shift_in = [sem(f"shift_in{v}") for v in range(2)]
    vaug_done = sem("vaug_done")
    prod_done = sem("prod_done")
    sn_done = sem("sn_done")
    max_ps = sem("max_ps")
    max_rd = sem("max_rd")
    mrow = sem("mrow")
    diff_done = sem("diff_done")
    mT_ps = sem("mT_ps")
    mT_cp = sem("mT_cp")
    mrow_in = [sem(f"mrow_in{h}") for h in range(2)]
    p_done = sem("p_done")
    pvn_done = sem("pvn_done")
    nn_done = sem("nn_done")
    exp_ps = sem("exp_ps")
    exp_done = sem("exp_done")
    ctx_ps = sem("ctx_ps")
    ctx_cp = sem("ctx_cp")
    cx_ps = sem("cx_ps")
    nd = sem("nd")
    fin = sem("fin")
    oT_ps = sem("oT_ps")
    oT_cp = sem("oT_cp")
    o_ps = sem("o_ps")
    o_done = sem("o_done")

    MAX_STEPS = [(1, 0), (1, 1), (0, 0), (1, 2), (1, 3), (0, 1)]
    EXP_STEPS = [(0, 0), (0, 1), (1, 0), (0, 2), (0, 3), (1, 1)]
    NS = len(MAX_STEPS)
    NCST = 6 + 1 + 6 + 5
    hd = "p (h d) -> p h d"

    def pipeline(eng, body):
        def one(b, hb, u, known):
            body(lambda k: (b + k, (u + k) % 2, hb + (u + k) // 2),
                 {k: known is None or 0 <= known + k < NB for k in range(-3, 4)})

        for b in range(-2, 4):
            one(b, b // 2, b % 2, b)
        with eng.Fori(1, NB // 4 - 1) as j:
            for u in range(4):
                one(j * 4 + u, j * 2 + u // 2, u % 2, None)
        for b in range(NB - 4, NB + 2):
            one(b, b // 2, b % 2, b)

    with nc.Block() as block:
        @block.sync
        def _(sp):
            def cst(dst, src):
                sp.dma_start(dst, src, allow_slow_non_contiguous=True).then_inc(cst_in, 16)

            for i in range(2):
                cst(q_st[i][0:PROD, :, :], c["c_stair_q"][:, None, :].to_broadcast([PROD, H, S]))
                cst(k_st[i][0:PROD, :, :], c["c_stair_k"][:, None, :].to_broadcast([PROD, H, S]))
                cst(k_st[i][MAXROW:ROWS, :, :], c["c_ones"][:, None, :].to_broadcast([3, H, S]))
            cst(near_mask[:], c["c_near"])
            for a in range(2):
                rows, cols = slice(a * P // 2, (a + 1) * P // 2), slice(a * E // 2, (a + 1) * E // 2)
                cst(bias_col[rows, 0:1], b_q[cols].rearrange("(h d o) -> d h o", d=D, o=1))
                cst(bias_col[rows, 1:2], b_k[cols].rearrange("(h d o) -> d h o", d=D, o=1))
                cst(bias_col[rows, 2:3], rel_k[0, :].rearrange("(d h o) -> d h o", h=1, o=1).to_broadcast([D, HH, 1]))
            cst(b_rows[:, 0:E], b_q[None, :].to_broadcast([P, E]))
            cst(b_rows[:, E:2 * E], b_k[None, :].to_broadcast([P, E]))
            cst(b_rows[:, 2 * E:], b_v[None, :].to_broadcast([P, E]))
            cst(rk_all[:], rel_k[None, 0:NEAR, :].to_broadcast([P, NEAR, D]))
            cst(rv_all[:], rel_v[None, 0:NEAR, :].to_broadcast([P, NEAR, D]))

            def stack(half, v):
                hs = slice(half * HH, (half + 1) * HH)
                rows = slice(half * P // 2, (half + 1) * P // 2)
                for w, st in enumerate((q_st[v], k_st[v])):
                    src = parts_dram[v][w, :, rows, :].rearrange("c (d h) q -> c d (h q)", d=D)
                    sp.dma_start(st[PROD:MAXROW, hs, :].rearrange("r h q -> r (h q)"), src).then_inc(stack_in[v][half], 16)

            def load_stage(n):
                for s in range(TOPK):
                    sp.dma_start(stage[:, s, :, 0:E], xn_dram[:, bass.ds(n * TT, TT), :]).then_inc(staged, 16)

            def body(at, on):
                b, u, hb = at(0)

                def rows_of_max(k, half):
                    n, v, hn = at(k)
                    sp.wait_ge(mT_cp, n * 2 + half + 1)
                    sp.dma_start(q_st[v][MAXROW:ROWS, half * HH:(half + 1) * HH, :], max_T[half][:]).then_inc(mrow_in[half], 16)

                if on[0]:
                    rows_of_max(0, 1)
                    if on[-1]:
                        sp.wait_ge(scattered, b * 64)
                    load_stage(b)
                if on[2]:
                    n, v, hn = at(2)
                    sp.wait_ge(part_p, n * 3 + 3)
                    if on[0]:
                        for half in range(2):
                            sp.wait_ge(stack_in[v][half], hn * 2 * 16)
                    for half in range(2):
                        rows = slice(half * P // 2, (half + 1) * P // 2)
                        sp.dma_start(parts_dram[v].rearrange("w c p q -> p (w c) q")[rows],
                                     parts[v][rows].rearrange("p w c q -> p (w c) q")).then_inc(parts_out[v][half], 16)
                    if on[0]:
                        sp.wait_ge(exp_ps, b * NS + 3)
                    sp.wait_ge(parts_out[v][0], hn * 16 + 16)
                    stack(0, v)
                if on[1]:
                    rows_of_max(1, 0)
                if on[2]:
                    n, v, hn = at(2)
                    sp.wait_ge(tok_ev, n * 6 + 6)
                    a, kb, nr = tok_a[v], tok_b[v], near_kv[v]
                    for dst, src in ((nr[2:P, :, 2, :], a[0:P - 2, :, E:]), (nr[0:2, 1, 2, :], a[P - 2:P, 0, E:]),
                                     (nr[1:P, :, 1, :], kb[0:P - 1, :, :]), (nr[0:1, 1, 1, :], kb[P - 1:P, 0, :])):
                        sp.dma_start(dst, src).then_inc(shift_in[v], 16)
                    if on[0]:
                        sp.wait_ge(exp_ps, b * NS + 6)
                    sp.wait_ge(parts_out[v][1], hn * 16 + 16)
                    stack(1, v)

            pipeline(sp, body)

        NSTK = 2 * 16

        @block.gpsimd
        def _(pool):
            for i in range(2):
                nc.gpsimd.memset(near_kv[i][:], 0.0).then_inc(zeroed, 1)
                nc.gpsimd.memset(v_aug[i][:], 0.0).then_inc(zeroed, 1)
            pool.wait_ge(zeroed, 4)
            for i in range(2):
                nc.gpsimd.memset(v_aug[i][:, :, :, D:D + 1], 1.0).then_inc(zeroed, 1)

            pool.wait_ge(pad_out, PADS * 16)

            def body(at, on):
                b, u, hb = at(0)
                if on[1]:
                    n, v, hn = at(1)
                    pool.wait_ge(shift_in[v], hn * 64 + 64)
                    if on[0]:
                        pool.wait_ge(sn_done, b * 3 + 1)
                    for t in range(TT):
                        last = nc.gpsimd.tensor_tensor(prod[:, t, :, :], near_kv[v][:, t, :, 0:E],
                                                       tok_a[v][:, t, None, 0:E].to_broadcast([P, NEAR, E]), ALU.mult)
                    last.then_inc(prod_done, 1)
                if on[2]:
                    n, v, hn = at(2)
                    pool.wait_ge(part_a, n * 4 + 2)
                    nc.gpsimd.tensor_tensor(rem[:], qk32[:], parts[v][:, :, 1, :], ALU.subtract).then_inc(part_p, 1)
                if on[0]:
                    pool.wait_ge(p_done, b + 1)
                    if on[-1]:
                        pool.wait_ge(nn_done, b * 2)
                    for t in range(TT):
                        for n in range(NEAR):
                            last = nc.gpsimd.tensor_tensor(pv_near[:, t, n, :].rearrange(hd, d=D),
                                                           near_kv[u][:, t, n, E:].rearrange(hd, d=D),
                                                           p_near[u][:, t, n, :, None].to_broadcast([P, H, D]), ALU.mult)
                    last.then_inc(pvn_done, 1)
                if on[2]:
                    n, v, hn = at(2)
                    q, k = parts[v][:, 0, :, :], parts[v][:, 1, :, :]
                    pool.wait_ge(part_a, n * 4 + 4)
                    nc.gpsimd.tensor_tensor(q[:, 5, :], rem[:, 0, :], q[:, 4, :], ALU.subtract).then_inc(part_p, 1)
                    nc.gpsimd.tensor_tensor(k[:, 0, :], rem[:, 1, :], k[:, 4, :], ALU.subtract).then_inc(part_p, 1)
                if on[0]:
                    if on[-1]:
                        pool.wait_ge(scattered, b * 64)
                    for s in range(TOPK):
                        nc.gpsimd.tensor_copy(stage[:, s, :, E].bitcast(U32), dest_all[:, s, bass.ds(b * TT, TT)]).then_inc(tagged, 1)
                    nc.gpsimd.tensor_copy(stage_pos[:], pos_all[:, bass.ds(b * TT, TT), :]).then_inc(tagged, 1)
                    pool.wait_ge(staged, b * 32 + 32)
                    pool.wait_ge(tagged, b * 3 + 3)
                    pool.sem_inc(stage_ready, 1)
                    for s in range(TOPK):
                        for t in range(TT):
                            nc.gpsimd.indirect_dma_start(xd, bass.IndirectOffsetOnAxis(ap=stage_pos[:, t, s:s + 1], axis=0),
                                                         stage[:, s, t, :], None).then_inc(scattered, 16)
            pipeline(pool, body)
            pool.wait_ge(scattered, NB * 64)

        @block.scalar
        def _(act):
            act.wait_ge(bias_done, 12)
            act.wait_ge(zeroed, 6)
            nc.scalar.activation(xb[0][:], xnT[:, 0:S], ACT.Copy).then_inc(xb_done, 1)

            def body(at, on):
                b, u, hb = at(0)

                def step(s):
                    act.wait_ge(exp_ps, b * NS + s + 1)
                    if on[-1]:
                        act.wait_ge(ctx_ps, b * 2 - (1 if s < 3 else 0))
                    nc.scalar.activation(probs[s][:], ps_exp[:], ACT.Exp, scale=RS).then_inc(exp_done, 1)

                def qk():
                    n, v, hn = at(2)
                    act.wait_ge(qk_ps, n + 1)
                    if on[1]:
                        act.wait_ge(part_p, n * 3)
                    nc.scalar.activation(qk32[:, 0, :], X0[:, 0:S], ACT.Identity, bias=bias_col[:, 0:1]).then_inc(qk_cp, 1)
                    nc.scalar.activation(qk32[:, 1, :], X0[:, S:2 * S], ACT.Identity, bias=bias_col[:, 3:4]).then_inc(qk_cp, 1)
                    act.wait_ge(qk_cp, n * 2 + 2)
                    if on[0]:
                        for half in range(2):
                            act.wait_ge(parts_out[v][half], hn * 16)
                    for w, slots in ((0, slice(0, 3)), (1, slice(1, 6, 2))):
                        nc.scalar.activation(parts[v][:, w, slots, :], qk32[:, w, None, :].to_broadcast([P, 3, S]),
                                             ACT.Copy).then_inc(part_a, 1)

                def qk2():
                    n, v, hn = at(2)
                    act.wait_ge(part_p, n * 3 + 1)
                    for w, slots in ((0, slice(3, 5)), (1, slice(2, 5, 2))):
                        nc.scalar.activation(parts[v][:, w, slots, :], rem[:, w, None, :].to_broadcast([P, 2, S]),
                                             ACT.Copy).then_inc(part_a, 1)

                def vaug():
                    n, v, hn = at(1)
                    act.wait_ge(tok_ev, n * 6 + 6)
                    if on[-1]:
                        act.wait_ge(ctx_ps, b * 2)
                    nc.scalar.activation(v_aug[v][:, :, :, 0:D], tok_a[v][:, :, 2 * E:].rearrange("p t (h d) -> p t h d", d=D),
                                         ACT.Copy).then_inc(vaug_done, 1)

                def ctx_copy(k, half):
                    n, v, hn = at(k)
                    act.wait_ge(ctx_ps, n * 2 + half + 1)
                    if half == 0 and on[-1]:
                        act.wait_ge(cx_ps, b * 2)
                    nc.scalar.activation(ctx_T[:, 2 * half:2 * half + 2, :], ps_ctx[:, half * 512:(half + 1) * 512],
                                         ACT.Copy).then_inc(ctx_cp, 1)

                def max_copy(k, half):
                    n, v, hn = at(k)
                    act.wait_ge(mT_ps, n * 2 + half + 1)
                    if on[k - 1]:
                        act.wait_ge(mrow_in[half], n * 16)
                    nc.scalar.activation(max_T[half][:], X1[0:3 * HH, 3 * E:].bitcast(BF16), ACT.Copy).then_inc(mT_cp, 1)

                for s in range(NS):
                    if on[0]:
                        step(s)
                    if s == 0:
                        if on[0]:
                            act.wait_ge(diff_done, b + 1)
                            nc.scalar.activation(p_near[u][:], near_diff[:], ACT.Exp, scale=RS).then_inc(p_done, 1)
                        if on[0]:
                            max_copy(0, 1)
                        if on[-1]:
                            ctx_copy(-1, 1)
                        if on[2]:
                            qk()
                    if s == 1 and on[1]:
                        vaug()
                    if s == 2 and on[2]:
                        qk2()
                    if s == 3 and on[-2]:
                        n, v, hn = at(-2)
                        act.wait_ge(oT_ps, n + 1)
                        nc.scalar.activation(o_T[:], X0[:, 0:S], ACT.Copy).then_inc(oT_cp, 1)
                    if s == 4 and on[1]:
                        max_copy(1, 0)
                    if s == 4 and on[3]:
                        n, v, hn = at(3)
                        if on[1]:
                            act.wait_ge(tok_ps, (n - 1) * 2)
                        nc.scalar.activation(xb[v][:], xnT[:, bass.ds(n * S, S)], ACT.Copy).then_inc(xb_done, 1)
                    if s == 5 and on[0]:
                        ctx_copy(0, 0)

            pipeline(act, body)

        @block.vector
        def _(dve):
            dve.wait_ge(cst_in, 16 * NCST)
            nc.vector.tensor_tensor(bias_col[:, 3:4], bias_col[:, 1:2], bias_col[:, 2:3], ALU.add).then_inc(bias_done, 1)
            nc.vector.tensor_copy(bias_a[:, 0:E], b_rows[:, 0:E]).then_inc(bias_done, 1)
            for dst, first, entry in ((bias_a, E, 0), (bias_b, 0, 1), (bias_c, 0, 2)):
                for w, tab in ((0, rk_all), (1, rv_all)):
                    nc.vector.tensor_tensor(dst[:, first + w * E:first + (w + 1) * E].rearrange(hd, d=D),
                                            b_rows[:, (1 + w) * E:(2 + w) * E].rearrange(hd, d=D),
                                            tab[:, entry, None, :].to_broadcast([P, H, D]), ALU.add).then_inc(bias_done, 1)
            for w in range(2):
                for a in range(2):
                    cols = slice(a * E // 2, (a + 1) * E // 2)
                    nc.vector.tensor_copy(w_turn[:, w, cols].rearrange("p (d h) -> p d h", d=D),
                                          wqkv[:, w * E + a * E // 2:w * E + (a + 1) * E // 2]
                                          .rearrange("p (h d) -> p d h", d=D)).then_inc(bias_done, 1)
            dve.wait_ge(bias_done, 12)
            dve.wait_ge(zeroed, 6)

            def body(at, on):
                b, u, hb = at(0)

                def tok(t):
                    n, v, hn = at(2)
                    dve.wait_ge(tok_ps, n * 2 + t + 1)
                    if t == 0 and on[0]:
                        dve.wait_ge(shift_in[v], hn * 64)
                        dve.wait_ge(pvn_done, b + 1)
                        dve.wait_ge(vaug_done, b + 1)
                    nc.vector.tensor_tensor(tok_a[v][:, t, :], X1[:, 0:3 * E], bias_a[:], ALU.add).then_inc(tok_ev, 1)
                    nc.vector.tensor_tensor(tok_b[v][:, t, :], X1[:, E:3 * E], bias_b[:], ALU.add).then_inc(tok_ev, 1)
                    nc.vector.tensor_tensor(near_kv[v][:, t, 0, :], X1[:, E:3 * E], bias_c[:], ALU.add).then_inc(tok_ev, 1)

                def max_step(s):
                    n, v, hn = at(1)
                    t, g = MAX_STEPS[s]
                    dve.wait_ge(max_ps, n * NS + s + 1)
                    w = 4 if t == 1 else 8
                    nc.vector.tensor_reduce(far_top[:, t, w * g:w * g + w], ps_max[:].rearrange("p (h k) -> p h k", h=w),
                                            AX.X, ALU.max).then_inc(max_rd, 1)

                def near_scores():
                    n, v, hn = at(1)
                    dve.wait_ge(prod_done, n + 1)
                    nc.vector.tensor_reduce(s_near[:], prod[:].rearrange("p t n (h d) -> p (t n) h d", d=D),
                                            AX.X, ALU.add).then_inc(sn_done, 1)
                    dve.wait_ge(sn_done, n * 3 + 1)
                    flat = s_near[:].rearrange("p t n h -> p (t n h)")
                    nc.vector.tensor_tensor(flat, flat, near_mask[:], ALU.add).then_inc(sn_done, 1)
                    dve.wait_ge(sn_done, n * 3 + 2)
                    nc.vector.tensor_reduce(near_top[:], s_near[:].rearrange("p t n h -> p t h n"),
                                            AX.X, ALU.max).then_inc(sn_done, 1)

                def row_max_step(half, step):
                    n, v, hn = at(1)
                    first = n * 12 + half * 6
                    hs = slice(half * HH, (half + 1) * HH)
                    m = row_max[:, :, hs]
                    mp = [max_parts[:, half, :, i, :] for i in range(3)]
                    if step == 0:
                        dve.wait_ge(max_rd, n * NS + 3 * half + 3)
                        dve.wait_ge(sn_done, n * 3 + 3)
                        nc.vector.tensor_tensor(m, far_top[:, :, hs], near_top[:, :, hs], ALU.max).then_inc(mrow, 1)
                        return
                    dve.wait_ge(mrow, first + step)
                    if step == 1:
                        if on[0]:
                            dve.wait_ge(mT_ps, n * 2 - 1 + half)
                        nc.vector.tensor_scalar(mp[0], m, -1.0, None, ALU.mult).then_inc(mrow, 1)
                    elif step == 2:
                        nc.vector.scalar_tensor_tensor(neg_res[0][:], m, -1.0, mp[0], ALU.mult, ALU.subtract).then_inc(mrow, 1)
                    elif step == 3:
                        nc.vector.tensor_copy(mp[1], neg_res[0][:]).then_inc(mrow, 1)
                    elif step == 4:
                        nc.vector.tensor_tensor(neg_res[1][:], neg_res[0][:], mp[1], ALU.subtract).then_inc(mrow, 1)
                    else:
                        nc.vector.tensor_copy(mp[2], neg_res[1][:]).then_inc(mrow, 1)

                def near_sum(w, k):
                    n, v, hn = at(k)
                    if w == 0:
                        dve.wait_ge(p_done, n + 1)
                        nc.vector.tensor_reduce(den_near[v][:], p_near[v][:].rearrange("p t n h -> p t h n"),
                                                AX.X, ALU.add).then_inc(nn_done, 1)
                    else:
                        dve.wait_ge(pvn_done, n + 1)
                        nc.vector.tensor_reduce(num_near[v][:], pv_near[:].rearrange("p t n e -> p t e n"),
                                                AX.X, ALU.add).then_inc(nn_done, 1)

                def out_step(t, step):
                    n, v, hn = at(-1)
                    acc = X0[:].rearrange("p (h r) -> p h r", r=32)
                    if step == 0:
                        dve.wait_ge(cx_ps, n * 2 + t + 1)
                        if t == 0:
                            dve.wait_ge(nn_done, n * 2 + 2)
                        nc.vector.tensor_tensor(den[:, t, :], acc[:, :, D], den_near[v][:, t, :], ALU.add).then_inc(nd, 1)
                    elif step == 1:
                        nc.vector.tensor_tensor(num[:, t, :].rearrange(hd, d=D), acc[:, :, 0:D],
                                                num_near[v][:, t, :].rearrange(hd, d=D), ALU.add).then_inc(nd, 1)
                    elif step == 2:
                        dve.wait_ge(nd, n * 4 + 2 * t + 1)
                        nc.vector.reciprocal(rden[:, t, :], den[:, t, :]).then_inc(fin, 1)
                    else:
                        dve.wait_ge(fin, n * 4 + 2 * t + 1)
                        dve.wait_ge(nd, n * 4 + 2 * t + 2)
                        if t == 0 and on[-3]:
                            dve.wait_ge(oT_ps, n - 1)
                        nc.vector.tensor_tensor(o_tok[v][:, t, :].rearrange(hd, d=D), num[:, t, :].rearrange(hd, d=D),
                                                rden[:, t, :, None].to_broadcast([P, H, D]), ALU.mult).then_inc(fin, 1)

                def store_out():
                    n, v, hn = at(-2)
                    dve.wait_ge(o_ps, n + 1)
                    nc.vector.tensor_tensor(attn_all[:, bass.ds(n * 2, 2), :],
                                            X0[:, 256:512].rearrange("p (t e) -> p t e", t=TT),
                                            bo_row[:, None, :].to_broadcast([P, TT, E]), ALU.add).then_inc(o_done, 1)

                def near_differences():
                    n, v, hn = at(1)
                    if on[0]:
                        dve.wait_ge(p_done, n)
                    dve.wait_ge(mrow, n * 12 + 7)
                    nc.vector.tensor_tensor(near_diff[:], s_near[:], row_max[:, :, None, :].to_broadcast([P, TT, NEAR, H]),
                                            ALU.subtract).then_inc(diff_done, 1)

                for s in range(NS):
                    if on[1]:
                        max_step(s)
                    if s == 0 and on[-1]:
                        near_sum(1, -1)
                    if s == 1:
                        if on[1]:
                            near_scores()
                    if s == 2:
                        for i in range(6):
                            if on[1]:
                                row_max_step(0, i)
                            if on[-1] and i < 4:
                                out_step(0, i)
                        if on[2]:
                            tok(0)
                    if s == 3 and on[2]:
                        tok(1)
                    if s == 4 and on[-2]:
                        store_out()
                if on[1]:
                    row_max_step(1, 0)
                    row_max_step(1, 1)
                    near_differences()
                    row_max_step(1, 2)
                if on[-1]:
                    out_step(1, 0)
                if on[1]:
                    row_max_step(1, 3)
                if on[-1]:
                    out_step(1, 1)
                if on[1]:
                    row_max_step(1, 4)
                if on[-1]:
                    out_step(1, 2)
                if on[1]:
                    row_max_step(1, 5)
                if on[0]:
                    near_sum(0, 0)
                if on[-1]:
                    out_step(1, 3)

            pipeline(dve, body)

        @block.tensor
        def _(pe):
            pe.wait_ge(bias_done, 12)
            pe.wait_ge(zeroed, 6)

            def body(at, on):
                b, u, hb = at(0)

                def qk_proj():
                    n, v, hn = at(2)
                    pe.wait_ge(xb_done, n + 1)
                    if on[-2]:
                        pe.wait_ge(nd, b * 4 - 4)
                    elif on[1]:
                        pe.wait_ge(qk_cp, n * 2)
                    nc.tensor.matmul(X0[:, 0:S], w_turn[:, 0, :], xb[v][:], start=True, stop=True, skip_group_check=True)
                    nc.tensor.matmul(X0[:, S:], w_turn[:, 1, :], xb[v][:], start=True, stop=True,
                                     skip_group_check=True).then_inc(qk_ps, 1)

                def tok_proj(t):
                    n, v, hn = at(2)
                    if t == 1 or on[1]:
                        pe.wait_ge(tok_ev, n * 6 + 3 * t)
                    if t == 0 and on[0]:
                        pe.wait_ge(mT_cp, b * 2 + 2)
                    nc.tensor.matmul(X1[:, 0:3 * E], xb[v][:, t * P:(t + 1) * P], wqkv[:], start=True, stop=True,
                                     skip_group_check=True).then_inc(tok_ps, 1)

                def max_step(s):
                    n, v, hn = at(1)
                    t, g = MAX_STEPS[s]
                    if s % 3 == 0:
                        pe.wait_ge(stack_in[v][s // 3], hn * NSTK + NSTK)
                    if s > 0 or on[0]:
                        pe.wait_ge(max_rd, n * NS + s)
                    q, k = q_st[v], k_st[v]
                    if t == 1:
                        for i in range(4):
                            nc.tensor.matmul(ps_max[:, i * S + P:(i + 1) * S], q[0:MAXROW, 4 * g + i, P:],
                                             k[0:MAXROW, 4 * g + i, P:], start=True, stop=True, skip_group_check=True)
                        for i in range(4):
                            last = nc.tensor.matmul(ps_max[:, i * S:i * S + P], q[EDGE:MAXROW, 4 * g + i, P:],
                                                    k[EDGE:MAXROW, 4 * g + i, 0:P], start=True, stop=True, skip_group_check=True)
                    else:
                        for i in range(8):
                            last = nc.tensor.matmul(ps_max[:, i * P:(i + 1) * P], q[0:MAXROW, 8 * g + i, 0:P],
                                                    k[0:MAXROW, 8 * g + i, 0:P], start=True, stop=True, skip_group_check=True)
                    last.then_inc(max_ps, 1)

                def exp_step(s):
                    t, g = EXP_STEPS[s]
                    if s % 3 == 0:
                        pe.wait_ge(mrow_in[s // 3], b * 16 + 16)
                    if s > 0 or on[-1]:
                        pe.wait_ge(exp_done, b * NS + s)
                    q, k = q_st[u], k_st[u]
                    if t == 0:
                        for i in range(4):
                            nc.tensor.matmul(ps_exp[:, i * S:i * S + P], k[0:ROWS, 4 * g + i, 0:P],
                                             q[0:ROWS, 4 * g + i, 0:P], start=True, stop=True, skip_group_check=True)
                        for i in range(4):
                            last = nc.tensor.matmul(ps_exp[:, i * S + P:(i + 1) * S], k[EDGE:ROWS, 4 * g + i, 0:P],
                                                    q[EDGE:ROWS, 4 * g + i, P:], start=True, stop=True, skip_group_check=True)
                    else:
                        for i in range(8):
                            last = nc.tensor.matmul(ps_exp[:, i * P:(i + 1) * P], k[0:ROWS, 8 * g + i, P:],
                                                    q[0:ROWS, 8 * g + i, P:], start=True, stop=True, skip_group_check=True)
                    last.then_inc(exp_ps, 1)

                def pv(k, s):
                    n, v, hn = at(k)
                    t, g = EXP_STEPS[s]
                    if s == 0:
                        pe.wait_ge(vaug_done, n + 1)
                    if s % 3 == 0 and on[-1]:
                        pe.wait_ge(ctx_cp, n * 2 - 1 + s // 3)
                    pe.wait_ge(exp_done, n * NS + s + 1)
                    for i in range(4 if t == 0 else 8):
                        h = 4 * g + i if t == 0 else 8 * g + i
                        gg, row = h // 4, 32 * (h % 4)
                        if t == 0:
                            last = nc.tensor.matmul(ps_ctx[row:row + 32, gg * S:(gg + 1) * S], v_aug[v][:, 0, h, :],
                                                    probs[s][:, i * S:(i + 1) * S], start=(gg % 2 == 0), stop=False,
                                                    skip_group_check=True)
                        else:
                            last = nc.tensor.matmul(ps_ctx[row:row + 32, gg * S + P:(gg + 1) * S], v_aug[v][:, 1, h, :],
                                                    probs[s][:, i * P:(i + 1) * P], start=False, stop=True,
                                                    skip_group_check=True)
                    if s % 3 == 2:
                        last.then_inc(ctx_ps, 1)

                def ctx_turn(t):
                    n, v, hn = at(-1)
                    if t == 0:
                        pe.wait_ge(ctx_cp, n * 2 + 2)
                        if on[2]:
                            pe.wait_ge(qk_cp, b * 2 + 6)
                        elif on[-2]:
                            pe.wait_ge(nd, b * 4 - 4)
                    else:
                        pe.wait_ge(nd, n * 4 + 2)
                        if on[-2]:
                            pe.wait_ge(o_done, n)
                    for g in range(4):
                        last = nc.tensor.transpose(X0[:, g * P:(g + 1) * P], ctx_T[:, g, t * P:(t + 1) * P], ident[:])
                    last.then_inc(cx_ps, 1)

                def max_turn(k, half):
                    n, v, hn = at(k)
                    pe.wait_ge(mrow, n * 12 + 6 * half + 6)
                    if half == 1 or on[k - 1]:
                        pe.wait_ge(mT_cp, n * 2 + half)
                    if half == 0 and on[2]:
                        pe.wait_ge(tok_ev, (b + 2) * 6 + 6)
                    for t in range(TT):
                        last = nc.tensor.transpose(X1[0:3 * HH, 3 * E + t * P // 2:3 * E + (t + 1) * P // 2].bitcast(BF16),
                                                   max_parts[:, half, t, :, :].rearrange("p n h -> p (n h)"), ident_bf[:])
                    last.then_inc(mT_ps, 1)

                def out_turn():
                    n, v, hn = at(-2)
                    pe.wait_ge(fin, n * 4 + 4)
                    if on[-1]:
                        pe.wait_ge(nd, n * 4 + 6)
                    for t in range(TT):
                        last = nc.tensor.transpose(X0[:, t * P:(t + 1) * P], o_tok[v][:, t, :], ident[:])
                    last.then_inc(oT_ps, 1)

                def out_proj():
                    n, v, hn = at(-2)
                    pe.wait_ge(oT_cp, n + 1)
                    for t in range(TT):
                        last = nc.tensor.matmul(X0[:, 256 + t * P:256 + (t + 1) * P], o_T[:, t * P:(t + 1) * P], wo[:],
                                                start=True, stop=True, skip_group_check=True)
                    last.then_inc(o_ps, 1)

                for s in range(NS):
                    if on[1]:
                        max_step(s)
                    if on[0]:
                        exp_step(s)
                    if s == 0:
                        if on[-1]:
                            pv(-1, NS - 1)
                        if on[0]:
                            max_turn(0, 1)
                        if on[2]:
                            qk_proj()
                    if s == 1 and on[2]:
                        tok_proj(0)
                    if s == 2 and on[-1]:
                        ctx_turn(0)
                    if s == 3 and on[-2]:
                        out_turn()
                    if s == 3 and on[2]:
                        tok_proj(1)
                    if s == 4 and on[1]:
                        max_turn(1, 0)
                    if s == 4 and on[-2]:
                        out_proj()
                    if s == 5 and on[-1]:
                        ctx_turn(1)
                    if s > 0 and on[0]:
                        pv(0, s - 1)

            pipeline(pe, body)


def experts(nc, ctx, NT, x_t, attn_all, tile_expert, ident, b1_sb, w1, w2, b2, xd, out_t):
    def sb(name, shape, dt=F32):
        return ctx.enter_context(nc.sbuf_tensor(name, shape, dt))

    def sem(name):
        return ctx.enter_context(nc.semaphore(name))

    def bank(name):
        return ctx.enter_context(nc.psum_tensor(name, [P, 512], F32))

    N = NT * P
    NTILE = tile_expert.shape[1]
    TS = SLOT_T // P
    OUT_G = min(8, NT)
    GT = NT // OUT_G
    HELD = OUT_G // 2
    W2, B1, B2 = FFN, FFN + FC * E, FFN + FC * E + FC
    WIDTH = B2 + E
    w_all = sb("w_all", [P, NEXP, WIDTH])
    w_cur = [sb(f"w_cur{i}", [P, WIDTH]) for i in range(4)]
    slots = [sb(f"slots{i}", [P, TS, E + 1]) for i in range(RING)]
    y_sb = [sb(f"y_sb{i}", [P, TS, E]) for i in range(RING)]
    xT = [sb(f"xT{i}", [P, SLOT_T]) for i in range(2)]
    hT = [sb(f"hT{i}", [P, FC, SLOT_T]) for i in range(2)]
    x_all = sb("x_again", [P, NT, E])
    y_first = sb("y_first", [P, NT, E])
    y_second = sb("y_second", [P, HELD * GT, E])
    yd = nc.dram_tensor("outputs_dram", [TOPK * N + PADS * P, E], F32, kind="Internal").ap()
    ps_x = [bank(f"ps_turn{i}") for i in range(2)]
    ps_h = [[bank(f"ps_h{i}{j}") for j in range(2)] for i in range(2)]
    ps_y = [bank(f"ps_y{i}") for i in range(2)]

    w_in = sem("w_in")
    b1_cp = sem("b1_cp")
    x_in = sem("x_again_in")
    slots_in = [sem(f"slots_in{i}") for i in range(RING)]
    w_cp = sem("w_cp")
    x_ps = sem("x_ps")
    x_cp = sem("x_cp")
    h_ps = sem("h_ps")
    h_act = sem("h_act")
    h_dve = sem("h_dve")
    y_ps = sem("y_ps")
    y_cp = sem("y_cp")
    y_taken = sem("y_taken")
    y_out = [sem(f"y_out{i}") for i in range(RING)]
    y_in = [sem(f"y_in{g}") for g in range(OUT_G)]
    summed = sem("summed")
    gated = sem("gated")
    scaled = sem("scaled")
    fin = sem("fin_out")
    out_done = sem("out_done")

    def pipeline(eng, body):
        def one(i, q, u, known):
            body(lambda k: (i + k, (u + k) % RING, q + (u + k) // RING), lambda k: known is None or 0 <= known + k < NTILE)

        first = RING - 2
        for i in range(-2, first):
            one(i, i // RING, i % RING, i)
        with eng.Fori(0, NTILE // RING - 1) as j:
            for u in range(first, first + RING):
                one(j * RING + u, j + u // RING, u % RING, None)
        for i in range(NTILE - 2, NTILE):
            one(i, i // RING, i % RING, i)

    with nc.Block() as block:
        @block.sync
        def _(sp):
            sp.dma_start(w_all[:, :, 0:W2], w1.rearrange("e p f -> p e f")).then_inc(w_in, 16)
            for e in range(NEXP):
                sp.dma_start(w_all[:, e, W2:B1].rearrange("p (c n) -> p c n", n=E),
                             w2[e].rearrange("(c p) n -> p c n", p=P)).then_inc(w_in, 16)
            sp.dma_start(w_all[:, :, B2:], b2[None, :, :].to_broadcast([P, NEXP, E])).then_inc(w_in, 16)

            def body(at, on):
                if on(2):
                    n, u, q = at(2)
                    if on(2 - RING):
                        sp.wait_ge(y_out[u], q * 32)
                    sp.dma_start(slots[u][:], xd.rearrange("(n p) e -> p n e", p=P)[:, bass.ds(n * TS, TS), :]).then_inc(slots_in[u], 16)

            pipeline(sp, body)
            sp.dma_start(x_all[:], x_t).then_inc(x_in, 16)
            for i in range(RING):
                sp.wait_ge(y_out[i], NTILE // RING * 32)
            for g in range(OUT_G):
                ts = slice(g * GT, (g + 1) * GT)
                if g >= HELD:
                    sp.wait_ge(summed, g - HELD + 1)
                for s, dst in enumerate((y_first[:, ts, :], y_second[:, g % HELD * GT:(g % HELD + 1) * GT, :])):
                    sp.dma_start(dst, yd[s * N:(s + 1) * N, :].rearrange("(t p) e -> p t e", p=P)[:, ts, :]
                                 ).then_inc(y_in[g], 16)
            for g in range(OUT_G):
                ts = slice(g * GT, (g + 1) * GT)
                sp.wait_ge(fin, g + 1)
                sp.dma_start(out_t[:, ts, :], x_all[:, ts, :]).then_inc(out_done, 16)
            sp.wait_ge(out_done, 16 * OUT_G)

        @block.gpsimd
        def _(pool):
            def body(at, on):
                if on(0):
                    n, u, q = at(0)
                    pool.wait_ge(y_cp, n + 1)
                    pool.sem_inc(y_taken, 1)
                    for t in range(TS):
                        nc.gpsimd.indirect_dma_start(yd, bass.IndirectOffsetOnAxis(ap=slots[u][:, t, E:].bitcast(U32), axis=0),
                                                     y_sb[u][:, t, :], None).then_inc(y_out[u], 16)

            pipeline(pool, body)

        @block.tensor
        def _(pe):
            def body(at, on):
                if on(2):
                    n, u, q = at(2)
                    pe.wait_ge(slots_in[u], q * 16 + 16)
                    if on(0):
                        pe.wait_ge(x_cp, n - 1)
                    for t in range(TS):
                        last = nc.tensor.transpose(ps_x[u % 2][:, t * P:(t + 1) * P], slots[u][:, t, 0:E], ident[:])
                    last.then_inc(x_ps, 1)
                if on(1):
                    n, u, q = at(1)
                    pe.wait_ge(x_cp, n + 1)
                    pe.wait_ge(w_cp, n + 1)
                    if on(-1):
                        pe.wait_ge(h_act, n - 1)
                        pe.wait_ge(h_dve, n - 1)
                    for f in range(FC):
                        last = nc.tensor.matmul(ps_h[u % 2][f // 2][:, f % 2 * SLOT_T:(f % 2 + 1) * SLOT_T],
                                                w_cur[u % 4][:, f * P:(f + 1) * P], xT[u % 2][:], start=True, stop=True,
                                                skip_group_check=True)
                    last.then_inc(h_ps, 1)
                if on(0):
                    n, u, q = at(0)
                    pe.wait_ge(h_act, n + 1)
                    pe.wait_ge(h_dve, n + 1)
                    if on(-2):
                        pe.wait_ge(y_cp, n - 1)
                    for t in range(TS):
                        for f in range(FC):
                            last = nc.tensor.matmul(ps_y[u % 2][:, t * E:(t + 1) * E], hT[u % 2][:, f, t * P:(t + 1) * P],
                                                    w_cur[u % 4][:, W2 + f * E:W2 + (f + 1) * E],
                                                    start=(f == 0), stop=(f == FC - 1), skip_group_check=True)
                    last.then_inc(y_ps, 1)

            pipeline(pe, body)

        @block.scalar
        def _(act):
            def body(at, on):
                if on(2):
                    n, u, q = at(2)
                    act.wait_ge(x_ps, n + 1)
                    if on(0):
                        act.wait_ge(h_ps, n - 1)
                    nc.scalar.activation(xT[u % 2][:], ps_x[u % 2][:, 0:SLOT_T], ACT.Copy).then_inc(x_cp, 1)
                if on(1):
                    n, u, q = at(1)
                    act.wait_ge(h_ps, n + 1)
                    if on(-1):
                        act.wait_ge(y_ps, n - 1)
                    for f in range(2):
                        last = nc.scalar.activation(hT[u % 2][:, f, :], ps_h[u % 2][0][:, f * SLOT_T:(f + 1) * SLOT_T],
                                                    ACT.Relu, bias=w_cur[u % 4][:, B1 + f:B1 + f + 1])
                    last.then_inc(h_act, 1)

            pipeline(act, body)
            for g in range(OUT_G):
                ts = slice(g * GT, (g + 1) * GT)
                act.wait_ge(summed, g + 1)
                nc.scalar.activation(y_first[:, ts, :], y_first[:, ts, :], ACT.Silu).then_inc(gated, 1)

        @block.vector
        def _(dve):
            dve.wait_ge(w_in, 16 * (2 + NEXP))
            nc.vector.tensor_copy(w_all[:, :, B1:B2], b1_sb[:]).then_inc(b1_cp, 1)
            dve.wait_ge(b1_cp, 1)

            def body(at, on):
                if on(2):
                    n, u, q = at(2)
                    if on(-2):
                        dve.wait_ge(y_cp, n - 3)
                    e = dve.value_load(tile_expert[0:1, bass.ds(n, 1)], min_val=0, max_val=NEXP - 1)
                    nc.vector.tensor_copy(w_cur[u % 4][:], w_all[:, bass.ds(e, 1), :].rearrange("p a w -> p (a w)")).then_inc(w_cp, 1)
                if on(1):
                    n, u, q = at(1)
                    dve.wait_ge(h_ps, n + 1)
                    if on(-1):
                        dve.wait_ge(y_ps, n - 1)
                    for f in range(2, 4):
                        last = nc.vector.tensor_scalar(hT[u % 2][:, f, :], ps_h[u % 2][1][:, (f - 2) * SLOT_T:(f - 1) * SLOT_T],
                                                       w_cur[u % 4][:, B1 + f:B1 + f + 1], 0.0, ALU.add, ALU.max)
                    last.then_inc(h_dve, 1)
                if on(0):
                    n, u, q = at(0)
                    dve.wait_ge(y_ps, n + 1)
                    nc.vector.tensor_tensor(y_sb[u][:], ps_y[u % 2][:, 0:TS * E].rearrange("p (t e) -> p t e", e=E),
                                            w_cur[u % 4][:, None, B2:].to_broadcast([P, TS, E]), ALU.add).then_inc(y_cp, 1)

            pipeline(dve, body)
            dve.wait_ge(x_in, 16)

            def add_choices(g):
                ts = slice(g * GT, (g + 1) * GT)
                dve.wait_ge(y_in[g], 32)
                nc.vector.tensor_tensor(y_first[:, ts, :], y_first[:, ts, :], y_second[:, g % HELD * GT:(g % HELD + 1) * GT, :], ALU.add).then_inc(summed, 1)

            add_choices(0)
            for g in range(OUT_G):
                ts = slice(g * GT, (g + 1) * GT)
                if g + 1 < OUT_G:
                    add_choices(g + 1)
                dve.wait_ge(gated, g + 1)
                nc.vector.tensor_tensor(y_first[:, ts, :], y_first[:, ts, :], attn_all[:, ts, :], ALU.mult).then_inc(scaled, 1)
                dve.wait_ge(scaled, g + 1)
                nc.vector.tensor_tensor(x_all[:, ts, :], x_all[:, ts, :], y_first[:, ts, :], ALU.add).then_inc(fin, 1)


NAMES = ["L0_attn_x", "L0_attn_W_q", "L0_attn_b_q", "L0_attn_W_k", "L0_attn_b_k", "L0_attn_W_v", "L0_attn_b_v",
         "L0_attn_W_o", "L0_attn_b_o", "L0_attn_rel_k_table", "L0_attn_rel_v_table", "L0_ffn_gate_w", "L0_ffn_gate_b",
         "L0_ffn_w1", "L0_ffn_b1", "L0_ffn_w2", "L0_ffn_b2"]


def kernel(**inputs):
    import concourse.bacc as bacc
    from concourse.bass_utils import run_bass_kernel_spmd

    nc = bacc.Bacc("TRN2", target_bir_lowering=False, num_devices=1)
    arrays, args = {}, []
    for name in NAMES:
        a = np.ascontiguousarray(inputs[name])
        arrays[f"in_{name}"] = a
        args.append(nc.dram_tensor(f"in_{name}", a.shape, mybir.dt.from_np(a.dtype), kind="ExternalInput").ap())
    shape = arrays["in_L0_attn_x"].shape
    consts = {}
    for name, a in shape_constants(shape[0]).items():
        arrays[name] = a
        consts[name] = nc.dram_tensor(name, a.shape, mybir.dt.from_np(a.dtype), kind="ExternalInput").ap()
    out = nc.dram_tensor("out_0_dram", shape, F32, kind="ExternalOutput").ap()
    program(nc, *args, consts, out)
    r = run_bass_kernel_spmd(nc, [arrays], core_ids=[0])
    return r.results[0]["out_0_dram"]
```

```python
from contextlib import ExitStack

import concourse.bass as bass
import numpy as np
from concourse import mybir

F32 = mybir.dt.float32
U32 = mybir.dt.uint32
BF16 = mybir.dt.bfloat16
ALU = mybir.AluOpType
ACT = mybir.ActivationFunctionType
AX = mybir.AxisListType


P = 128
S = 256
E = 128
H = 16
D = E // H
TT = S // P
NEAR = 3
FFN = 512
NEXP = 8
FC = FFN // P
TOPK = 2
SLOT_T = 256
RING = 8
PADS = RING * SLOT_T // P
EPS = 1e-5
NEG = -1.0e9

PAIRS = P // 2
EDGE = PAIRS
PROD = EDGE + 1
Q_PARTS = [0, 0, 0, 1, 1, 2]
K_PARTS = [2, 0, 1, 0, 1, 0]
MAXROW = PROD + len(Q_PARTS) * D
ROWS = MAXROW + 3


def expert_tiles(nb):
    return -(-(nb * S * TOPK // SLOT_T + NEXP - 1) // RING) * RING


def shape_constants(nb):
    tokens = nb * S
    ntile = expert_tiles(nb)
    ids = (np.arange(TOPK)[:, None] * tokens + np.arange(tokens)).astype(np.uint32)
    pad = np.zeros((P, PADS, E + 1), np.uint32)
    pad[:, :, E] = TOPK * tokens + np.arange(PADS) * P + np.arange(P)[:, None]
    bf = mybir.dt.np(BF16)
    q = np.arange(S)
    stair_q = np.zeros((PROD, S), np.float32)
    stair_q[(q % P) // 2, q] = 1.0
    stair_q[EDGE, P:P + 2] = 1.0
    stair_k = np.zeros((PROD, S), np.float32)
    for j in range(PAIRS):
        stair_k[j, (q % P) > 2 * j - 2] = NEG
    stair_k[EDGE, P - 1] = NEG
    near = np.zeros((P, TT, NEAR, H), np.float32)
    near[0::2, :, 2] = NEG
    near[0, 0, 1] = NEG
    near[0:2, 0, 2] = NEG
    return {
        "c_stair_q": stair_q.astype(bf), "c_stair_k": stair_k.astype(bf),
        "c_ones": np.ones((3, S), bf),
        "c_near": near.reshape(P, TT * NEAR * H),
        "c_dest": np.ascontiguousarray(ids.reshape(TOPK, tokens // P, P).transpose(2, 0, 1)),
        "c_pad": pad.view(np.float32),
        "c_before": np.triu(np.ones((P, P), np.float32), 1), "c_all": np.ones((P, P), np.float32),
        "c_tile": np.broadcast_to(np.arange(ntile, dtype=np.float32), (P, ntile)).copy(),
        "c_tile_start": np.broadcast_to(SLOT_T * np.arange(ntile, dtype=np.float32), (P, ntile)).copy(),
        "c_ident": np.eye(P, dtype=np.float32), "c_ident_bf": np.eye(P).astype(bf),
    }


def program(nc, x, W_q, b_q, W_k, b_k, W_v, b_v, W_o, b_o, rel_k, rel_v, gate_w, gate_b,
            w1, b1, w2, b2, c, out):
    NB = x.shape[0]
    NT = NB * TT
    CH = 4
    NCH = NT // CH
    RS = float(D) ** -0.5

    x_t = x.rearrange("b (t p) e -> p (b t) e", p=P)
    out_t = out.rearrange("b (t p) e -> p (b t) e", p=P)

    with ExitStack() as ctx:
        def sb(name, shape, dt=F32):
            return ctx.enter_context(nc.sbuf_tensor(name, shape, dt))

        def sem(name):
            return ctx.enter_context(nc.semaphore(name))

        N = NB * S
        NTILE = expert_tiles(NB)
        attn_all = sb("attn_all", [P, NT, E])
        ident = sb("ident", [P, P])
        ident_bf = sb("ident_bf", [P, P], BF16)
        wqkv = sb("wqkv", [P, 3 * E])
        wo = sb("wo", [P, E])
        bo_row = sb("bo_row", [P, E])
        b1_sb = sb("b1_sb", [P, NEXP, FC])
        pos_all = sb("pos_all", [P, NT, TOPK], U32)
        dest_all = sb("dest_all", [P, TOPK, NT], U32)
        tile_expert = sb("tile_expert", [P, NTILE], U32)
        turned = ctx.enter_context(ExitStack())
        xnT = turned.enter_context(nc.sbuf_tensor("xnT", [P, NT * P], F32))

        def sb_up_to_1(name, shape, dt=F32):
            return turned.enter_context(nc.sbuf_tensor(name, shape, dt))

        q_st = [sb_up_to_1(f"q_st{i}", [P, H, S], BF16) for i in range(2)]
        k_st = [sb_up_to_1(f"k_st{i}", [P, H, S], BF16) for i in range(2)]
        near_mask = sb_up_to_1("near_mask", [P, TT * NEAR * H])
        bias_col = sb_up_to_1("bias_col", [P, 4])
        rk_all = sb_up_to_1("rk_all", [P, NEAR, D])
        rv_all = sb_up_to_1("rv_all", [P, NEAR, D])
        b_rows = sb_up_to_1("b_rows", [P, 3 * E])
        cst_in = sem("cst_in")
        xn_dram = nc.dram_tensor("xn_dram", [P, NT, E], F32, kind="Internal").ap()
        xd = nc.dram_tensor("slots_dram", [NTILE * SLOT_T, E + 1], F32, kind="Internal").ap()
        pad_out = sem("pad_out")

        with ExitStack() as c0:
            def sb0(name, shape, dt=F32):
                return c0.enter_context(nc.sbuf_tensor(name, shape, dt))

            x_all = sb0("x_all", [P, NT, E])
            pad = sb0("pad", [P, PADS, E + 1])
            stats = sb0("stats", [P, NT, 6])
            mean = sb0("mean", [P, NT])
            diff = sb0("diff", [P, NT])
            var = sb0("var", [P, NT])
            rstd = sb0("rstd", [P, NT])
            eps = sb0("eps", [P, 1])
            gw = sb0("gw", [P, NEXP])
            gb_row = sb0("gb_row", [P, NEXP])
            before = sb0("before", [P, P])
            ones = sb0("ones", [P, P])
            tile_no = sb0("tile_no", [P, NTILE])
            tile_start = sb0("tile_start", [P, NTILE])
            xn_chunk = [sb0(f"xn_chunk{i}", [P, CH, E]) for i in range(4)]
            logits = sb0("logits", [P, NT, NEXP])
            top = sb0("top", [P, NT])
            ex = sb0("ex", [P, NT, NEXP])
            esum = sb0("esum", [P, NT])
            order = sb0("order", [P, NEXP])
            first = sb0("first", [P, NT, NEXP])
            chosen = sb0("chosen", [P, NT, NEXP])
            choice = sb0("choice", [P, TOPK, NT, NEXP])
            upto = [sb0(f"upto{i}", [P, NT, NEXP]) for i in range(2)]
            place = sb0("place", [P, NT, NEXP])
            tiles_over = sb0("tiles_over", [P, NEXP, NTILE])
            tiles_of = sb0("tiles_of", [P, NEXP])
            tiles_upto = [sb0(f"tiles_upto{i}", [P, NEXP]) for i in range(2)]
            base = sb0("base", [P, NEXP])
            experts_over = sb0("experts_over", [P, NTILE, NEXP])
            expert_no = sb0("expert_no", [P, NTILE])
            pos = sb0("pos", [P, NT, TOPK])
            ps_t = [c0.enter_context(nc.psum_tensor(f"ps_t{i}", [P, CH * P], F32)) for i in range(2)]
            ps_l = c0.enter_context(nc.psum_tensor("ps_l", [P, NT, NEXP], F32))
            ps_before = c0.enter_context(nc.psum_tensor("ps_before", [P, NT, NEXP], F32))
            ps_total = c0.enter_context(nc.psum_tensor("ps_total", [P, NT, NEXP], F32))

            NG = NCH // 4
            GT, GC = NT // NG, NCH // NG
            x_in = [sem(f"x_in{g}") for g in range(NG)]
            turn_in = sem("turn_in")
            wt_in = sem("wt_in")
            pad_in = sem("pad_in")
            dest_in = sem("dest_in")
            stat_done = sem("stat_done")
            mv_done = sem("mv_done")
            std_done = sem("std_done")
            rstd_done = sem("rstd_done")
            eps_done = sem("eps_done")
            xn_done = sem("xn_done")
            xn_out = [sem(f"xn_out{i}") for i in range(4)]
            tr_done = sem("tr_done")
            xT_done = sem("xT_done")
            lg_ps = sem("lg_ps")
            route = sem("route")
            ex_done = sem("ex_done")
            count_ps = sem("count_ps")

            WT = 16 * 12
            R_SHIFTED, R_CHOSEN = 3, 19

            with nc.Block() as block:
                @block.sync
                def _(sp):
                    for g in range(NG):
                        sp.dma_start(x_all[:, g * GT:(g + 1) * GT, :], x_t[:, g * GT:(g + 1) * GT, :]).then_inc(x_in[g], 16)
                    sp.dma_start(b1_sb[:], b1.rearrange("e (c p) -> p e c", p=P), allow_slow_non_contiguous=True
                        ).then_inc(wt_in, 16)
                    for k in range(NCH):
                        sp.wait_ge(xn_done, (k + 1) * CH)
                        sp.dma_start(xn_dram[:, k * CH:(k + 1) * CH, :], xn_chunk[k % 4][:]).then_inc(xn_out[k % 4], 16)

                    def cst(dst, src):
                        sp.dma_start(dst, src, allow_slow_non_contiguous=True).then_inc(cst_in, 16)

                    for i in range(2):
                        cst(q_st[i][0:PROD, :, :], c["c_stair_q"][:, None, :].to_broadcast([PROD, H, S]))
                        cst(k_st[i][0:PROD, :, :], c["c_stair_k"][:, None, :].to_broadcast([PROD, H, S]))
                        cst(k_st[i][MAXROW:ROWS, :, :], c["c_ones"][:, None, :].to_broadcast([3, H, S]))
                    cst(near_mask[:], c["c_near"])
                    for a in range(2):
                        rows, cols = slice(a * P // 2, (a + 1) * P // 2), slice(a * E // 2, (a + 1) * E // 2)
                        cst(bias_col[rows, 0:1], b_q[cols].rearrange("(h d o) -> d h o", d=D, o=1))
                        cst(bias_col[rows, 1:2], b_k[cols].rearrange("(h d o) -> d h o", d=D, o=1))
                        cst(bias_col[rows, 2:3], rel_k[0, :].rearrange("(d h o) -> d h o", h=1, o=1).to_broadcast([D, H // 2, 1]))
                    cst(b_rows[:, 0:E], b_q[None, :].to_broadcast([P, E]))
                    cst(b_rows[:, E:2 * E], b_k[None, :].to_broadcast([P, E]))
                    cst(b_rows[:, 2 * E:], b_v[None, :].to_broadcast([P, E]))
                    cst(rk_all[:], rel_k[None, 0:NEAR, :].to_broadcast([P, NEAR, D]))
                    cst(rv_all[:], rel_v[None, 0:NEAR, :].to_broadcast([P, NEAR, D]))

                    for i in range(4):
                        sp.wait_ge(xn_out[i], 16 * (NCH // 4))

                @block.gpsimd
                def _(pool):
                    pool.wait_ge(pad_in, 16)
                    pool.wait_ge(xn_done, NT)
                    slots = xd.rearrange("(m j p) e -> j p m e", j=PADS, p=P)
                    for j in range(PADS):
                        pool.dma_start(slots[j], pad[:, j, None, :].to_broadcast([P, NTILE * SLOT_T // P // PADS, E + 1])
                                       ).then_inc(pad_out, 16)

                @block.vector
                def _(dve):
                    nc.vector.memset(eps[:], EPS).then_inc(eps_done, 1)

                    def statistics(g):
                        dve.wait_ge(x_in[g], 16)
                        for i in range(g * GT, (g + 1) * GT):
                            nc.vector.bn_stats(stats[:, i, :], x_all[:, i, :]).then_inc(stat_done, 1)
                        ts = slice(g * GT, (g + 1) * GT)
                        me, mo, ve, vo = (stats[:, ts, i] for i in (1, 4, 2, 5))
                        dve.wait_ge(stat_done, (g + 1) * GT)
                        nc.vector.tensor_tensor(mean[:, ts], me, mo, ALU.add).then_inc(mv_done, 1)
                        nc.vector.tensor_tensor(diff[:, ts], me, mo, ALU.subtract).then_inc(mv_done, 1)
                        nc.vector.tensor_tensor(var[:, ts], ve, vo, ALU.add).then_inc(mv_done, 1)
                        dve.wait_ge(mv_done, g * 6 + 2)
                        nc.vector.tensor_scalar(mean[:, ts], mean[:, ts], 0.5, None, ALU.mult).then_inc(mv_done, 1)
                        nc.vector.tensor_tensor(diff[:, ts], diff[:, ts], diff[:, ts], ALU.mult).then_inc(mv_done, 1)
                        dve.wait_ge(mv_done, g * 6 + 5)
                        nc.vector.scalar_tensor_tensor(var[:, ts], diff[:, ts], E / 4.0, var[:, ts],
                                                       ALU.mult, ALU.add).then_inc(mv_done, 1)

                    def normalise(g):
                        ts = slice(g * GT, (g + 1) * GT)
                        dve.wait_ge(std_done, g + 1)
                        nc.vector.reciprocal(rstd[:, ts], rstd[:, ts]).then_inc(rstd_done, 1)
                        dve.wait_ge(rstd_done, g + 1)
                        for k in range(g * GC, (g + 1) * GC):
                            if k >= 4:
                                dve.wait_ge(tr_done, k - 3)
                                dve.wait_ge(xn_out[k % 4], k // 4 * 16)
                            for t in range(CH):
                                i = k * CH + t
                                nc.vector.tensor_scalar(xn_chunk[k % 4][:, t, :], x_all[:, i, :], mean[:, i:i + 1],
                                                        rstd[:, i:i + 1], ALU.subtract, ALU.mult).then_inc(xn_done, 1)

                    statistics(0)
                    for g in range(NG):
                        if g + 1 < NG:
                            statistics(g + 1)
                        normalise(g)

                    steps = [0]

                    def one():
                        steps[0] += 1
                        return 1

                    per_tile = [P, NT, NEXP]
                    dve.wait_ge(wt_in, WT)
                    dve.wait_ge(lg_ps, NCH)
                    nc.vector.tensor_tensor(logits[:], ps_l[:], gb_row[:, None, :].to_broadcast(per_tile), ALU.add
                        ).then_inc(route, one())
                    dve.wait_ge(route, steps[0])
                    nc.vector.tensor_reduce(top[:], logits[:], AX.X, ALU.max).then_inc(route, one())
                    dve.wait_ge(route, steps[0])
                    nc.vector.tensor_tensor(logits[:], logits[:], top[:, :, None].to_broadcast(per_tile), ALU.subtract
                        ).then_inc(route, one())
                    assert steps[0] == R_SHIFTED
                    dve.wait_ge(ex_done, 1)
                    nc.vector.tensor_reduce(esum[:], ex[:], AX.X, ALU.add).then_inc(route, one())
                    dve.wait_ge(route, steps[0])
                    nc.vector.reciprocal(top[:], esum[:]).then_inc(route, one())
                    dve.wait_ge(route, steps[0])
                    nc.vector.tensor_tensor(ex[:], ex[:], top[:, :, None].to_broadcast(per_tile), ALU.mult
                    ).then_inc(route, one())
                    dve.wait_ge(route, steps[0])
                    nc.vector.tensor_scalar(order[:], tile_no[:, 0:NEXP], -1.0, float(NEXP), ALU.mult, ALU.add).then_inc(route, one())
                    for s in range(TOPK):
                        dve.wait_ge(route, steps[0])
                        nc.vector.tensor_reduce(top[:], ex[:], AX.X, ALU.max).then_inc(route, one())
                        dve.wait_ge(route, steps[0])
                        nc.vector.tensor_tensor(first[:], ex[:], top[:, :, None].to_broadcast(per_tile), ALU.is_equal
                                                ).then_inc(route, one())
                        dve.wait_ge(route, steps[0])
                        nc.vector.tensor_tensor(first[:], first[:], order[:, None, :].to_broadcast(per_tile), ALU.mult
                                                ).then_inc(route, one())
                        dve.wait_ge(route, steps[0])
                        nc.vector.tensor_reduce(top[:], first[:], AX.X, ALU.max).then_inc(route, one())
                        dve.wait_ge(route, steps[0])
                        nc.vector.tensor_tensor(choice[:, s], first[:], top[:, :, None].to_broadcast(per_tile), ALU.is_equal
                                                ).then_inc(route, one())
                        dve.wait_ge(route, steps[0])
                        if s == 0:
                            nc.vector.scalar_tensor_tensor(ex[:], choice[:, 0], -2.0, ex[:], ALU.mult, ALU.add
                                                           ).then_inc(route, one())
                    nc.vector.tensor_tensor(chosen[:], choice[:, 0], choice[:, 1], ALU.add).then_inc(route, one())
                    assert steps[0] == R_CHOSEN
                    dve.wait_ge(count_ps, 2)
                    nc.vector.tensor_copy(upto[0][:], ps_total[:]).then_inc(route, one())
                    dve.wait_ge(route, steps[0])
                    cur, shift = 0, 1
                    while shift < NT:
                        nc.vector.tensor_tensor(upto[1 - cur][:, shift:], upto[cur][:, shift:],
                                                upto[cur][:, :NT - shift], ALU.add).then_inc(route, one())
                        nc.vector.tensor_copy(upto[1 - cur][:, 0:shift], upto[cur][:, 0:shift]).then_inc(route, one())
                        dve.wait_ge(route, steps[0])
                        cur, shift = 1 - cur, shift * 2
                    total, spare = upto[cur], upto[1 - cur]
                    nc.vector.tensor_tensor(spare[:], total[:], ps_total[:], ALU.subtract).then_inc(route, one())
                    wide = [P, NEXP, NTILE]
                    nc.vector.tensor_tensor(tiles_over[:], total[:, NT - 1, :, None].to_broadcast(wide),
                                            tile_start[:, None, :].to_broadcast(wide), ALU.is_gt).then_inc(route, one())
                    dve.wait_ge(route, steps[0])
                    nc.vector.tensor_tensor(place[:], spare[:], ps_before[:], ALU.add).then_inc(route, one())
                    nc.vector.tensor_reduce(tiles_of[:], tiles_over[:], AX.X, ALU.add).then_inc(route, one())
                    dve.wait_ge(route, steps[0])
                    nc.vector.tensor_copy(tiles_upto[0][:], tiles_of[:]).then_inc(route, one())
                    dve.wait_ge(route, steps[0])
                    cur, shift = 0, 1
                    while shift < NEXP:
                        nc.vector.tensor_tensor(tiles_upto[1 - cur][:, shift:], tiles_upto[cur][:, shift:],
                                                tiles_upto[cur][:, :NEXP - shift], ALU.add).then_inc(route, one())
                        nc.vector.tensor_copy(tiles_upto[1 - cur][:, 0:shift], tiles_upto[cur][:, 0:shift]
                    ).then_inc(route, one())
                        dve.wait_ge(route, steps[0])
                        cur, shift = 1 - cur, shift * 2
                    nc.vector.tensor_tensor(base[:], tiles_upto[cur][:], tiles_of[:], ALU.subtract).then_inc(route, one())
                    nc.vector.tensor_tensor(experts_over[:], tile_no[:, :, None].to_broadcast([P, NTILE, NEXP]),
                                            tiles_upto[cur][:, None, :].to_broadcast([P, NTILE, NEXP]), ALU.is_ge
                           ).then_inc(route, one())
                    dve.wait_ge(route, steps[0])
                    nc.vector.tensor_scalar(base[:], base[:], float(SLOT_T), None, ALU.mult).then_inc(route, one())
                    nc.vector.tensor_reduce(expert_no[:], experts_over[:], AX.X, ALU.add).then_inc(route, one())
                    dve.wait_ge(route, steps[0])
                    nc.vector.tensor_scalar(tile_expert[:], expert_no[:], float(NEXP - 1), None, ALU.min
                  ).then_inc(route, one())
                    nc.vector.tensor_tensor(place[:], place[:], base[:, None, :].to_broadcast(per_tile), ALU.add
                        ).then_inc(route, one())
                    dve.wait_ge(route, steps[0])
                    for s in range(TOPK):
                        nc.vector.tensor_tensor(choice[:, s], choice[:, s], place[:], ALU.mult).then_inc(route, one())
                    dve.wait_ge(route, steps[0])
                    for s in range(TOPK):
                        nc.vector.tensor_reduce(pos[:, :, s], choice[:, s], AX.X, ALU.add).then_inc(route, one())
                    dve.wait_ge(route, steps[0])
                    nc.vector.tensor_copy(pos_all[:], pos[:]).then_inc(route, one())

                @block.tensor
                def _(pe):
                    pe.wait_ge(turn_in, 32)

                    def turn(k):
                        pe.wait_ge(xn_done, (k + 1) * CH)
                        if k >= 2:
                            pe.wait_ge(xT_done, k - 1)
                        for t in range(CH):
                            last = nc.tensor.transpose(ps_t[k % 2][:, t * P:(t + 1) * P], xn_chunk[k % 4][:, t, :], ident[:])
                        last.then_inc(tr_done, 1)

                    def gate(k):
                        pe.wait_ge(xT_done, k + 1)
                        for t in range(k * CH, (k + 1) * CH):
                            last = nc.tensor.matmul(ps_l[:, t, :], xnT[:, t * P:(t + 1) * P], gw[:], start=True, stop=True,
                                                    skip_group_check=True)
                        last.then_inc(lg_ps, 1)

                    turn(0)
                    for k in range(NCH):
                        if k + 1 < NCH:
                            turn(k + 1)
                        gate(k)
                    pe.wait_ge(wt_in, WT)
                    pe.wait_ge(route, R_CHOSEN)
                    nc.tensor.matmul(ps_total[:], ones[:], chosen[:], start=True, stop=True).then_inc(count_ps, 1)
                    nc.tensor.matmul(ps_before[:], before[:], chosen[:], start=True, stop=True).then_inc(count_ps, 1)

                @block.scalar
                def _(act):
                    act.dma_start(ident[:], c["c_ident"]).then_inc(turn_in, 16)
                    act.dma_start(gw[:], gate_w).then_inc(turn_in, 16)
                    act.dma_start(gb_row[:], gate_b[None, :].to_broadcast([P, NEXP])).then_inc(wt_in, 16)
                    act.dma_start(ones[:], c["c_all"]).then_inc(wt_in, 16)
                    act.dma_start(before[:], c["c_before"]).then_inc(wt_in, 16)
                    act.dma_start(pad[:], c["c_pad"]).then_inc(pad_in, 16)
                    act.dma_start(tile_no[:], c["c_tile"]).then_inc(wt_in, 16)
                    act.dma_start(tile_start[:], c["c_tile_start"]).then_inc(wt_in, 16)
                    act.dma_start(ident_bf[:], c["c_ident_bf"]).then_inc(wt_in, 16)
                    act.dma_start(bo_row[:], b_o[None, :].to_broadcast([P, E])).then_inc(wt_in, 16)
                    act.dma_start(wqkv[:, 0:E], W_q).then_inc(wt_in, 16)
                    act.dma_start(wqkv[:, E:2 * E], W_k).then_inc(wt_in, 16)
                    act.dma_start(wqkv[:, 2 * E:], W_v).then_inc(wt_in, 16)
                    act.dma_start(wo[:], W_o).then_inc(wt_in, 16)
                    act.dma_start(dest_all[:], c["c_dest"]).then_inc(dest_in, 16)
                    act.wait_ge(eps_done, 1)

                    def deviation(g):
                        ts = slice(g * GT, (g + 1) * GT)
                        act.wait_ge(mv_done, (g + 1) * 6)
                        nc.scalar.activation(rstd[:, ts], var[:, ts], ACT.Sqrt, bias=eps[:], scale=1.0 / E).then_inc(std_done, 1)

                    deviation(0)
                    for g in range(NG):
                        if g + 1 < NG:
                            deviation(g + 1)
                        for k in range(g * GC, (g + 1) * GC):
                            act.wait_ge(tr_done, k + 1)
                            nc.scalar.activation(xnT[:, k * CH * P:(k + 1) * CH * P], ps_t[k % 2][:], ACT.Copy
                        ).then_inc(xT_done, 1)
                    act.wait_ge(route, R_SHIFTED)
                    nc.scalar.activation(ex[:], logits[:], ACT.Exp).then_inc(ex_done, 1)
                    act.wait_ge(dest_in, 16)

        with ExitStack() as c1:
            attention(nc, c1, NB, RS, xnT, attn_all, wqkv, wo, ident, ident_bf, bo_row,
                      b_q, b_k, b_v, rel_k, rel_v, c, xn_dram, xd, pos_all, dest_all, pad_out,
                      (q_st, k_st, near_mask, bias_col, rk_all, rv_all, b_rows, cst_in))

        turned.close()
        with ExitStack() as c2:
            experts(nc, c2, NT, x_t, attn_all, tile_expert, ident, b1_sb, w1, w2, b2, xd, out_t)


def attention(nc, ctx, NB, RS, xnT, attn_all, wqkv, wo, ident, ident_bf, bo_row, b_q, b_k, b_v, rel_k, rel_v, c,
              xn_dram, xd, pos_all, dest_all, pad_out, loaded):
    def sb(name, shape, dt=F32):
        return ctx.enter_context(nc.sbuf_tensor(name, shape, dt))

    def sem(name):
        return ctx.enter_context(nc.semaphore(name))

    def bank(name, n=1):
        return ctx.enter_context(nc.psum_tensor(name, [P, n * 512], F32))

    HH = H // 2
    NP = len(Q_PARTS)
    q_st, k_st, near_mask, bias_col, rk_all, rv_all, b_rows, cst_in = loaded
    w_turn = sb("w_turn", [P, 2, E])
    xb = [sb(f"xb{i}", [P, S]) for i in range(2)]
    qk32 = sb("qk32", [P, 2, S])
    rem = sb("rem", [P, 2, S])
    parts = [sb(f"parts{i}", [P, 2, NP, S], BF16) for i in range(2)]
    parts_dram = [nc.dram_tensor(f"parts_dram{i}", [2, NP, P, S], BF16, kind="Internal").ap() for i in range(2)]
    tok_a = [sb(f"tok_a{i}", [P, TT, 3 * E]) for i in range(2)]
    tok_b = [sb(f"tok_b{i}", [P, TT, 2 * E]) for i in range(2)]
    near_kv = [sb(f"near_kv{i}", [P, TT, NEAR, 2 * E]) for i in range(2)]
    v_aug = [sb(f"v_aug{i}", [P, TT, H, 32]) for i in range(2)]
    prod = sb("prod", [P, TT, NEAR, E])
    pv_near = sb("pv_near", [P, TT, NEAR, E])
    s_near = sb("s_near", [P, TT, NEAR, H])
    near_top = sb("near_top", [P, TT, H])
    far_top = sb("far_top", [P, TT, H])
    row_max = sb("row_max", [P, TT, H])
    neg_res = [sb(f"neg_res{i}", [P, TT, HH]) for i in range(2)]
    max_parts = sb("max_parts", [P, 2, TT, 3, HH], BF16)
    max_T = [sb(f"max_T{i}", [3 * HH, S], BF16) for i in range(2)]
    near_diff = sb("near_diff", [P, TT, NEAR, H])
    p_near = [sb(f"p_near{i}", [P, TT, NEAR, H]) for i in range(2)]
    num_near = [sb(f"num_near{i}", [P, TT, E]) for i in range(2)]
    den_near = [sb(f"den_near{i}", [P, TT, H]) for i in range(2)]
    probs = [sb(f"probs{i}", [P, 1024]) for i in range(6)]
    ctx_T = sb("ctx_T", [P, 4, S])
    num = sb("num", [P, TT, E])
    den = sb("den", [P, TT, H])
    rden = sb("rden", [P, TT, H])
    o_tok = [sb(f"o_tok{i}", [P, TT, E]) for i in range(2)]
    o_T = sb("o_T", [P, S])
    rel_b = sb("rel_b", [P, 2 * E])
    rel_c = sb("rel_c", [P, 2 * E])
    bias_f = probs[0][0:3, 0:4 * E]
    bias_part = [probs[1 + i][0:3, 0:2 * E].bitcast(BF16) for i in range(3)]
    bias_rem = [probs[1 + i][0:3, 4 * E:] for i in range(2)]
    bias_rows = sb("bias_rows", [3, 4 * E], BF16)
    ones3 = sb("ones3", [3, P], BF16)

    ps_max = bank("ps_max", 2)
    ps_exp = bank("ps_exp", 2)
    ps_ctx = bank("ps_ctx", 2)
    X0 = bank("ps_x0")
    X1 = bank("ps_x1")

    stage = sb("stage", [P, TOPK, TT, E + 1])
    stage_pos = sb("stage_pos", [P, TT, TOPK], U32)

    staged = sem("staged")
    tagged = sem("tagged")
    stage_ready = sem("stage_ready")
    scattered = sem("scattered")
    zeroed = sem("zeroed")
    bias_done = sem("bias_done")
    NBIAS = 10 + 5 + 3 + 4
    xb_done = sem("xb_done")
    qk_ps = sem("qk_ps")
    qk_cp = sem("qk_cp")
    part_a = sem("part_a")
    part_p = sem("part_p")
    stack_in = [[sem(f"stack_in{v}{h}") for h in range(2)] for v in range(2)]
    parts_out = [[sem(f"parts_out{v}{h}") for h in range(2)] for v in range(2)]
    tok_ps = sem("tok_ps")
    tok_act = sem("tok_act")
    tok_ev = sem("tok_ev")
    shift_in = [sem(f"shift_in{v}") for v in range(2)]
    vaug_done = sem("vaug_done")
    prod_done = sem("prod_done")
    sn_done = sem("sn_done")
    max_ps = sem("max_ps")
    max_rd = sem("max_rd")
    mrow = sem("mrow")
    diff_done = sem("diff_done")
    mT_ps = sem("mT_ps")
    mT_cp = sem("mT_cp")
    mrow_in = [sem(f"mrow_in{h}") for h in range(2)]
    p_done = sem("p_done")
    pvn_done = sem("pvn_done")
    nden_done = sem("nden_done")
    nnum_done = sem("nnum_done")
    exp_ps = sem("exp_ps")
    exp_done = sem("exp_done")
    ctx_ps = sem("ctx_ps")
    ctx_cp = sem("ctx_cp")
    cx_ps = sem("cx_ps")
    nd = sem("nd")
    fin = sem("fin")
    oT_ps = sem("oT_ps")
    oT_cp = sem("oT_cp")
    o_ps = sem("o_ps")
    o_done = sem("o_done")

    MAX_STEPS = [(1, 0), (1, 1), (0, 0), (1, 2), (1, 3), (0, 1)]
    EXP_STEPS = [(0, 0), (0, 1), (1, 0), (0, 2), (0, 3), (1, 1)]
    NS = len(MAX_STEPS)
    NCST = 6 + 1 + 6 + 5
    hd = "p (h d) -> p h d"

    def pipeline(eng, body):
        def one(b, hb, u, known):
            body(lambda k: (b + k, (u + k) % 2, hb + (u + k) // 2),
                 {k: known is None or 0 <= known + k < NB for k in range(-3, 5)})

        for b in range(-3, 4):
            one(b, b // 2, b % 2, b)
        with eng.Fori(1, NB // 4 - 1) as j:
            for u in range(4):
                one(j * 4 + u, j * 2 + u // 2, u % 2, None)
        for b in range(NB - 4, NB + 2):
            one(b, b // 2, b % 2, b)

    with nc.Block() as block:
        @block.sync
        def _(sp):
            def stack(half, v):
                hs = slice(half * HH, (half + 1) * HH)
                rows = slice(half * P // 2, (half + 1) * P // 2)
                for w, st in enumerate((q_st[v], k_st[v])):
                    src = parts_dram[v][w, :, rows, :].rearrange("c (d h) q -> c d (h q)", d=D)
                    sp.dma_start(st[PROD:MAXROW, hs, :].rearrange("r h q -> r (h q)"), src).then_inc(stack_in[v][half], 16)

            def load_stage(n):
                for s in range(TOPK):
                    sp.dma_start(stage[:, s, :, 0:E], xn_dram[:, bass.ds(n * TT, TT), :]).then_inc(staged, 16)

            def body(at, on):
                b, u, hb = at(0)

                def rows_of_max(k, half):
                    n, v, hn = at(k)
                    sp.wait_ge(mT_cp, n * 2 + half + 1)
                    sp.dma_start(q_st[v][MAXROW:ROWS, half * HH:(half + 1) * HH, :], max_T[half][:]).then_inc(mrow_in[half], 16)

                if on[0]:
                    rows_of_max(0, 1)
                    if on[-1]:
                        sp.wait_ge(scattered, b * 64)
                    load_stage(b)
                if on[2]:
                    n, v, hn = at(2)
                    if on[0]:
                        sp.wait_ge(exp_ps, b * NS + 3)
                    sp.wait_ge(parts_out[v][0], hn * 16 + 16)
                    stack(0, v)
                if on[1]:
                    rows_of_max(1, 0)
                if on[2]:
                    n, v, hn = at(2)
                    sp.wait_ge(tok_ev, n * 4 + 4)
                    a, kb, nr = tok_a[v], tok_b[v], near_kv[v]
                    for dst, src in ((nr[2:P, :, 2, :], a[0:P - 2, :, E:]), (nr[0:2, 1, 2, :], a[P - 2:P, 0, E:]),
                                     (nr[1:P, :, 1, :], kb[0:P - 1, :, :]), (nr[0:1, 1, 1, :], kb[P - 1:P, 0, :])):
                        sp.dma_start(dst, src).then_inc(shift_in[v], 16)
                if on[3]:
                    n, v, hn = at(3)
                    sp.wait_ge(part_p, n * 3 + 3)
                    if on[1]:
                        for half in range(2):
                            sp.wait_ge(stack_in[v][half], hn * 2 * 16)
                    for half in range(2):
                        rows = slice(half * P // 2, (half + 1) * P // 2)
                        sp.dma_start(parts_dram[v].rearrange("w c p q -> p (w c) q")[rows],
                                     parts[v][rows].rearrange("p w c q -> p (w c) q")).then_inc(parts_out[v][half], 16)
                if on[2]:
                    n, v, hn = at(2)
                    if on[0]:
                        sp.wait_ge(exp_ps, b * NS + 6)
                    sp.wait_ge(parts_out[v][1], hn * 16 + 16)
                    stack(1, v)

            pipeline(sp, body)

        NSTK = 2 * 16

        @block.gpsimd
        def _(pool):
            for i in range(2):
                nc.gpsimd.memset(near_kv[i][:], 0.0).then_inc(zeroed, 1)
                nc.gpsimd.memset(v_aug[i][:], 0.0).then_inc(zeroed, 1)
            pool.wait_ge(zeroed, 4)
            for i in range(2):
                nc.gpsimd.memset(v_aug[i][:, :, :, D:D + 1], 1.0).then_inc(zeroed, 1)

            pool.wait_ge(pad_out, PADS * 16)

            def body(at, on):
                b, u, hb = at(0)
                if on[1]:
                    n, v, hn = at(1)
                    pool.wait_ge(shift_in[v], hn * 64 + 64)
                    if on[0]:
                        pool.wait_ge(sn_done, b * 3 + 1)
                    for t in range(TT):
                        last = nc.gpsimd.tensor_tensor(prod[:, t, :, :], near_kv[v][:, t, :, 0:E],
                                                       tok_a[v][:, t, None, 0:E].to_broadcast([P, NEAR, E]), ALU.mult)
                    last.then_inc(prod_done, 1)
                if on[0]:
                    pool.wait_ge(p_done, b + 1)
                    if on[-1]:
                        pool.wait_ge(nnum_done, b * 2)
                    for t in range(TT):
                        for n in range(NEAR):
                            last = nc.gpsimd.tensor_tensor(pv_near[:, t, n, :].rearrange(hd, d=D),
                                                           near_kv[u][:, t, n, E:].rearrange(hd, d=D),
                                                           p_near[u][:, t, n, :, None].to_broadcast([P, H, D]), ALU.mult)
                    last.then_inc(pvn_done, 1)
                if on[3]:
                    n, v, hn = at(3)
                    pool.wait_ge(part_a, n * 4 + 2)
                    nc.gpsimd.tensor_tensor(rem[:], qk32[:], parts[v][:, :, 1, :], ALU.subtract).then_inc(part_p, 1)
                if on[3]:
                    n, v, hn = at(3)
                    q, k = parts[v][:, 0, :, :], parts[v][:, 1, :, :]
                    pool.wait_ge(part_a, n * 4 + 4)
                    nc.gpsimd.tensor_tensor(q[:, 5, :], rem[:, 0, :], q[:, 4, :], ALU.subtract).then_inc(part_p, 1)
                    nc.gpsimd.tensor_tensor(k[:, 0, :], rem[:, 1, :], k[:, 4, :], ALU.subtract).then_inc(part_p, 1)
                if on[0]:
                    if on[-2]:
                        pool.wait_ge(nd, b * 4 - 4)
                    pool.wait_ge(pvn_done, b + 1)
                    nc.gpsimd.tensor_tensor(num_near[u][:], pv_near[:, :, 0, :], pv_near[:, :, 1, :], ALU.add
                       ).then_inc(nnum_done, 1)
                    pool.wait_ge(nnum_done, b * 2 + 1)
                    nc.gpsimd.tensor_tensor(num_near[u][:], num_near[u][:], pv_near[:, :, 2, :], ALU.add
                  ).then_inc(nnum_done, 1)
                if on[0]:
                    if on[-1]:
                        pool.wait_ge(scattered, b * 64)
                    for s in range(TOPK):
                        nc.gpsimd.tensor_copy(stage[:, s, :, E].bitcast(U32), dest_all[:, s, bass.ds(b * TT, TT)]
                           ).then_inc(tagged, 1)
                    nc.gpsimd.tensor_copy(stage_pos[:], pos_all[:, bass.ds(b * TT, TT), :]).then_inc(tagged, 1)
                    pool.wait_ge(staged, b * 32 + 32)
                    pool.wait_ge(tagged, b * 3 + 3)
                    pool.sem_inc(stage_ready, 1)
                    for s in range(TOPK):
                        for t in range(TT):
                            nc.gpsimd.indirect_dma_start(xd, bass.IndirectOffsetOnAxis(ap=stage_pos[:, t, s:s + 1], axis=0),
                                                         stage[:, s, t, :], None).then_inc(scattered, 16)
            pipeline(pool, body)
            pool.wait_ge(scattered, NB * 64)

        @block.scalar
        def _(act):
            act.wait_ge(bias_done, NBIAS)
            act.wait_ge(zeroed, 6)
            nc.scalar.activation(xb[0][:], xnT[:, 0:S], ACT.Copy).then_inc(xb_done, 1)

            def body(at, on):
                b, u, hb = at(0)

                def step(s):
                    act.wait_ge(exp_ps, b * NS + s + 1)
                    if on[-1]:
                        act.wait_ge(ctx_ps, b * 2 - (1 if s < 3 else 0))
                    nc.scalar.activation(probs[s][:], ps_exp[:], ACT.Exp, scale=RS).then_inc(exp_done, 1)

                def qk():
                    n, v, hn = at(3)
                    act.wait_ge(qk_ps, n + 1)
                    if on[2]:
                        act.wait_ge(part_p, n * 3)
                    nc.scalar.activation(qk32[:, 0, :], X0[:, 0:S], ACT.Identity, bias=bias_col[:, 0:1]).then_inc(qk_cp, 1)
                    nc.scalar.activation(qk32[:, 1, :], X0[:, S:2 * S], ACT.Identity, bias=bias_col[:, 3:4]).then_inc(qk_cp, 1)

                def first_parts():
                    n, v, hn = at(3)
                    act.wait_ge(qk_cp, n * 2 + 2)
                    if on[1]:
                        for half in range(2):
                            act.wait_ge(parts_out[v][half], hn * 16)
                    for w, slots in ((0, slice(0, 3)), (1, slice(1, 6, 2))):
                        nc.scalar.activation(parts[v][:, w, slots, :], qk32[:, w, None, :].to_broadcast([P, 3, S]),
                                             ACT.Copy).then_inc(part_a, 1)

                def qk2():
                    n, v, hn = at(3)
                    act.wait_ge(part_p, n * 3 + 1)
                    for w, slots in ((0, slice(3, 5)), (1, slice(2, 5, 2))):
                        nc.scalar.activation(parts[v][:, w, slots, :], rem[:, w, None, :].to_broadcast([P, 2, S]),
                                             ACT.Copy).then_inc(part_a, 1)

                def tok(t):
                    n, v, hn = at(2)
                    act.wait_ge(tok_ps, n * 2 + t + 1)
                    if t == 0 and on[0]:
                        act.wait_ge(vaug_done, b + 1)
                        act.wait_ge(prod_done, b + 1)
                    nc.scalar.activation(tok_a[v][:, t, :], X1[:, 0:3 * E], ACT.Copy).then_inc(tok_act, 1)

                def vaug():
                    n, v, hn = at(1)
                    act.wait_ge(tok_act, n * 2 + 2)
                    if on[-1]:
                        act.wait_ge(ctx_ps, b * 2)
                    nc.scalar.activation(v_aug[v][:, :, :, 0:D], tok_a[v][:, :, 2 * E:].rearrange("p t (h d) -> p t h d", d=D),
                                         ACT.Copy).then_inc(vaug_done, 1)

                def ctx_copy(k, half):
                    n, v, hn = at(k)
                    act.wait_ge(ctx_ps, n * 2 + half + 1)
                    if half == 0 and on[-1]:
                        act.wait_ge(cx_ps, b * 2)
                    nc.scalar.activation(ctx_T[:, 2 * half:2 * half + 2, :], ps_ctx[:, half * 512:(half + 1) * 512],
                                         ACT.Copy).then_inc(ctx_cp, 1)

                def max_copy(k, half):
                    n, v, hn = at(k)
                    act.wait_ge(mT_ps, n * 2 + half + 1)
                    if on[k - 1]:
                        act.wait_ge(mrow_in[half], n * 16)
                    nc.scalar.activation(max_T[half][:], X1[0:3 * HH, 3 * E:].bitcast(BF16), ACT.Copy).then_inc(mT_cp, 1)

                for s in range(NS):
                    if s == 1 and on[0]:
                        max_copy(0, 1)
                    if on[0]:
                        step(s)
                    if s == 0:
                        if on[-1]:
                            ctx_copy(-1, 1)
                        if on[0]:
                            act.wait_ge(diff_done, b + 1)
                            nc.scalar.activation(p_near[u][:], near_diff[:], ACT.Exp, scale=RS).then_inc(p_done, 1)
                        if on[3]:
                            qk()
                    if s == 1 and on[3]:
                        first_parts()
                    if s == 1 and on[2]:
                        tok(0)
                    if s == 2 and on[3]:
                        qk2()
                    if s == 2 and on[1]:
                        vaug()
                    if s == 3 and on[-2]:
                        n, v, hn = at(-2)
                        act.wait_ge(oT_ps, n + 1)
                        nc.scalar.activation(o_T[:], X0[:, 0:S], ACT.Copy).then_inc(oT_cp, 1)
                    if s == 3 and on[2]:
                        tok(1)
                    if s == 4 and on[-2]:
                        n, v, hn = at(-2)
                        act.wait_ge(o_ps, n + 1)
                        nc.scalar.activation(attn_all[:, bass.ds(n * 2, 2), :],
                                             X0[:, 256:512].rearrange("p (t e) -> p t e", t=TT), ACT.Copy).then_inc(o_done, 1)
                    if s == 4 and on[1]:
                        max_copy(1, 0)
                    if s == 4 and on[4]:
                        n, v, hn = at(4)
                        if on[2]:
                            act.wait_ge(tok_ps, (n - 1) * 2)
                        nc.scalar.activation(xb[v][:], xnT[:, bass.ds(n * S, S)], ACT.Copy).then_inc(xb_done, 1)
                    if s == 5 and on[0]:
                        ctx_copy(0, 0)

            pipeline(act, body)

        @block.vector
        def _(dve):
            dve.wait_ge(cst_in, 16 * NCST)
            nc.vector.tensor_tensor(bias_col[:, 3:4], bias_col[:, 1:2], bias_col[:, 2:3], ALU.add).then_inc(bias_done, 1)
            nc.vector.tensor_copy(bias_f[:, 0:E], b_rows[0:3, 0:E]).then_inc(bias_done, 1)
            nc.vector.tensor_copy(bias_f[:, 3 * E:], bo_row[0:3, :]).then_inc(bias_done, 1)
            for w, tab in ((1, rk_all), (2, rv_all)):
                nc.vector.tensor_tensor(bias_f[:, w * E:(w + 1) * E].rearrange(hd, d=D),
                                        b_rows[0:3, w * E:(w + 1) * E].rearrange(hd, d=D),
                                        tab[0:3, 0, None, :].to_broadcast([3, H, D]), ALU.add).then_inc(bias_done, 1)
                for dst, entry in ((rel_b, 1), (rel_c, 2)):
                    nc.vector.tensor_tensor(dst[:, (w - 1) * E:w * E].rearrange(hd, d=D),
                                            tab[:, entry, None, :].to_broadcast([P, H, D]),
                                            tab[:, 0, None, :].to_broadcast([P, H, D]), ALU.subtract).then_inc(bias_done, 1)
            nc.vector.memset(ones3[:], 1.0).then_inc(bias_done, 1)
            dve.wait_ge(bias_done, 10)
            left = bias_f
            for i in range(3):
                nc.vector.tensor_copy(bias_part[i], left).then_inc(bias_done, 1)
                if i < 2:
                    dve.wait_ge(bias_done, 11 + 2 * i)
                    nc.vector.tensor_tensor(bias_rem[i], left, bias_part[i], ALU.subtract).then_inc(bias_done, 1)
                    dve.wait_ge(bias_done, 12 + 2 * i)
                    left = bias_rem[i]
            dve.wait_ge(bias_done, 15)
            nc.vector.tensor_scalar(bias_rows[:], bias_part[0], ident[0:3, 0:1], None, ALU.mult).then_inc(bias_done, 1)
            for i in (1, 2):
                dve.wait_ge(bias_done, 15 + i)
                nc.vector.scalar_tensor_tensor(bias_rows[:], bias_part[i], ident[0:3, i:i + 1], bias_rows[:],
                                               ALU.mult, ALU.add).then_inc(bias_done, 1)
            for w in range(2):
                for a in range(2):
                    cols = slice(a * E // 2, (a + 1) * E // 2)
                    nc.vector.tensor_copy(w_turn[:, w, cols].rearrange("p (d h) -> p d h", d=D),
                                          wqkv[:, w * E + a * E // 2:w * E + (a + 1) * E // 2]
                                          .rearrange("p (h d) -> p d h", d=D)).then_inc(bias_done, 1)
            dve.wait_ge(bias_done, NBIAS)
            dve.wait_ge(zeroed, 6)

            def body(at, on):
                b, u, hb = at(0)

                def tok(t, w):
                    n, v, hn = at(2)
                    if w == 0:
                        dve.wait_ge(tok_act, n * 2 + t + 1)
                        if t == 0 and on[0]:
                            dve.wait_ge(prod_done, b + 1)
                        nc.vector.tensor_tensor(tok_b[v][:, t, :], X1[:, E:3 * E], rel_b[:], ALU.add).then_inc(tok_ev, 1)
                    else:
                        if t == 0 and on[0]:
                            dve.wait_ge(pvn_done, b + 1)
                        nc.vector.tensor_tensor(near_kv[v][:, t, 0, :], X1[:, E:3 * E], rel_c[:], ALU.add).then_inc(tok_ev, 1)

                def max_step(s):
                    n, v, hn = at(1)
                    t, g = MAX_STEPS[s]
                    dve.wait_ge(max_ps, n * NS + s + 1)
                    w = 4 if t == 1 else 8
                    nc.vector.tensor_reduce(far_top[:, t, w * g:w * g + w], ps_max[:].rearrange("p (h k) -> p h k", h=w),
                                            AX.X, ALU.max).then_inc(max_rd, 1)

                def near_scores():
                    n, v, hn = at(1)
                    dve.wait_ge(prod_done, n + 1)
                    nc.vector.tensor_reduce(s_near[:], prod[:].rearrange("p t n (h d) -> p (t n) h d", d=D),
                                            AX.X, ALU.add).then_inc(sn_done, 1)
                    dve.wait_ge(sn_done, n * 3 + 1)
                    flat = s_near[:].rearrange("p t n h -> p (t n h)")
                    nc.vector.tensor_tensor(flat, flat, near_mask[:], ALU.add).then_inc(sn_done, 1)
                    dve.wait_ge(sn_done, n * 3 + 2)
                    nc.vector.tensor_reduce(near_top[:], s_near[:].rearrange("p t n h -> p t h n"),
                                            AX.X, ALU.max).then_inc(sn_done, 1)

                def row_max_step(k, half, step):
                    n, v, hn = at(k)
                    first = n * 12 + half * 6
                    hs = slice(half * HH, (half + 1) * HH)
                    m = row_max[:, :, hs]
                    mp = [max_parts[:, half, :, i, :] for i in range(3)]
                    if step == 0:
                        dve.wait_ge(max_rd, n * NS + 3 * half + 3)
                        dve.wait_ge(sn_done, n * 3 + 3)
                        nc.vector.tensor_tensor(m, far_top[:, :, hs], near_top[:, :, hs], ALU.max).then_inc(mrow, 1)
                        return
                    dve.wait_ge(mrow, first + step)
                    if step == 1:
                        if on[k - 1]:
                            dve.wait_ge(mT_ps, n * 2 - 1 + half)
                        nc.vector.tensor_scalar(mp[0], m, -1.0, None, ALU.mult).then_inc(mrow, 1)
                    elif step == 2:
                        nc.vector.scalar_tensor_tensor(neg_res[0][:], m, -1.0, mp[0], ALU.mult, ALU.subtract).then_inc(mrow, 1)
                    elif step == 3:
                        nc.vector.tensor_copy(mp[1], neg_res[0][:]).then_inc(mrow, 1)
                    elif step == 4:
                        nc.vector.tensor_tensor(neg_res[1][:], neg_res[0][:], mp[1], ALU.subtract).then_inc(mrow, 1)
                    else:
                        nc.vector.tensor_copy(mp[2], neg_res[1][:]).then_inc(mrow, 1)

                def near_denominator():
                    dve.wait_ge(p_done, b + 1)
                    nc.vector.tensor_reduce(den_near[u][:], p_near[u][:].rearrange("p t n h -> p t h n"),
                                            AX.X, ALU.add).then_inc(nden_done, 1)

                def out_step(t, step):
                    n, v, hn = at(-1)
                    acc = X0[:].rearrange("p (h r) -> p h r", r=32)
                    if step == 0:
                        dve.wait_ge(cx_ps, n * 2 + t + 1)
                        if t == 0:
                            dve.wait_ge(nden_done, n + 1)
                        nc.vector.tensor_tensor(den[:, t, :], acc[:, :, D], den_near[v][:, t, :], ALU.add).then_inc(nd, 1)
                    elif step == 1:
                        if t == 0:
                            dve.wait_ge(nnum_done, n * 2 + 2)
                        nc.vector.tensor_tensor(num[:, t, :].rearrange(hd, d=D), acc[:, :, 0:D],
                                                num_near[v][:, t, :].rearrange(hd, d=D), ALU.add).then_inc(nd, 1)
                    elif step == 2:
                        dve.wait_ge(nd, n * 4 + 2 * t + 1)
                        nc.vector.reciprocal(rden[:, t, :], den[:, t, :]).then_inc(fin, 1)
                    else:
                        dve.wait_ge(fin, n * 4 + 2 * t + 1)
                        dve.wait_ge(nd, n * 4 + 2 * t + 2)
                        if t == 0 and on[-3]:
                            dve.wait_ge(oT_ps, n - 1)
                        nc.vector.tensor_tensor(o_tok[v][:, t, :].rearrange(hd, d=D), num[:, t, :].rearrange(hd, d=D),
                                                rden[:, t, :, None].to_broadcast([P, H, D]), ALU.mult).then_inc(fin, 1)

                def near_differences():
                    n, v, hn = at(1)
                    if on[0]:
                        dve.wait_ge(p_done, n)
                    dve.wait_ge(mrow, n * 12 + 7)
                    nc.vector.tensor_tensor(near_diff[:], s_near[:], row_max[:, :, None, :].to_broadcast([P, TT, NEAR, H]),
                                            ALU.subtract).then_inc(diff_done, 1)

                for s in range(NS):
                    if on[1]:
                        max_step(s)
                    if s == 0 and on[0]:
                        for i in (3, 4, 5):
                            row_max_step(0, 1, i)
                    if s == 1 and on[1]:
                        near_scores()
                    if s == 2:
                        if on[2]:
                            tok(0, 0)
                        if on[1]:
                            row_max_step(1, 0, 0)
                        if on[2]:
                            tok(0, 1)
                        if on[-1]:
                            out_step(0, 0)
                            out_step(0, 1)
                    if s == 3:
                        for i in range(1, 6):
                            if on[1]:
                                row_max_step(1, 0, i)
                            if on[-1] and i == 1:
                                out_step(0, 2)
                            if on[2] and i in (3, 4):
                                tok(1, i - 3)
                    if s == 4 and on[0]:
                        near_denominator()
                    if s == 4 and on[-1]:
                        out_step(0, 3)
                for i in range(3):
                    if on[1]:
                        row_max_step(1, 1, i)
                    if on[1] and i == 1:
                        near_differences()
                    if on[-1]:
                        out_step(1, i)
                if on[-1]:
                    out_step(1, 3)

            pipeline(dve, body)

        @block.tensor
        def _(pe):
            pe.wait_ge(bias_done, NBIAS)
            pe.wait_ge(zeroed, 6)

            def body(at, on):
                b, u, hb = at(0)

                def qk_proj():
                    n, v, hn = at(3)
                    pe.wait_ge(xb_done, n + 1)
                    if on[-2]:
                        pe.wait_ge(nd, b * 4 - 4)
                    elif on[2]:
                        pe.wait_ge(qk_cp, n * 2)
                    nc.tensor.matmul(X0[:, 0:S], w_turn[:, 0, :], xb[v][:], start=True, stop=True, skip_group_check=True)
                    nc.tensor.matmul(X0[:, S:], w_turn[:, 1, :], xb[v][:], start=True, stop=True,
                                     skip_group_check=True).then_inc(qk_ps, 1)

                def tok_proj(t):
                    n, v, hn = at(2)
                    if t == 1 or on[1]:
                        pe.wait_ge(tok_ev, n * 4 + 2 * t)
                    if t == 0 and on[0]:
                        pe.wait_ge(mT_cp, b * 2 + 2)
                    nc.tensor.matmul(X1[:, 0:3 * E], xb[v][:, t * P:(t + 1) * P], wqkv[:], start=True, stop=False,
                                     skip_group_check=True)
                    nc.tensor.matmul(X1[:, 0:3 * E], ones3[:], bias_rows[:, 0:3 * E], start=False, stop=True,
                                     skip_group_check=True).then_inc(tok_ps, 1)

                def max_step(s):
                    n, v, hn = at(1)
                    t, g = MAX_STEPS[s]
                    if s % 3 == 0:
                        pe.wait_ge(stack_in[v][s // 3], hn * NSTK + NSTK)
                    if s > 0 or on[0]:
                        pe.wait_ge(max_rd, n * NS + s)
                    q, k = q_st[v], k_st[v]
                    if t == 1:
                        for i in range(4):
                            nc.tensor.matmul(ps_max[:, i * S + P:(i + 1) * S], q[0:MAXROW, 4 * g + i, P:],
                                             k[0:MAXROW, 4 * g + i, P:], start=True, stop=True, skip_group_check=True)
                        for i in range(4):
                            last = nc.tensor.matmul(ps_max[:, i * S:i * S + P], q[EDGE:MAXROW, 4 * g + i, P:],
                                                    k[EDGE:MAXROW, 4 * g + i, 0:P], start=True, stop=True, skip_group_check=True)
                    else:
                        for i in range(8):
                            last = nc.tensor.matmul(ps_max[:, i * P:(i + 1) * P], q[0:MAXROW, 8 * g + i, 0:P],
                                                    k[0:MAXROW, 8 * g + i, 0:P], start=True, stop=True, skip_group_check=True)
                    last.then_inc(max_ps, 1)

                def exp_step(s):
                    t, g = EXP_STEPS[s]
                    if s % 3 == 0:
                        pe.wait_ge(mrow_in[s // 3], b * 16 + 16)
                    if s > 0 or on[-1]:
                        pe.wait_ge(exp_done, b * NS + s)
                    q, k = q_st[u], k_st[u]
                    if t == 0:
                        for i in range(4):
                            nc.tensor.matmul(ps_exp[:, i * S:i * S + P], k[0:ROWS, 4 * g + i, 0:P],
                                             q[0:ROWS, 4 * g + i, 0:P], start=True, stop=True, skip_group_check=True)
                        for i in range(4):
                            last = nc.tensor.matmul(ps_exp[:, i * S + P:(i + 1) * S], k[EDGE:ROWS, 4 * g + i, 0:P],
                                                    q[EDGE:ROWS, 4 * g + i, P:], start=True, stop=True, skip_group_check=True)
                    else:
                        for i in range(8):
                            last = nc.tensor.matmul(ps_exp[:, i * P:(i + 1) * P], k[0:ROWS, 8 * g + i, P:],
                                                    q[0:ROWS, 8 * g + i, P:], start=True, stop=True, skip_group_check=True)
                    last.then_inc(exp_ps, 1)

                def pv(k, s):
                    n, v, hn = at(k)
                    t, g = EXP_STEPS[s]
                    if s == 0:
                        pe.wait_ge(vaug_done, n + 1)
                    if s % 3 == 0 and on[-1]:
                        pe.wait_ge(ctx_cp, n * 2 - 1 + s // 3)
                    pe.wait_ge(exp_done, n * NS + s + 1)
                    for i in range(4 if t == 0 else 8):
                        h = 4 * g + i if t == 0 else 8 * g + i
                        gg, row = h // 4, 32 * (h % 4)
                        if t == 0:
                            last = nc.tensor.matmul(ps_ctx[row:row + 32, gg * S:(gg + 1) * S], v_aug[v][:, 0, h, :],
                                                    probs[s][:, i * S:(i + 1) * S], start=(gg % 2 == 0), stop=False,
                                                    skip_group_check=True)
                        else:
                            last = nc.tensor.matmul(ps_ctx[row:row + 32, gg * S + P:(gg + 1) * S], v_aug[v][:, 1, h, :],
                                                    probs[s][:, i * P:(i + 1) * P], start=False, stop=True,
                                                    skip_group_check=True)
                    if s % 3 == 2:
                        last.then_inc(ctx_ps, 1)

                def ctx_turn(t):
                    n, v, hn = at(-1)
                    if t == 0:
                        pe.wait_ge(ctx_cp, n * 2 + 2)
                        if on[3]:
                            pe.wait_ge(qk_cp, b * 2 + 8)
                        elif on[-2]:
                            pe.wait_ge(nd, b * 4 - 4)
                    else:
                        pe.wait_ge(nd, n * 4 + 2)
                        if on[-2]:
                            pe.wait_ge(o_done, n)
                    for g in range(4):
                        last = nc.tensor.transpose(X0[:, g * P:(g + 1) * P], ctx_T[:, g, t * P:(t + 1) * P], ident[:])
                    last.then_inc(cx_ps, 1)

                def max_turn(k, half):
                    n, v, hn = at(k)
                    pe.wait_ge(mrow, n * 12 + 6 * half + 6)
                    if half == 1 or on[k - 1]:
                        pe.wait_ge(mT_cp, n * 2 + half)
                    if half == 0 and on[2]:
                        pe.wait_ge(tok_ev, (b + 2) * 4 + 4)
                    for t in range(TT):
                        last = nc.tensor.transpose(X1[0:3 * HH, 3 * E + t * P // 2:3 * E + (t + 1) * P // 2].bitcast(BF16),
                                                   max_parts[:, half, t, :, :].rearrange("p n h -> p (n h)"), ident_bf[:])
                    last.then_inc(mT_ps, 1)

                def out_turn():
                    n, v, hn = at(-2)
                    pe.wait_ge(fin, n * 4 + 4)
                    if on[-1]:
                        pe.wait_ge(nd, n * 4 + 6)
                    for t in range(TT):
                        last = nc.tensor.transpose(X0[:, t * P:(t + 1) * P], o_tok[v][:, t, :], ident[:])
                    last.then_inc(oT_ps, 1)

                def out_proj():
                    n, v, hn = at(-2)
                    pe.wait_ge(oT_cp, n + 1)
                    for t in range(TT):
                        nc.tensor.matmul(X0[:, 256 + t * P:256 + (t + 1) * P], o_T[:, t * P:(t + 1) * P], wo[:],
                                         start=True, stop=False, skip_group_check=True)
                        last = nc.tensor.matmul(X0[:, 256 + t * P:256 + (t + 1) * P], ones3[:], bias_rows[:, 3 * E:],
                                                start=False, stop=True, skip_group_check=True)
                    last.then_inc(o_ps, 1)

                for s in range(NS):
                    if on[1]:
                        max_step(s)
                    if s == 1 and on[0]:
                        max_turn(0, 1)
                    if on[0]:
                        exp_step(s)
                    if s == 4 and on[-2]:
                        out_proj()
                    if s == 4 and on[0]:
                        pv(0, 3)
                    if s == 0 and on[-1]:
                        pv(-1, NS - 1)
                    if s == 0 and on[3]:
                        qk_proj()
                    if s == 1 and on[2]:
                        tok_proj(0)
                    if s == 2 and on[-1]:
                        ctx_turn(0)
                    if s == 3 and on[-2]:
                        out_turn()
                    if s == 3 and on[2]:
                        tok_proj(1)
                    if s == 4 and on[1]:
                        max_turn(1, 0)
                    if s == 5 and on[-1]:
                        ctx_turn(1)
                    if s not in (0, 4) and on[0]:
                        pv(0, s - 1)

            pipeline(pe, body)


def experts(nc, ctx, NT, x_t, attn_all, tile_expert, ident, b1_sb, w1, w2, b2, xd, out_t):
    def sb(name, shape, dt=F32):
        return ctx.enter_context(nc.sbuf_tensor(name, shape, dt))

    def sem(name):
        return ctx.enter_context(nc.semaphore(name))

    def bank(name):
        return ctx.enter_context(nc.psum_tensor(name, [P, 512], F32))

    N = NT * P
    NTILE = tile_expert.shape[1]
    TS = SLOT_T // P
    OUT_G = min(8, NT)
    GT = NT // OUT_G
    HELD = OUT_G // 2
    W2, B1, B2 = FFN, FFN + FC * E, FFN + FC * E + FC
    WIDTH = B2 + E
    w_all = sb("w_all", [P, NEXP, WIDTH])
    w_cur = [sb(f"w_cur{i}", [P, WIDTH]) for i in range(4)]
    slots = [sb(f"slots{i}", [P, TS, E + 1]) for i in range(RING)]
    y_sb = [sb(f"y_sb{i}", [P, TS, E]) for i in range(RING)]
    xT = [sb(f"xT{i}", [P, SLOT_T]) for i in range(2)]
    hT = [sb(f"hT{i}", [P, FC, SLOT_T]) for i in range(2)]
    x_all = sb("x_again", [P, NT, E])
    y_first = sb("y_first", [P, NT, E])
    y_second = sb("y_second", [P, HELD * GT, E])
    yd = nc.dram_tensor("outputs_dram", [TOPK * N + PADS * P, E], F32, kind="Internal").ap()
    ps_x = [bank(f"ps_turn{i}") for i in range(2)]
    ps_h = [[bank(f"ps_h{i}{j}") for j in range(2)] for i in range(2)]
    ps_y = [bank(f"ps_y{i}") for i in range(2)]

    w_in = sem("w_in")
    b1_cp = sem("b1_cp")
    x_in = sem("x_again_in")
    slots_in = [sem(f"slots_in{i}") for i in range(RING)]
    w_cp = sem("w_cp")
    x_ps = sem("x_ps")
    x_cp = sem("x_cp")
    h_ps = sem("h_ps")
    h_act = sem("h_act")
    h_dve = sem("h_dve")
    y_ps = sem("y_ps")
    y_cp = sem("y_cp")
    y_taken = sem("y_taken")
    y_out = [sem(f"y_out{i}") for i in range(RING)]
    y_in = [sem(f"y_in{g}") for g in range(OUT_G)]
    summed = sem("summed")
    gated = sem("gated")
    scaled = sem("scaled")
    fin = sem("fin_out")
    out_done = sem("out_done")

    def pipeline(eng, body):
        def one(i, q, u, known):
            body(lambda k: (i + k, (u + k) % RING, q + (u + k) // RING), lambda k: known is None or 0 <= known + k < NTILE)

        first = RING - 2
        for i in range(-2, first):
            one(i, i // RING, i % RING, i)
        with eng.Fori(0, NTILE // RING - 1) as j:
            for u in range(first, first + RING):
                one(j * RING + u, j + u // RING, u % RING, None)
        for i in range(NTILE - 2, NTILE):
            one(i, i // RING, i % RING, i)

    with nc.Block() as block:
        @block.sync
        def _(sp):
            sp.dma_start(w_all[:, :, 0:W2], w1.rearrange("e p f -> p e f")).then_inc(w_in, 16)
            for e in range(NEXP):
                sp.dma_start(w_all[:, e, W2:B1].rearrange("p (c n) -> p c n", n=E),
                             w2[e].rearrange("(c p) n -> p c n", p=P)).then_inc(w_in, 16)
            sp.dma_start(w_all[:, :, B2:], b2[None, :, :].to_broadcast([P, NEXP, E])).then_inc(w_in, 16)

            def body(at, on):
                if on(2):
                    n, u, q = at(2)
                    if on(2 - RING):
                        sp.wait_ge(y_out[u], q * 32)
                    sp.dma_start(slots[u][:], xd.rearrange("(n p) e -> p n e", p=P)[:, bass.ds(n * TS, TS), :]
                        ).then_inc(slots_in[u], 16)

            pipeline(sp, body)
            sp.dma_start(x_all[:], x_t).then_inc(x_in, 16)
            for i in range(RING):
                sp.wait_ge(y_out[i], NTILE // RING * 32)
            for g in range(OUT_G):
                ts = slice(g * GT, (g + 1) * GT)
                if g >= HELD:
                    sp.wait_ge(summed, g - HELD + 1)
                for s, dst in enumerate((y_first[:, ts, :], y_second[:, g % HELD * GT:(g % HELD + 1) * GT, :])):
                    sp.dma_start(dst, yd[s * N:(s + 1) * N, :].rearrange("(t p) e -> p t e", p=P)[:, ts, :]
                                 ).then_inc(y_in[g], 16)
            for g in range(OUT_G):
                ts = slice(g * GT, (g + 1) * GT)
                sp.wait_ge(fin, g + 1)
                sp.dma_start(out_t[:, ts, :], x_all[:, ts, :]).then_inc(out_done, 16)
            sp.wait_ge(out_done, 16 * OUT_G)

        @block.gpsimd
        def _(pool):
            def body(at, on):
                if on(0):
                    n, u, q = at(0)
                    pool.wait_ge(y_cp, n + 1)
                    pool.sem_inc(y_taken, 1)
                    for t in range(TS):
                        nc.gpsimd.indirect_dma_start(yd, bass.IndirectOffsetOnAxis(ap=slots[u][:, t, E:].bitcast(U32), axis=0),
                                                     y_sb[u][:, t, :], None).then_inc(y_out[u], 16)

            pipeline(pool, body)

        @block.tensor
        def _(pe):
            def body(at, on):
                if on(2):
                    n, u, q = at(2)
                    pe.wait_ge(slots_in[u], q * 16 + 16)
                    if on(0):
                        pe.wait_ge(x_cp, n - 1)
                    for t in range(TS):
                        last = nc.tensor.transpose(ps_x[u % 2][:, t * P:(t + 1) * P], slots[u][:, t, 0:E], ident[:])
                    last.then_inc(x_ps, 1)
                if on(1):
                    n, u, q = at(1)
                    pe.wait_ge(x_cp, n + 1)
                    pe.wait_ge(w_cp, n + 1)
                    if on(-1):
                        pe.wait_ge(h_act, n - 1)
                        pe.wait_ge(h_dve, n - 1)
                    for f in range(FC):
                        last = nc.tensor.matmul(ps_h[u % 2][f // 2][:, f % 2 * SLOT_T:(f % 2 + 1) * SLOT_T],
                                                w_cur[u % 4][:, f * P:(f + 1) * P], xT[u % 2][:], start=True, stop=True,
                                                skip_group_check=True)
                    last.then_inc(h_ps, 1)
                if on(0):
                    n, u, q = at(0)
                    pe.wait_ge(h_act, n + 1)
                    pe.wait_ge(h_dve, n + 1)
                    if on(-2):
                        pe.wait_ge(y_cp, n - 1)
                    for t in range(TS):
                        for f in range(FC):
                            last = nc.tensor.matmul(ps_y[u % 2][:, t * E:(t + 1) * E], hT[u % 2][:, f, t * P:(t + 1) * P],
                                                    w_cur[u % 4][:, W2 + f * E:W2 + (f + 1) * E],
                                                    start=(f == 0), stop=(f == FC - 1), skip_group_check=True)
                    last.then_inc(y_ps, 1)

            pipeline(pe, body)

        @block.scalar
        def _(act):
            def body(at, on):
                if on(2):
                    n, u, q = at(2)
                    act.wait_ge(x_ps, n + 1)
                    if on(0):
                        act.wait_ge(h_ps, n - 1)
                    nc.scalar.activation(xT[u % 2][:], ps_x[u % 2][:, 0:SLOT_T], ACT.Copy).then_inc(x_cp, 1)
                if on(1):
                    n, u, q = at(1)
                    act.wait_ge(h_ps, n + 1)
                    if on(-1):
                        act.wait_ge(y_ps, n - 1)
                    for f in range(2):
                        last = nc.scalar.activation(hT[u % 2][:, f, :], ps_h[u % 2][0][:, f * SLOT_T:(f + 1) * SLOT_T],
                                                    ACT.Relu, bias=w_cur[u % 4][:, B1 + f:B1 + f + 1])
                    last.then_inc(h_act, 1)

            pipeline(act, body)
            for g in range(OUT_G):
                ts = slice(g * GT, (g + 1) * GT)
                act.wait_ge(summed, g + 1)
                nc.scalar.activation(y_first[:, ts, :], y_first[:, ts, :], ACT.Silu).then_inc(gated, 1)

        @block.vector
        def _(dve):
            dve.wait_ge(w_in, 16 * (2 + NEXP))
            nc.vector.tensor_copy(w_all[:, :, B1:B2], b1_sb[:]).then_inc(b1_cp, 1)
            dve.wait_ge(b1_cp, 1)

            def body(at, on):
                if on(2):
                    n, u, q = at(2)
                    if on(-2):
                        dve.wait_ge(y_cp, n - 3)
                    e = dve.value_load(tile_expert[0:1, bass.ds(n, 1)], min_val=0, max_val=NEXP - 1)
                    nc.vector.tensor_copy(w_cur[u % 4][:], w_all[:, bass.ds(e, 1), :].rearrange("p a w -> p (a w)")
                        ).then_inc(w_cp, 1)
                if on(1):
                    n, u, q = at(1)
                    dve.wait_ge(h_ps, n + 1)
                    if on(-1):
                        dve.wait_ge(y_ps, n - 1)
                    for f in range(2, 4):
                        last = nc.vector.tensor_scalar(hT[u % 2][:, f, :], ps_h[u % 2][1][:, (f - 2) * SLOT_T:(f - 1) * SLOT_T],
                                                       w_cur[u % 4][:, B1 + f:B1 + f + 1], 0.0, ALU.add, ALU.max)
                    last.then_inc(h_dve, 1)
                if on(0):
                    n, u, q = at(0)
                    dve.wait_ge(y_ps, n + 1)
                    nc.vector.tensor_tensor(y_sb[u][:], ps_y[u % 2][:, 0:TS * E].rearrange("p (t e) -> p t e", e=E),
                                            w_cur[u % 4][:, None, B2:].to_broadcast([P, TS, E]), ALU.add).then_inc(y_cp, 1)

            pipeline(dve, body)
            dve.wait_ge(x_in, 16)

            def add_choices(g):
                ts = slice(g * GT, (g + 1) * GT)
                dve.wait_ge(y_in[g], 32)
                nc.vector.tensor_tensor(y_first[:, ts, :], y_first[:, ts, :], y_second[:, g % HELD * GT:(g % HELD + 1) * GT, :], ALU.add).then_inc(summed, 1)

            add_choices(0)
            for g in range(OUT_G):
                ts = slice(g * GT, (g + 1) * GT)
                if g + 1 < OUT_G:
                    add_choices(g + 1)
                dve.wait_ge(gated, g + 1)
                nc.vector.tensor_tensor(y_first[:, ts, :], y_first[:, ts, :], attn_all[:, ts, :], ALU.mult).then_inc(scaled, 1)
                dve.wait_ge(scaled, g + 1)
                nc.vector.tensor_tensor(x_all[:, ts, :], x_all[:, ts, :], y_first[:, ts, :], ALU.add).then_inc(fin, 1)


NAMES = ["L0_attn_x", "L0_attn_W_q", "L0_attn_b_q", "L0_attn_W_k", "L0_attn_b_k", "L0_attn_W_v", "L0_attn_b_v",
         "L0_attn_W_o", "L0_attn_b_o", "L0_attn_rel_k_table", "L0_attn_rel_v_table", "L0_ffn_gate_w", "L0_ffn_gate_b",
         "L0_ffn_w1", "L0_ffn_b1", "L0_ffn_w2", "L0_ffn_b2"]


def kernel(**inputs):
    import concourse.bacc as bacc
    from concourse.bass_utils import run_bass_kernel_spmd

    nc = bacc.Bacc("TRN2", target_bir_lowering=False, num_devices=1)
    arrays, args = {}, []
    for name in NAMES:
        a = np.ascontiguousarray(inputs[name])
        arrays[f"in_{name}"] = a
        args.append(nc.dram_tensor(f"in_{name}", a.shape, mybir.dt.from_np(a.dtype), kind="ExternalInput").ap())
    shape = arrays["in_L0_attn_x"].shape
    consts = {}
    for name, a in shape_constants(shape[0]).items():
        arrays[name] = a
        consts[name] = nc.dram_tensor(name, a.shape, mybir.dt.from_np(a.dtype), kind="ExternalInput").ap()
    out = nc.dram_tensor("out_0_dram", shape, F32, kind="ExternalOutput").ap()
    program(nc, *args, consts, out)
    r = run_bass_kernel_spmd(nc, [arrays], core_ids=[0])
    return r.results[0]["out_0_dram"]
```
